# Optimizing a Trainium2 kernel written in Bass

```python
import numpy as np
import jax
import jax.numpy as jnp

def _softmax(x, axis=-1):
    return jax.nn.softmax(x, axis=axis)

def _gelu(x):
    return jax.nn.gelu(x, approximate=True)

def _silu(x):
    return jax.nn.silu(x)

def _sigmoid(x):
    return jax.nn.sigmoid(x)

def _layernorm(x, axis=-1, eps=1e-05):
    m = jnp.mean(x, axis=axis, keepdims=True)
    v = jnp.var(x, axis=axis, keepdims=True)
    return (x - m) / jnp.sqrt(v + eps)

def _scatter_add(tgt, idx, src, axis=0):
    return tgt.at[idx].add(src)

def _segment_sum(src, seg, n):
    return jax.ops.segment_sum(src, seg, n)
kernel_name = 'mk_gnn_preln_d4_gnn_r32_6f1fed'

def setup_inputs(seed: int=0):
    np.random.seed(seed)
    _w = jnp.asarray

    def _rec_inputs():
        import jax
        import jax.numpy as jnp
        _gk = jax.random.key(seed)
        x = -0.0001978 + 0.9998 * jax.random.normal(jax.random.fold_in(_gk, 1), (3125, 128), jnp.float32)
        src = jax.random.randint(jax.random.fold_in(_gk, 2), (50000,), 0, 3125, jnp.int32)
        dst = jax.random.randint(jax.random.fold_in(_gk, 3), (50000,), 0, 3125, jnp.int32)
        _o = jnp.argsort(dst, stable=True)
        src = src[_o]
        dst = dst[_o]
        return (x, src, dst)
    x, src, dst = _rec_inputs()

    def _L0_gnn_setup():
        import jax, jax.numpy as jnp
        import numpy as np
        N, DIM, K = (50000, 128, 9)
        FFN = 4 * DIM
        EPS = 1e-05

        def layer_norm(x, g, b):
            mu = jnp.mean(x, axis=-1, keepdims=True)
            var = jnp.mean(jnp.square(x - mu), axis=-1, keepdims=True)
            return (x - mu) * jax.lax.rsqrt(var + EPS) * g + b
        key = jax.random.key(seed)
        ks = jax.random.split(key, 12)
        E = N * K
        src = jax.random.randint(ks[0], (E,), 0, N)
        dst = jnp.repeat(jnp.arange(N), K)
        edge_index = jnp.stack([src, dst]).astype(jnp.int64)
        s = lambda k, shape, fan_in: jax.random.normal(k, shape, jnp.float32) / np.sqrt(fan_in)
        return {'x': jax.random.normal(ks[1], (N, DIM), jnp.float32), 'edge_index': edge_index, 'W_in_w': s(ks[2], (DIM, DIM), DIM), 'W_in_b': jnp.zeros((DIM,), jnp.float32), 'W_upd_w': s(ks[3], (2 * DIM, DIM), 2 * DIM), 'W_upd_b': jnp.zeros((DIM,), jnp.float32), 'W_out_w': s(ks[4], (DIM, DIM), DIM), 'W_out_b': jnp.zeros((DIM,), jnp.float32), 'ln1_g': jnp.ones((DIM,), jnp.float32), 'ln1_b': jnp.zeros((DIM,), jnp.float32), 'ln2_g': jnp.ones((DIM,), jnp.float32), 'ln2_b': jnp.zeros((DIM,), jnp.float32), 'ffn1_w': s(ks[5], (DIM, FFN), DIM), 'ffn1_b': jnp.zeros((FFN,), jnp.float32), 'ffn2_w': s(ks[6], (FFN, DIM), FFN), 'ffn2_b': jnp.zeros((DIM,), jnp.float32)}
    _L0_gnn_all = _L0_gnn_setup()
    _L0_gnn_in = {k: v for k, v in _L0_gnn_all.items() if k in ('W_in_w', 'W_in_b', 'W_upd_w', 'W_upd_b', 'W_out_w', 'W_out_b', 'ln1_g', 'ln1_b', 'ln2_g', 'ln2_b', 'ffn1_w', 'ffn1_b', 'ffn2_w', 'ffn2_b')}
    del _L0_gnn_all

    def _L1_gnn_setup():
        import jax, jax.numpy as jnp
        import numpy as np
        N, E, D_IN, HID, OUT, H = (625, 10000, 128, 128, 128, 4)

        def _lin(key, fan_in, fan_out):
            kw, kb = jax.random.split(key)
            W = jax.random.normal(kw, (fan_in, fan_out), jnp.float32) * 0.05
            b = jax.random.normal(kb, (fan_out,), jnp.float32) * 0.05
            return (W, b)

        def _transformer_conv(x, src, dst, Wq, bq, Wk, bk, Wv, bv, Ws, bs, heads, out_ch, concat):
            n = x.shape[0]
            q = (x @ Wq + bq).reshape(n, heads, out_ch)
            k = (x @ Wk + bk).reshape(n, heads, out_ch)
            v = (x @ Wv + bv).reshape(n, heads, out_ch)
            alpha = jnp.einsum('ehc,ehc->eh', q[dst], k[src]) / jnp.sqrt(jnp.float32(out_ch))
            m = jax.ops.segment_max(alpha, dst, num_segments=n)
            alpha = jnp.exp(alpha - m[dst])
            s = jax.ops.segment_sum(alpha, dst, num_segments=n)
            alpha = alpha / (s[dst] + 1e-16)
            out = jax.ops.segment_sum(alpha[..., None] * v[src], dst, num_segments=n)
            if concat:
                out = out.reshape(n, heads * out_ch)
            else:
                out = out.mean(axis=1)
            return out + x @ Ws + bs
        key = jax.random.key(seed)
        ks = jax.random.split(key, 10)
        x = jax.random.normal(ks[0], (N, D_IN), jnp.float32)
        edge_index = jax.random.randint(ks[1], (2, E), 0, N, jnp.int32)
        Wq0, bq0 = _lin(ks[2], D_IN, H * HID)
        Wk0, bk0 = _lin(ks[3], D_IN, H * HID)
        Wv0, bv0 = _lin(ks[4], D_IN, H * HID)
        Ws0, bs0 = _lin(ks[5], D_IN, H * HID)
        Wq1, bq1 = _lin(ks[6], H * HID, H * OUT)
        Wk1, bk1 = _lin(ks[7], H * HID, H * OUT)
        Wv1, bv1 = _lin(ks[8], H * HID, H * OUT)
        Ws1, bs1 = _lin(ks[9], H * HID, OUT)
        return dict(x=x, edge_index=edge_index, Wq0=Wq0, bq0=bq0, Wk0=Wk0, bk0=bk0, Wv0=Wv0, bv0=bv0, Ws0=Ws0, bs0=bs0, Wq1=Wq1, bq1=bq1, Wk1=Wk1, bk1=bk1, Wv1=Wv1, bv1=bv1, Ws1=Ws1, bs1=bs1)
    _L1_gnn_all = _L1_gnn_setup()
    _L1_gnn_in = {k: v for k, v in _L1_gnn_all.items() if k in ('Wq0', 'bq0', 'Wk0', 'bk0', 'Wv0', 'bv0', 'Ws0', 'bs0', 'Wq1', 'bq1', 'Wk1', 'bk1', 'Wv1', 'bv1', 'Ws1', 'bs1')}
    del _L1_gnn_all

    def _L2_gnn_setup():
        import jax, jax.numpy as jnp
        import numpy as np
        N_NODES = 50000
        C_IN = 128
        C_OUT = 128
        N_EDGES = 25000
        NEG_SLOPE_GAT = 0.2
        NEG_SLOPE_ACT = 0.01
        EPS = 1e-05

        def _gatv2_block(x, edge_index, W_l, W_r, att, bias, ln_w, ln_b):
            n = x.shape[0]
            loop = jnp.arange(n, dtype=edge_index.dtype)
            src = jnp.concatenate([edge_index[0], loop])
            dst = jnp.concatenate([edge_index[1], loop])
            x_l = x @ W_l
            x_r = x @ W_r
            m = x_l[src] + x_r[dst]
            logits = jax.nn.leaky_relu(m, NEG_SLOPE_GAT) @ att
            seg_max = jax.ops.segment_max(logits, dst, num_segments=n)
            expv = jnp.exp(logits - seg_max[dst])
            denom = jax.ops.segment_sum(expv, dst, num_segments=n)
            alpha = expv / denom[dst]
            out = jax.ops.segment_sum(alpha[:, None] * x_l[src], dst, num_segments=n) + bias
            out = jax.nn.leaky_relu(out, NEG_SLOPE_ACT)
            mu = out.mean()
            out = out - mu
            std = jnp.sqrt((out * out).mean())
            out = out / (std + EPS)
            return out * ln_w + ln_b
        key = jax.random.key(seed)
        ks = jax.random.split(key, 8)
        s_in = 1.0 / np.sqrt(C_IN)
        x = jax.random.normal(ks[0], (N_NODES, C_IN), dtype=jnp.float32)
        edge_index = jax.random.randint(ks[1], (2, N_EDGES), 0, N_NODES, dtype=jnp.int64)
        W_l = jax.random.uniform(ks[2], (C_IN, C_OUT), jnp.float32, -s_in, s_in)
        W_r = jax.random.uniform(ks[3], (C_IN, C_OUT), jnp.float32, -s_in, s_in)
        att = jax.random.uniform(ks[4], (C_OUT,), jnp.float32, -1.0 / np.sqrt(C_OUT), 1.0 / np.sqrt(C_OUT))
        bias = jnp.zeros((C_OUT,), jnp.float32)
        ln_w = jnp.ones((C_OUT,), jnp.float32)
        ln_b = jnp.zeros((C_OUT,), jnp.float32)
        return {'x': x, 'edge_index': edge_index, 'W_l': W_l, 'W_r': W_r, 'att': att, 'bias': bias, 'ln_w': ln_w, 'ln_b': ln_b}
    _L2_gnn_all = _L2_gnn_setup()
    _L2_gnn_in = {k: v for k, v in _L2_gnn_all.items() if k in ('W_l', 'W_r', 'att', 'bias', 'ln_w', 'ln_b')}
    del _L2_gnn_all

    def _L3_gnn_setup():
        import jax, jax.numpy as jnp
        import numpy as np
        N_NODES = 3125
        N_EDGES = 20000
        HIDDEN = 128
        EPS = 1e-06
        key = jax.random.key(seed)
        k_x, k_w, k_a, k_e = jax.random.split(key, 4)
        x = jax.random.normal(k_x, (N_NODES, HIDDEN), dtype=jnp.float32)
        W = jax.random.normal(k_w, (HIDDEN, HIDDEN), dtype=jnp.float32) / np.sqrt(HIDDEN)
        b = jnp.zeros((HIDDEN,), dtype=jnp.float32)
        att_w = jax.random.normal(k_a, (1, 2 * HIDDEN), dtype=jnp.float32) / np.sqrt(2 * HIDDEN)
        norm_w = jnp.ones((HIDDEN,), dtype=jnp.float32)
        norm_b = jnp.zeros((HIDDEN,), dtype=jnp.float32)
        e = jax.random.randint(k_e, (N_EDGES, 2), 0, N_NODES, dtype=jnp.int64)
        return {'x': x, 'W': W, 'b': b, 'att_w': att_w, 'norm_w': norm_w, 'norm_b': norm_b, 'e': e}
    _L3_gnn_all = _L3_gnn_setup()
    _L3_gnn_in = {k: v for k, v in _L3_gnn_all.items() if k in ('W', 'b', 'att_w', 'norm_w', 'norm_b')}
    del _L3_gnn_all
    return {'x': x, 'src': src, 'dst': dst, 'L0_gnn_W_in_w': _L0_gnn_in['W_in_w'], 'L0_gnn_W_in_b': _L0_gnn_in['W_in_b'], 'L0_gnn_W_upd_w': _L0_gnn_in['W_upd_w'], 'L0_gnn_W_upd_b': _L0_gnn_in['W_upd_b'], 'L0_gnn_W_out_w': _L0_gnn_in['W_out_w'], 'L0_gnn_W_out_b': _L0_gnn_in['W_out_b'], 'L0_gnn_ln1_g': _L0_gnn_in['ln1_g'], 'L0_gnn_ln1_b': _L0_gnn_in['ln1_b'], 'L0_gnn_ln2_g': _L0_gnn_in['ln2_g'], 'L0_gnn_ln2_b': _L0_gnn_in['ln2_b'], 'L0_gnn_ffn1_w': _L0_gnn_in['ffn1_w'], 'L0_gnn_ffn1_b': _L0_gnn_in['ffn1_b'], 'L0_gnn_ffn2_w': _L0_gnn_in['ffn2_w'], 'L0_gnn_ffn2_b': _L0_gnn_in['ffn2_b'], 'L1_gnn_Wq0': _L1_gnn_in['Wq0'], 'L1_gnn_bq0': _L1_gnn_in['bq0'], 'L1_gnn_Wk0': _L1_gnn_in['Wk0'], 'L1_gnn_bk0': _L1_gnn_in['bk0'], 'L1_gnn_Wv0': _L1_gnn_in['Wv0'], 'L1_gnn_bv0': _L1_gnn_in['bv0'], 'L1_gnn_Ws0': _L1_gnn_in['Ws0'], 'L1_gnn_bs0': _L1_gnn_in['bs0'], 'L1_gnn_Wq1': _L1_gnn_in['Wq1'], 'L1_gnn_bq1': _L1_gnn_in['bq1'], 'L1_gnn_Wk1': _L1_gnn_in['Wk1'], 'L1_gnn_bk1': _L1_gnn_in['bk1'], 'L1_gnn_Wv1': _L1_gnn_in['Wv1'], 'L1_gnn_bv1': _L1_gnn_in['bv1'], 'L1_gnn_Ws1': _L1_gnn_in['Ws1'], 'L1_gnn_bs1': _L1_gnn_in['bs1'], 'L2_gnn_W_l': _L2_gnn_in['W_l'], 'L2_gnn_W_r': _L2_gnn_in['W_r'], 'L2_gnn_att': _L2_gnn_in['att'], 'L2_gnn_bias': _L2_gnn_in['bias'], 'L2_gnn_ln_w': _L2_gnn_in['ln_w'], 'L2_gnn_ln_b': _L2_gnn_in['ln_b'], 'L3_gnn_W': _L3_gnn_in['W'], 'L3_gnn_b': _L3_gnn_in['b'], 'L3_gnn_att_w': _L3_gnn_in['att_w'], 'L3_gnn_norm_w': _L3_gnn_in['norm_w'], 'L3_gnn_norm_b': _L3_gnn_in['norm_b']}

def reference(x, src, dst, L0_gnn_W_in_w, L0_gnn_W_in_b, L0_gnn_W_upd_w, L0_gnn_W_upd_b, L0_gnn_W_out_w, L0_gnn_W_out_b, L0_gnn_ln1_g, L0_gnn_ln1_b, L0_gnn_ln2_g, L0_gnn_ln2_b, L0_gnn_ffn1_w, L0_gnn_ffn1_b, L0_gnn_ffn2_w, L0_gnn_ffn2_b, L1_gnn_Wq0, L1_gnn_bq0, L1_gnn_Wk0, L1_gnn_bk0, L1_gnn_Wv0, L1_gnn_bv0, L1_gnn_Ws0, L1_gnn_bs0, L1_gnn_Wq1, L1_gnn_bq1, L1_gnn_Wk1, L1_gnn_bk1, L1_gnn_Wv1, L1_gnn_bv1, L1_gnn_Ws1, L1_gnn_bs1, L2_gnn_W_l, L2_gnn_W_r, L2_gnn_att, L2_gnn_bias, L2_gnn_ln_w, L2_gnn_ln_b, L3_gnn_W, L3_gnn_b, L3_gnn_att_w, L3_gnn_norm_w, L3_gnn_norm_b):
    import jax
    import jax.numpy as jnp

    def _L0_gnn_ref(x, edge_index, W_in_w, W_in_b, W_upd_w, W_upd_b, W_out_w, W_out_b, ln1_g, ln1_b, ln2_g, ln2_b, ffn1_w, ffn1_b, ffn2_w, ffn2_b):
        import jax, jax.numpy as jnp
        import numpy as np
        N, DIM, K = (50000, 128, 9)
        FFN = 4 * DIM
        EPS = 1e-05

        def layer_norm(x, g, b):
            mu = jnp.mean(x, axis=-1, keepdims=True)
            var = jnp.mean(jnp.square(x - mu), axis=-1, keepdims=True)
            return (x - mu) * jax.lax.rsqrt(var + EPS) * g + b
        src, dst = (edge_index[0], edge_index[1])
        n = x.shape[0]
        h = x @ W_in_w + W_in_b
        diff = h[src] - h[dst]
        seg_max = jax.ops.segment_max(diff, dst, num_segments=n)
        counts = jax.ops.segment_sum(jnp.ones_like(dst, jnp.int32), dst, num_segments=n)
        max_diff = jnp.where((counts > 0)[:, None], seg_max, 0.0)
        h = jnp.concatenate([h, max_diff], axis=-1) @ W_upd_w + W_upd_b
        h = h @ W_out_w + W_out_b
        x = layer_norm(x + h, ln1_g, ln1_b)
        f = jax.nn.gelu(x @ ffn1_w + ffn1_b, approximate=False) @ ffn2_w + ffn2_b
        return layer_norm(x + f, ln2_g, ln2_b)

    def _L1_gnn_ref(x, edge_index, Wq0, bq0, Wk0, bk0, Wv0, bv0, Ws0, bs0, Wq1, bq1, Wk1, bk1, Wv1, bv1, Ws1, bs1):
        import jax, jax.numpy as jnp
        import numpy as np
        N, E, D_IN, HID, OUT, H = (625, 10000, 128, 128, 128, 4)

        def _lin(key, fan_in, fan_out):
            kw, kb = jax.random.split(key)
            W = jax.random.normal(kw, (fan_in, fan_out), jnp.float32) * 0.05
            b = jax.random.normal(kb, (fan_out,), jnp.float32) * 0.05
            return (W, b)

        def _transformer_conv(x, src, dst, Wq, bq, Wk, bk, Wv, bv, Ws, bs, heads, out_ch, concat):
            n = x.shape[0]
            q = (x @ Wq + bq).reshape(n, heads, out_ch)
            k = (x @ Wk + bk).reshape(n, heads, out_ch)
            v = (x @ Wv + bv).reshape(n, heads, out_ch)
            alpha = jnp.einsum('ehc,ehc->eh', q[dst], k[src]) / jnp.sqrt(jnp.float32(out_ch))
            m = jax.ops.segment_max(alpha, dst, num_segments=n)
            alpha = jnp.exp(alpha - m[dst])
            s = jax.ops.segment_sum(alpha, dst, num_segments=n)
            alpha = alpha / (s[dst] + 1e-16)
            out = jax.ops.segment_sum(alpha[..., None] * v[src], dst, num_segments=n)
            if concat:
                out = out.reshape(n, heads * out_ch)
            else:
                out = out.mean(axis=1)
            return out + x @ Ws + bs
        src, dst = (edge_index[0], edge_index[1])
        h = _transformer_conv(x, src, dst, Wq0, bq0, Wk0, bk0, Wv0, bv0, Ws0, bs0, H, HID, True)
        h = jax.nn.relu(h)
        out = _transformer_conv(h, src, dst, Wq1, bq1, Wk1, bk1, Wv1, bv1, Ws1, bs1, H, OUT, False)
        return out

    def _L2_gnn_ref(x, edge_index, W_l, W_r, att, bias, ln_w, ln_b):
        import jax, jax.numpy as jnp
        import numpy as np
        N_NODES = 50000
        C_IN = 128
        C_OUT = 128
        N_EDGES = 25000
        NEG_SLOPE_GAT = 0.2
        NEG_SLOPE_ACT = 0.01
        EPS = 1e-05

        def _gatv2_block(x, edge_index, W_l, W_r, att, bias, ln_w, ln_b):
            n = x.shape[0]
            loop = jnp.arange(n, dtype=edge_index.dtype)
            src = jnp.concatenate([edge_index[0], loop])
            dst = jnp.concatenate([edge_index[1], loop])
            x_l = x @ W_l
            x_r = x @ W_r
            m = x_l[src] + x_r[dst]
            logits = jax.nn.leaky_relu(m, NEG_SLOPE_GAT) @ att
            seg_max = jax.ops.segment_max(logits, dst, num_segments=n)
            expv = jnp.exp(logits - seg_max[dst])
            denom = jax.ops.segment_sum(expv, dst, num_segments=n)
            alpha = expv / denom[dst]
            out = jax.ops.segment_sum(alpha[:, None] * x_l[src], dst, num_segments=n) + bias
            out = jax.nn.leaky_relu(out, NEG_SLOPE_ACT)
            mu = out.mean()
            out = out - mu
            std = jnp.sqrt((out * out).mean())
            out = out / (std + EPS)
            return out * ln_w + ln_b
        return _gatv2_block(x, edge_index, W_l, W_r, att, bias, ln_w, ln_b)

    def _L3_gnn_ref(x, W, b, att_w, norm_w, norm_b, e):
        import jax, jax.numpy as jnp
        import numpy as np
        N_NODES = 3125
        N_EDGES = 20000
        HIDDEN = 128
        EPS = 1e-06
        n_nodes = x.shape[0]
        src, dst = (e[:, 0], e[:, 1])
        m = x[src] @ W.T + b
        s = x[dst] @ W.T + b
        a = jnp.exp(jax.nn.leaky_relu(jnp.concatenate((m, s), axis=1) @ att_w.T, negative_slope=0.2))
        _unused = jax.ops.segment_sum(a * m, dst, num_segments=n_nodes)
        n = jax.ops.segment_sum(a, dst, num_segments=n_nodes)
        h = jax.nn.relu(x / jnp.where(n == 0.0, 1.0, n))
        y = h + x
        inv_rms = jax.lax.rsqrt(jnp.mean(y * y, axis=-1, keepdims=True) + EPS)
        return norm_w * (y * inv_rms) + norm_b
    edge_index = jnp.stack([src, dst])
    edge_index_t = jnp.stack([src, dst], axis=1)
    h = jnp.maximum(_layernorm(x, axis=-1), 0.0)
    x = x + _L0_gnn_ref(h, edge_index, L0_gnn_W_in_w, L0_gnn_W_in_b, L0_gnn_W_upd_w, L0_gnn_W_upd_b, L0_gnn_W_out_w, L0_gnn_W_out_b, L0_gnn_ln1_g, L0_gnn_ln1_b, L0_gnn_ln2_g, L0_gnn_ln2_b, L0_gnn_ffn1_w, L0_gnn_ffn1_b, L0_gnn_ffn2_w, L0_gnn_ffn2_b)
    h = jnp.maximum(_layernorm(x, axis=-1), 0.0)
    x = x + _L1_gnn_ref(h, edge_index, L1_gnn_Wq0, L1_gnn_bq0, L1_gnn_Wk0, L1_gnn_bk0, L1_gnn_Wv0, L1_gnn_bv0, L1_gnn_Ws0, L1_gnn_bs0, L1_gnn_Wq1, L1_gnn_bq1, L1_gnn_Wk1, L1_gnn_bk1, L1_gnn_Wv1, L1_gnn_bv1, L1_gnn_Ws1, L1_gnn_bs1)
    h = jnp.maximum(_layernorm(x, axis=-1), 0.0)
    x = x + _L2_gnn_ref(h, edge_index, L2_gnn_W_l, L2_gnn_W_r, L2_gnn_att, L2_gnn_bias, L2_gnn_ln_w, L2_gnn_ln_b)
    h = jnp.maximum(_layernorm(x, axis=-1), 0.0)
    x = x + _L3_gnn_ref(h, L3_gnn_W, L3_gnn_b, L3_gnn_att_w, L3_gnn_norm_w, L3_gnn_norm_b, edge_index_t)
    return x

_drawn_inputs = setup_inputs


def setup_inputs(seed=0):
    import zlib

    import numpy as np

    out = dict(_drawn_inputs(seed))
    spreads = {'L0_gnn_W_in_b': (0.0, 0.1),
     'L0_gnn_W_upd_b': (0.0, 0.1),
     'L0_gnn_W_out_b': (0.0, 0.1),
     'L0_gnn_ln1_g': (1.0, 0.2),
     'L0_gnn_ln1_b': (0.0, 0.1),
     'L0_gnn_ln2_g': (1.0, 0.2),
     'L0_gnn_ln2_b': (0.0, 0.1),
     'L0_gnn_ffn1_b': (0.0, 0.275),
     'L0_gnn_ffn2_b': (0.0, 0.1),
     'L2_gnn_bias': (0.0, 0.1),
     'L2_gnn_ln_w': (1.0, 0.2),
     'L2_gnn_ln_b': (0.0, 0.1),
     'L3_gnn_b': (0.0, 2.0),
     'L3_gnn_norm_w': (1.0, 0.2),
     'L3_gnn_norm_b': (0.0, 0.1)}
    factors = {'L1_gnn_Wq0': 8.0,
     'L1_gnn_bq0': 8.0,
     'L1_gnn_Wk0': 8.0,
     'L1_gnn_bk0': 64.0,
     'L1_gnn_Wq1': 8.0,
     'L1_gnn_bq1': 28.54,
     'L1_gnn_Wk1': 8.0,
     'L1_gnn_bk1': 64.0,
     'L1_gnn_bv1': 4.387,
     'L2_gnn_W_r': 21.228,
     'L3_gnn_W': 64.0,
     'L3_gnn_att_w': 64.0}
    for name, (base, spread) in spreads.items():
        noise = np.random.default_rng([zlib.crc32(name.encode()), seed]).standard_normal(out[name].shape)
        drawn = base * np.exp(spread * noise) if base else spread * noise
        out[name] = jnp.asarray(drawn.astype(out[name].dtype))
    for name, factor in factors.items():
        out[name] = (out[name] * factor).astype(out[name].dtype)
    return out
```

```python
import numpy as np
import concourse.bass as bass
from concourse import mybir
from contextlib import ExitStack

F32, I32, BF16 = mybir.dt.float32, mybir.dt.int32, mybir.dt.bfloat16
ALU = mybir.AluOpType
ACT = mybir.ActivationFunctionType
AXX = mybir.AxisListType.X

NODES, EDGES, D = 3125, 50000, 128
HEADS = 4
FFN = 4 * D
HD = HEADS * D
HW1 = HEADS * (D + 1)
P = 128
WINDOWS = -(-NODES // P)
ROWS = WINDOWS * P
LAST = NODES - (WINDOWS - 1) * P
GROUP = 256
GROUPS = -(-EDGES // GROUP)
SLOTS = GROUPS * GROUP
STEPS = GROUPS + WINDOWS - 1
HALF = STEPS // 2
TILES = 2 * STEPS
U = 4
ITERS = STEPS // U
WBITS = 5
CH = 5
CHUNKS = WINDOWS // CH
BIG = 1.0e30
ds = bass.ds


class Count:

    def __init__(self, sem, ahead, unit):
        self.sem, self.ahead, self.unit, self.base = sem, ahead, unit, 0

    def done(self, n):
        return self.sem, n * self.unit + (self.base + self.ahead * self.unit)

    def free(self, n, depth):
        return self.sem, n * self.unit + (self.base + (self.ahead - depth) * self.unit)


def windows_of(eng, k, i):
    packed = eng.value_load(k.win[0:1, ds(i, 1)], min_val=0, max_val=(1 << (U * WBITS)) - 1)
    return [((packed >> (u * WBITS)) & ((1 << WBITS) - 1)).with_bounds(min_val=0, max_val=WINDOWS - 1) for u in range(U)]


def graph_phase(nc, k):
    with ExitStack() as ctx:
        def sb(name, shape, dt=F32):
            return ctx.enter_context(nc.sbuf_tensor(k.own(name), shape, dt))

        def pb(name, shape):
            return ctx.enter_context(nc.psum_tensor(k.own(name), shape, F32))

        def sem(name):
            return ctx.enter_context(nc.semaphore(k.own(name)))

        last_i = sb("last_i", [1, GROUPS], I32)
        lastw_i = sb("lastw_i", [1, GROUPS], I32)
        lastw = sb("lastw", [1, GROUPS])
        grp_i = sb("grp_i", [1, GROUPS], I32)
        grp = sb("grp", [1, GROUPS])
        key = sb("key", [1, GROUPS])
        step_col = sb("step_col", [P, 2])
        hits = sb("hits", [P, GROUPS])
        gcol = sb("gcol", [P, 2])
        gcol_i = sb("gcol_i", [P, 2], I32)
        wcol = sb("wcol", [P, 2])
        base = sb("base", [P, 2])
        it_i = sb("it_i", [P, P], I32)
        ip_i = sb("ip_i", [P, 1], I32)
        dst_i = sb("dst_i", [P, 2, GROUP], I32)
        src_i = sb("src_i", [P, 2, GROUP], I32)
        dst = sb("dst", [P, 2, GROUP])
        srcf = sb("srcf", [P, 2, GROUP])
        dloc = sb("dloc", [P, 2, GROUP])
        dloc_b = sb("dloc_b", [P, 2, GROUP], BF16)
        same = sb("same", [P, 2, GROUP])
        end = sb("end", [P, 2, GROUP])
        mask_b = sb("mask_b", [P, 2, GROUP], BF16)
        rows = sb("rows", [1, 2, STEPS])
        cont = sb("cont", [1, STEPS + 1])
        whole = sb("whole", [1, STEPS])
        mrows = sb("mrows", [1, 4, STEPS])
        wpack = sb("packed_windows", [1, ITERS])
        cont_c = sb("cont_c", [P, 2, 2])

        pa = pb("pa", [P, 512])
        pc = pb("pc", [P, 512])
        pd = pb("pd", [P, 12, P])

        s_last = sem("last_loaded")
        s_iota = sem("iotas_made")
        s_const = sem("consts_made")
        s_key = sem("key_made")
        s_keyb = sem("key_broadcast")
        s_g = sem("group_index_made")
        s_edges = sem("edges_gathered")
        s_winrow = sem("window_row_made")
        s_dst = sem("dst_floats_made")
        s_rows = sem("first_last_rows")
        s_mrow = sem("mask_rows_made")
        s_mrowb = sem("mask_rows_spread")
        s_end = sem("end_flags_made")
        s_cols = sem("edge_major_made")
        s_stored = sem("rows_stored")

        block = ctx.enter_context(nc.Block())

        @block.sync
        def _(sp):
            with nc.allow_non_contiguous_dma(reason="one value of each group"):
                sp.dma_start(last_i[:, :], k.dst.rearrange("(o g e) -> o g e", o=1, e=GROUP)[:, :, GROUP - 1])\
                  .then_inc(s_last, 16)
            sp.wait_ge(s_end, 1)
            for h in range(2):
                sp.dma_start(k.dloc_dram[h * HALF:(h + 1) * HALF, :], dloc_b[0:HALF, h, :]).then_inc(s_stored, 16)
                sp.dma_start(k.mask_dram[h * HALF:(h + 1) * HALF, :], mask_b[0:HALF, h, :]).then_inc(s_stored, 16)
            sp.wait_ge(s_stored, 64)

        @block.gpsimd
        def _(pool):
            nc.gpsimd.iota(it_i[:, :], [[1, P]], base=0, channel_multiplier=0)
            nc.gpsimd.iota(ip_i[:, :], [[1, 1]], base=0, channel_multiplier=1)
            nc.gpsimd.iota(grp_i[:, :], [[1, GROUPS]], base=0, channel_multiplier=0)
            nc.gpsimd.memset(k.ones_row[:, :], 1.0)
            nc.gpsimd.memset(k.ident[:, :], 0.0)
            pool.drain().then_inc(s_iota, 1)
            nc.gpsimd.affine_select(out=k.ident[:, :], in_=k.ident[:, :], compare_op=ALU.not_equal, fill=1.0,
                                    base=0, pattern=[[-1, P]], channel_multiplier=1).then_inc(s_const, 1)
            pool.wait_ge(s_g, 1)
            for h in range(2):
                for rows_i, table in ((dst_i, k.dst), (src_i, k.src)):
                    nc.gpsimd.indirect_dma_start(
                        rows_i[0:HALF, h, :], None, table.rearrange("(g e) -> g e", e=GROUP),
                        bass.IndirectOffsetOnAxis(ap=gcol_i[0:HALF, h:h + 1], axis=0)).then_inc(s_edges, 16)

        @block.vector
        def _(dve):
            v = nc.vector
            dve.wait_ge(s_last, 16)
            v.tensor_scalar(lastw_i[:, :], last_i[:, :], 7, None, ALU.arith_shift_right)
            dve.wait_ge(s_iota, 1)
            v.tensor_copy(k.iota_row[:, :], it_i[:, :])
            v.tensor_copy(k.iota_p[:, :], ip_i[:, :])
            v.tensor_copy(grp[:, :], grp_i[:, :])
            dve.drain()
            v.tensor_copy(lastw[:, :], lastw_i[:, :])
            v.tensor_copy(step_col[:, 0:1], k.iota_p[:, :])
            v.tensor_scalar(step_col[:, 1:2], k.iota_p[:, :], float(HALF), None, ALU.add)
            dve.drain()
            v.tensor_tensor(key[:, :], lastw[:, :], grp[:, :], ALU.add).then_inc(s_key, 1)
            dve.wait_ge(s_keyb, 1)
            for h in range(2):
                v.tensor_scalar(hits[:, :], pa[:, 0:GROUPS], step_col[:, h:h + 1], None, ALU.is_lt, ALU.add,
                                accum_out=gcol[:, h:h + 1])
                dve.drain()
            v.tensor_copy(gcol_i[:, :], gcol[:, :]).then_inc(s_g, 1)
            v.tensor_tensor(wcol[:, :], step_col[:, :], gcol[:, :], ALU.subtract)
            dve.drain()
            v.tensor_scalar(base[:, :], wcol[:, :], float(P), None, ALU.mult)
            dve.wait_ge(s_edges, 64)
            v.tensor_copy(dst[0:HALF], dst_i[0:HALF])
            v.tensor_copy(srcf[0:HALF], src_i[0:HALF])
            dve.drain().then_inc(s_dst, 1)
            for h in range(2):
                v.tensor_scalar(dloc[0:HALF, h, :], dst[0:HALF, h, :], base[0:HALF, h:h + 1], None, ALU.subtract)
            dve.drain()
            v.tensor_scalar(dloc[0:HALF], dloc[0:HALF], -1.0, float(P), ALU.max, ALU.min)
            v.tensor_tensor(same[0:HALF, :, 1:GROUP], dst[0:HALF, :, 1:GROUP], dst[0:HALF, :, 0:GROUP - 1],
                            ALU.is_equal)
            dve.drain()
            v.tensor_copy(dloc_b[0:HALF], dloc[0:HALF])
            v.memset(k.mask_t[:, :, 0:1], -BIG)
            v.memset(k.mask_t[:, :, GROUP:GROUP + 1], -BIG)
            v.tensor_scalar(k.mask_t[0:HALF, :, 1:GROUP], same[0:HALF, :, 1:GROUP], -1.0, BIG, ALU.add, ALU.mult)
            v.tensor_scalar(end[0:HALF, :, 0:GROUP - 1], same[0:HALF, :, 1:GROUP], -1.0, 1.0, ALU.mult, ALU.add)
            for h in range(2):
                for out, c in ((k.first_t, 0), (k.last_t, GROUP - 1)):
                    v.tensor_scalar(out[0:HALF, h, :], dst[0:HALF, h, :], dst[0:HALF, h, c:c + 1], None, ALU.is_equal)
            dve.drain()
            for out in (k.first_t, k.last_t):
                v.tensor_scalar(out[0:HALF], out[0:HALF], -1.0, BIG, ALU.add, ALU.mult)
            v.tensor_copy(mask_b[0:HALF, :, 1:GROUP], k.mask_t[0:HALF, :, 1:GROUP])
            dve.wait_ge(s_rows, 1)
            v.tensor_copy(rows[:, :, :], pc[0:1, 0:2 * STEPS].rearrange("o (a s) -> o a s", a=2))
            v.memset(cont[:, :], 0.0)
            dve.drain()
            v.tensor_tensor(cont[:, 1:STEPS], rows[:, 0, 1:STEPS], rows[:, 1, 0:STEPS - 1], ALU.is_equal)
            v.tensor_tensor(whole[:, :], rows[:, 0, :], rows[:, 1, :], ALU.is_equal)
            dve.drain()
            v.tensor_tensor(mrows[:, 0, :], whole[:, :], cont[:, 0:STEPS], ALU.mult)
            v.tensor_tensor(mrows[:, 1, :], whole[:, :], cont[:, 1:STEPS + 1], ALU.mult)
            v.tensor_copy(mrows[:, 2, :], cont[:, 0:STEPS])
            v.tensor_copy(mrows[:, 3, :], cont[:, 1:STEPS + 1])
            dve.drain()
            v.tensor_scalar(mrows[:, :, :], mrows[:, :, :], -1.0, BIG, ALU.add, ALU.mult).then_inc(s_mrow, 1)
            dve.wait_ge(s_mrowb, 1)
            v.tensor_copy(cont_c[0:HALF, :, :], pc[0:HALF, 0:4].rearrange("p (a h) -> p a h", a=2))
            v.tensor_copy(k.step_masks[:, 0:2, :], pa[0:HEADS, 0:2 * STEPS].rearrange("o (a s) -> o a s", a=2))
            dve.wait_ge(s_mrowb, 2)
            v.tensor_copy(k.step_masks[:, 2:4, :], pd[0:HEADS, 0:4, :].rearrange("o a s -> o (a s)")[:, 0:2 * STEPS]
                          .rearrange("o (a s) -> o a s", a=2))
            dve.drain()
            for h in range(2):
                v.tensor_scalar(mask_b[0:HALF, h, 0:1], cont_c[0:HALF, 0, h:h + 1], -1.0, BIG, ALU.add, ALU.mult)
                v.tensor_scalar(end[0:HALF, h, GROUP - 1:GROUP], cont_c[0:HALF, 1, h:h + 1], -1.0, 1.0,
                                ALU.mult, ALU.add)
            dve.drain().then_inc(s_end, 1)
            dve.wait_ge(s_cols, 1)
            for n, out in enumerate((k.dloc_e, k.end_e, k.src_e)):
                for h in range(2):
                    for j in range(2):
                        v.tensor_copy(out[:, 2 * HALF * h + j:2 * HALF * (h + 1):2], pd[:, 4 * n + 2 * h + j, 0:HALF])
            dve.wait_ge(s_winrow, 1)
            winrow = pc[0:1, 8:8 + STEPS].rearrange("o (i u) -> o i u", u=U)
            v.tensor_copy(wpack[:, :], winrow[:, :, U - 1])
            for u in reversed(range(U - 1)):
                dve.drain()
                v.scalar_tensor_tensor(wpack[:, :], wpack[:, :], float(1 << WBITS), winrow[:, :, u], ALU.mult, ALU.add)
            dve.drain()
            v.tensor_copy(k.win[:, :], wpack[:, :])
            dve.drain()

        @block.tensor
        def _(pe):
            t = nc.tensor
            pe.wait_ge(s_const, 1)
            pe.wait_ge(s_key, 1)
            t.matmul(pa[:, 0:GROUPS], k.ones_row[:, :], key[:, :], start=True, stop=True).then_inc(s_keyb, 1)
            pe.wait_ge(s_dst, 1)
            for a, c in ((0, 0), (1, GROUP - 1)):
                for h in range(2):
                    last = t.matmul(pc[0:1, a * STEPS + h * HALF:a * STEPS + (h + 1) * HALF],
                                    dst[0:HALF, h, c:c + 1], k.ident[0:HALF, 0:HALF], start=True, stop=True)
            last.then_inc(s_rows, 1)
            pe.wait_ge(s_mrow, 1)
            for a in range(2):
                for h in range(2):
                    t.matmul(pc[0:HALF, 2 * a + h:2 * a + h + 1], cont[:, a + h * HALF:a + (h + 1) * HALF],
                             k.ones_row[0:1, 0:1], start=True, stop=True)
            t.matmul(pa[0:HEADS, 0:2 * STEPS], k.ones_row[0:1, 0:HEADS], mrows[:, 0:2, :],
                     start=True, stop=True).then_inc(s_mrowb, 1)
            pm = pd[:, 0:4, :].rearrange("o a s -> o (a s)")
            t.matmul(pm[0:HEADS, 0:2 * STEPS], k.ones_row[0:1, 0:HEADS], mrows[:, 2:4, :],
                     start=True, stop=True).then_inc(s_mrowb, 1)
            pe.wait_ge(s_end, 1)
            for n, tt in enumerate((dloc, end, srcf)):
                for h in range(2):
                    for j in range(2):
                        last = t.transpose(pd[:, 4 * n + 2 * h + j, 0:HALF], tt[0:HALF, h, j * P:(j + 1) * P],
                                           k.ident[0:HALF, 0:HALF])
            last.then_inc(s_cols, 1)
            for h in range(2):
                last = t.matmul(pc[0:1, 8 + h * HALF:8 + (h + 1) * HALF], wcol[0:HALF, h:h + 1],
                                k.ident[0:HALF, 0:HALF], start=True, stop=True)
            last.then_inc(s_winrow, 1)


class Shared:

    def __init__(self, nc, ctx, arrays):
        self.x = arrays["x"]
        self.src = arrays["src"]
        self.dst = arrays["dst"]
        self.L0_gnn_W_in_b = arrays["L0_gnn_W_in_b"]
        self.L0_gnn_W_in_w = arrays["L0_gnn_W_in_w"]
        self.L0_gnn_W_out_b = arrays["L0_gnn_W_out_b"]
        self.L0_gnn_W_out_w = arrays["L0_gnn_W_out_w"]
        self.L0_gnn_W_upd_b = arrays["L0_gnn_W_upd_b"]
        self.L0_gnn_W_upd_w = arrays["L0_gnn_W_upd_w"]
        self.L0_gnn_ffn1_b = arrays["L0_gnn_ffn1_b"]
        self.L0_gnn_ffn1_w = arrays["L0_gnn_ffn1_w"]
        self.L0_gnn_ffn2_b = arrays["L0_gnn_ffn2_b"]
        self.L0_gnn_ffn2_w = arrays["L0_gnn_ffn2_w"]
        self.L0_gnn_ln1_b = arrays["L0_gnn_ln1_b"]
        self.L0_gnn_ln1_g = arrays["L0_gnn_ln1_g"]
        self.L0_gnn_ln2_b = arrays["L0_gnn_ln2_b"]
        self.L0_gnn_ln2_g = arrays["L0_gnn_ln2_g"]
        self.L1_gnn_Wk0 = arrays["L1_gnn_Wk0"]
        self.L1_gnn_Wk1 = arrays["L1_gnn_Wk1"]
        self.L1_gnn_Wq0 = arrays["L1_gnn_Wq0"]
        self.L1_gnn_Wq1 = arrays["L1_gnn_Wq1"]
        self.L1_gnn_Ws0 = arrays["L1_gnn_Ws0"]
        self.L1_gnn_Ws1 = arrays["L1_gnn_Ws1"]
        self.L1_gnn_Wv0 = arrays["L1_gnn_Wv0"]
        self.L1_gnn_Wv1 = arrays["L1_gnn_Wv1"]
        self.L1_gnn_bk0 = arrays["L1_gnn_bk0"]
        self.L1_gnn_bk1 = arrays["L1_gnn_bk1"]
        self.L1_gnn_bq0 = arrays["L1_gnn_bq0"]
        self.L1_gnn_bq1 = arrays["L1_gnn_bq1"]
        self.L1_gnn_bs0 = arrays["L1_gnn_bs0"]
        self.L1_gnn_bs1 = arrays["L1_gnn_bs1"]
        self.L1_gnn_bv0 = arrays["L1_gnn_bv0"]
        self.L1_gnn_bv1 = arrays["L1_gnn_bv1"]
        self.L2_gnn_W_l = arrays["L2_gnn_W_l"]
        self.L2_gnn_W_r = arrays["L2_gnn_W_r"]
        self.L2_gnn_att = arrays["L2_gnn_att"]
        self.L2_gnn_bias = arrays["L2_gnn_bias"]
        self.L2_gnn_ln_b = arrays["L2_gnn_ln_b"]
        self.L2_gnn_ln_w = arrays["L2_gnn_ln_w"]
        self.L3_gnn_W = arrays["L3_gnn_W"]
        self.L3_gnn_att_w = arrays["L3_gnn_att_w"]
        self.L3_gnn_b = arrays["L3_gnn_b"]
        self.L3_gnn_norm_b = arrays["L3_gnn_norm_b"]
        self.L3_gnn_norm_w = arrays["L3_gnn_norm_w"]
        self.nc, self.ctx, self.counts, self.names = nc, ctx, {}, {}

    def own(self, name):
        self.names[name] = self.names.get(name, -1) + 1
        return f"{name}_{self.names[name]}" if self.names[name] else name

    def fresh(self, name):
        return self.ctx.enter_context(self.nc.semaphore(name))

    def count(self, name, ahead=0, unit=1):
        if name not in self.counts:
            self.counts[name] = Count(self.fresh(name), ahead, unit)
        c = self.counts[name]
        c.ahead, c.unit = ahead, unit
        return c

    def close(self, n, *counts):
        for c in counts:
            c.base += (n + c.ahead) * c.unit


def onehot_phase(nc, k):
    UO = 5
    W = 4 * GROUP
    N = (STEPS * GROUP) // W
    with ExitStack() as ctx:
        local = ctx.enter_context(nc.sbuf_tensor(k.own("local_dst"), [P, UO, W], BF16))
        hot = ctx.enter_context(nc.sbuf_tensor(k.own("one_hot"), [P, UO, W], BF16))
        s_in = [ctx.enter_context(nc.semaphore(k.own(f"local_loaded{u}"))) for u in range(UO)]
        s_made = [ctx.enter_context(nc.semaphore(k.own(f"one_hot_made{u}"))) for u in range(UO)]
        s_out = [ctx.enter_context(nc.semaphore(k.own(f"one_hot_stored{u}"))) for u in range(UO)]
        block = ctx.enter_context(nc.Block())
        flat = k.dloc_dram.rearrange("s (o e) -> o (s e)", o=1)

        @block.sync
        def _(sp):
            with sp.Fori(0, N // UO) as i:
                for u in range(UO):
                    sp.wait_ge(s_made[u], i + 1)
                    sp.dma_start(local[:, u, :], flat[:, ds((i * UO + u) * W, W)].partition_broadcast(P)
                                 ).then_inc(s_in[u], 16)

        @block.vector
        def _(dve):
            for u in range(UO):
                dve.sem_inc(s_made[u])
            with dve.Fori(0, N // UO) as i:
                for u in range(UO):
                    dve.wait_ge(s_in[u], i * 16 + 16)
                    dve.wait_ge(s_out[u], i * 16 + 16)
                    nc.vector.tensor_scalar(hot[:, u, :], local[:, u, :], k.iota_p[:, 0:1], None, ALU.is_equal
                                            ).then_inc(s_made[u], 1)

        @block.scalar
        def _(act):
            for u in range(UO):
                act.sem_inc(s_out[u], 16)
            with act.Fori(0, N // UO) as i:
                for u in range(UO):
                    act.wait_ge(s_made[u], i + 2)
                    act.dma_start(k.hot_dram[:, ds((i * UO + u) * W, W)], hot[:, u, :]).then_inc(s_out[u], 16)
            for u in range(UO):
                act.wait_ge(s_out[u], 16 * (N // UO) + 16)



def norm_head(dve, x, w, var_made):
    v = w.vector
    v.tensor_reduce(w.mean[:, :], x, AXX, ALU.add)
    dve.drain()
    v.tensor_scalar(w.mean[:, :], w.mean[:, :], 1.0 / D, None, ALU.mult)
    dve.drain()
    v.tensor_tensor(w.c[:, :, :], x, w.mean[:, :].unsqueeze(2).broadcast_to([P, CH, D]), ALU.subtract)
    dve.drain()
    v.tensor_tensor(w.sq[:, :, :], w.c[:, :, :], w.c[:, :, :], ALU.mult)
    dve.drain()
    v.tensor_reduce(w.var[:, :], w.sq[:, :, :], AXX, ALU.add).then_inc(var_made.sem, 1)


def norm_sqrt(act, nc, w, var_made, sd_made, n):
    act.wait_ge(*var_made.done(n))
    nc.scalar.activation(w.sd[:, :], w.var[:, :], ACT.Sqrt, bias=w.eps[:, 0:1], scale=1.0 / D)\
      .then_inc(sd_made.sem, 1)


def norm_tail(dve, w, out, sd_made, n):
    v = w.vector
    dve.wait_ge(*sd_made.done(n))
    v.reciprocal(w.rstd[:, :], w.sd[:, :])
    dve.drain()
    v.tensor_tensor(out, w.c[:, :, :], w.rstd[:, :].unsqueeze(2).broadcast_to([P, CH, D]), ALU.mult)
    dve.drain()


def over_rows(row):
    return row.unsqueeze(1).broadcast_to([P, CH, D])


class Scratch:

    def __init__(self, nc, sb, name, eps):
        self.vector = nc.vector
        self.mean = sb(name + "_mean", [P, CH])
        self.var = sb(name + "_var", [P, CH])
        self.sd = sb(name + "_sd", [P, CH])
        self.rstd = sb(name + "_rstd", [P, CH])
        self.c = sb(name + "_c", [P, CH, D])
        self.sq = sb(name + "_sq", [P, CH, D])
        self.eps = eps


def chunk(t, i):
    return t[:, ds(i * CH, CH), :]


def rows_of(dram, i, width):
    return dram.rearrange("(w p) d -> p w d", p=P)[:, ds(i * CH, CH), 0:width]


def load_phase(nc, k):
    with ExitStack() as ctx:
        s_pad = ctx.enter_context(nc.semaphore(k.own("x_padding_cleared")))
        s_x = ctx.enter_context(nc.semaphore(k.own("x_loaded")))
        block = ctx.enter_context(nc.Block())

        @block.vector
        def _(dve):
            nc.vector.memset(k.X[:, WINDOWS - 1, :], 0.0).then_inc(s_pad, 1)
            nc.vector.memset(k.eps5[:, :], 1.0e-5)
            dve.drain()

        @block.sync
        def _(sp):
            sp.dma_start(k.X[:, 0:WINDOWS - 1, :], k.x[0:(WINDOWS - 1) * P, :].rearrange("(w p) d -> p w d", p=P))\
              .then_inc(s_x, 16)
            sp.wait_ge(s_pad, 1)
            sp.dma_start(k.X[0:LAST, WINDOWS - 1, :], k.x[(WINDOWS - 1) * P:NODES, :]).then_inc(s_x, 16)
            sp.wait_ge(s_x, 32)


def edge_conv_in_phase(nc, k):
    with ExitStack() as ctx:
        def sb(name, shape, dt=F32):
            return ctx.enter_context(nc.sbuf_tensor(k.own(name), shape, dt))
        wts = sb("w_in", [D, D])
        b = sb("b_in", [P, D])
        w = Scratch(nc, sb, "n0", k.eps5)
        h = sb("h", [P, CH, D])
        hT = sb("hT", [P, CH, D])
        g = sb("g", [P, CH, D])
        pT = ctx.enter_context(nc.psum_tensor(k.own("pT"), [P, 8, D], F32))
        pG = ctx.enter_context(nc.psum_tensor(k.own("pG"), [P, 8, D], F32))
        s_w = k.fresh("weights_in")
        var, sd, h_made, turned, hT_made, g_prod, g_made = (k.count(n) for n in (
            "var_made", "sd_made", "h_made", "h_turned", "hT_made", "g_product", "g_made"))
        g_out = k.count("rows_stored_chunk", 1, 16)
        with nc.Block() as block:
            @block.sync
            def _(sp):
                sp.dma_start(wts[:, :], k.L0_gnn_W_in_w).then_inc(s_w, 16)
                sp.dma_start(b[:, :], k.L0_gnn_W_in_b.rearrange("(o n) -> o n", o=1).partition_broadcast(P)).then_inc(s_w, 16)
                with sp.Fori(0, CHUNKS) as i:
                    sp.wait_ge(*g_made.done(i + 1))
                    sp.dma_start(rows_of(k.g_dram, i, D), g[:, :, :]).then_inc(g_out.sem, 16)
                sp.wait_ge(*g_out.done(CHUNKS))

            @block.vector
            def _(dve):
                v = nc.vector
                dve.wait_ge(s_w, 32)
                dve.sem_inc(g_out.sem, 16)
                with dve.Fori(0, CHUNKS) as i:
                    norm_head(dve, chunk(k.X, i), w, var)
                    norm_tail(dve, w, h[:, :, :], sd, i + 1)
                    v.tensor_scalar(h[:, :, :], h[:, :, :], 0.0, None, ALU.max)
                    dve.drain()
                    v.tensor_copy(chunk(k.H, i), h[:, :, :])
                    dve.drain().then_inc(h_made.sem, 1)
                    dve.wait_ge(*g_prod.done(i + 1))
                    dve.wait_ge(*g_out.free(i + 1, 1))
                    v.tensor_tensor(g[:, :, :], pG[:, 0:CH, :], over_rows(b[:, :]), ALU.add)
                    dve.drain().then_inc(g_made.sem, 1)
                    v.tensor_copy(chunk(k.G, i), g[:, :, :])
                    dve.drain()

            @block.scalar
            def _(act):
                with act.Fori(0, CHUNKS) as i:
                    norm_sqrt(act, nc, w, var, sd, i + 1)
                    act.wait_ge(*turned.done(i + 1))
                    nc.scalar.copy(hT[:, :, :], pT[:, 0:CH, :]).then_inc(hT_made.sem, 1)

            @block.tensor
            def _(pe):
                pe.wait_ge(s_w, 32)
                with pe.Fori(0, CHUNKS) as i:
                    pe.wait_ge(*h_made.done(i + 1))
                    for c in range(CH):
                        last = nc.tensor.transpose(pT[:, c, :], h[:, c, :], k.ident[:, :])
                    last.then_inc(turned.sem, 1)
                    pe.wait_ge(*hT_made.done(i + 1))
                    for c in range(CH):
                        last = nc.tensor.matmul(pG[:, c, :], hT[:, c, :], wts[:, :], start=True, stop=True)
                    last.then_inc(g_prod.sem, 1)
        k.close(CHUNKS, var, sd, h_made, turned, hT_made, g_prod, g_made, g_out)


def edge_max_phase(nc, k):
    with ExitStack() as ctx:
        def sb(name, shape, dt=F32):
            return ctx.enter_context(nc.sbuf_tensor(k.own(name), shape, dt))

        def pb(name):
            return ctx.enter_context(nc.psum_tensor(k.own(name), [P, 512], F32))
        idx = sb("staged_src", [P, 2, 4], I32)
        rows = sb("g_rows", [P, U, 2, D])
        mask = sb("mask_all", [P, 2, 2 * GROUP], BF16)
        scan = sb("running_max", [P, 2, GROUP])
        msg = sb("max_rows", [P, 2, 2, D + 4])
        sel = sb("select_end", [P, 2, 2, P])
        pT = [pb(f"gT{p}") for p in range(2)]
        pB = [pb(f"back{p}") for p in range(2)]
        pO = [pb(f"picked{p}") for p in range(2)]
        staged, turned, scanned, back, moved, selected, summed, added, passed = (k.count(n, a) for n, a in (
            ("src_staged", 0), ("rows_turned", U), ("max_scanned", U), ("max_turned_back", U),
            ("max_moved", U), ("selection_made", 0), ("window_summed", U), ("window_added", U), ("pool_passed", 0)))
        gathered = [k.count(f"rows_gathered{u}", 0, 32) for u in range(U)]
        masked = [k.count(f"mask_loaded{v}", 0, 16) for v in range(2)]
        flat = k.mask_dram.rearrange("s (o e) -> o (s e)", o=1)
        with nc.Block() as block:
            @block.sync
            def _(sp):
                with sp.Fori(0, ITERS) as i:
                    for h in range(2):
                        sp.wait_ge(*scanned.free(U * i + 2 * h + 2, U))
                        sp.dma_start(mask[:, h, :], flat[:, ds((2 * i + h) * 2 * GROUP, 2 * GROUP)].partition_broadcast(P)
                                     ).then_inc(masked[h].sem, 16)

            @block.gpsimd
            def _(pool):
                gather_rows(nc, k, pool, idx, rows, D, k.g_dram, staged, passed, (turned,), gathered)

            @block.tensor
            def _(pe):
                t = nc.tensor
                for c in (turned, back, summed):
                    pe.sem_inc(c.sem, U)

                def turn(i, u):
                    pe.wait_ge(*gathered[u].done(i + 1))
                    pe.wait_ge(*scanned.free(U * i + u + 1, 2))
                    for j in range(2):
                        last = t.transpose(pT[u % 2][:, j * P:(j + 1) * P], rows[:, u, j, :], k.ident[:, :])
                    last.then_inc(turned.sem, 1)

                def turn_back(i, u):
                    pe.wait_ge(*scanned.done(U * i + u + 1))
                    pe.wait_ge(*moved.free(U * i + u + 1, 2))
                    for j in range(2):
                        last = t.transpose(pB[u % 2][:, j * P:(j + 1) * P], scan[:, u % 2, j * P:(j + 1) * P],
                                           k.ident[:, :])
                    last.then_inc(back.sem, 1)

                def pick(i, u):
                    pe.wait_ge(*moved.done(U * i + u + 1))
                    pe.wait_ge(*selected.done(U * i + u + 1))
                    pe.wait_ge(*added.free(U * i + u + 1, 2))
                    for j in range(2):
                        last = t.matmul(pO[u % 2][:, 0:D + 1], sel[:, u % 2, j, :], msg[:, u % 2, j, 0:D + 1],
                                        start=(j == 0), stop=(j == 1))
                    last.then_inc(summed.sem, 1)

                with pe.Fori(0, ITERS) as i:
                    turn(i, 0)
                    turn(i, 1)
                    turn_back(i, 0)
                    turn(i, 2)
                    turn_back(i, 1)
                    pick(i, 0)
                    turn(i, 3)
                    turn_back(i, 2)
                    pick(i, 1)
                    turn_back(i, 3)
                    pick(i, 2)
                    pick(i, 3)

            @block.scalar
            def _(act):
                act.sem_inc(moved.sem, U)
                with act.Fori(0, ITERS) as i:
                    for u in range(U):
                        act.wait_ge(*back.done(U * i + u + 1))
                        act.wait_ge(*summed.free(U * i + u + 1, 2))
                        nc.scalar.copy(msg[:, u % 2, :, 0:D], pB[u % 2][:, 0:2 * P].rearrange("p (j d) -> p j d", j=2)
                                       ).then_inc(moved.sem, 1)

            @block.vector
            def _(dve):
                v = nc.vector
                v.memset(k.acc[:, 0:WINDOWS * (D + 1)], 0.0)
                v.memset(msg[:, :, :, D:D + 1], 1.0)
                v.memset(scan[:, 1, GROUP - 1:GROUP], -BIG)
                dve.drain()
                dve.sem_inc(scanned.sem, U)
                dve.sem_inc(added.sem, U)

                def run_max(i, u):
                    dve.drain()
                    dve.wait_ge(*turned.done(U * i + u + 1))
                    dve.wait_ge(*back.free(U * i + u + 1, 2))
                    if u % 2 == 0:
                        dve.wait_ge(*masked[u // 2].done(i + 1))
                    v.tensor_tensor_scan(scan[:, u % 2, :], mask[:, u // 2, (u % 2) * GROUP:(u % 2 + 1) * GROUP],
                                         pT[u % 2][:, 0:GROUP], scan[:, 1 - u % 2, GROUP - 1:GROUP], ALU.add, ALU.max
                                         ).then_inc(scanned.sem, 1)

                def select(i, u):
                    dve.wait_ge(*summed.free(U * i + u + 1, 2))
                    for j in range(2):
                        col = U * 2 * i + 2 * u + j
                        last = v.tensor_scalar(sel[:, u % 2, j, :], k.iota_row[:, :], k.dloc_e[:, ds(col, 1)],
                                               k.end_e[:, ds(col, 1)], ALU.is_equal, ALU.mult)
                    last.then_inc(selected.sem, 1)

                def add(i, u, win):
                    dve.drain()
                    dve.wait_ge(*summed.done(U * i + u + 1))
                    acc = k.acc[:, ds(win[u] * (D + 1), D + 1)]
                    v.tensor_tensor(acc, acc, pO[u % 2][:, 0:D + 1], ALU.add).then_inc(added.sem, 1)

                with dve.Fori(0, ITERS) as i:
                    win = windows_of(dve, k, i)
                    for u in range(U):
                        run_max(i, u)
                        select(i, u)
                        if u:
                            add(i, u - 1, win)
                    add(i, U - 1, win)
        k.close(STEPS, turned, scanned, back, moved, selected, summed, added)
        k.close(2 * ITERS, staged, passed)
        k.close(ITERS, *gathered, *masked)


def gather_rows(nc, k, pool, idx, rows, width, table, staged, passed, taken, gathered):
    with pool.Fori(0, ITERS) as i:
        for h in range(2):
            for c in taken:
                pool.wait_ge(*c.free(U * i + 2 * h + 2, U))
            pool.sem_inc(passed.sem)
            nc.gpsimd.tensor_copy(idx[:, h, :], k.src_e[:, ds(2 * U * i + 4 * h, 4)]).then_inc(staged.sem, 1)
            pool.wait_ge(*staged.done(2 * i + h + 1))
            pool.sem_inc(passed.sem)
            for n in range(4):
                u, j = 2 * h + n // 2, n % 2
                nc.gpsimd.indirect_dma_start(rows[:, u, j, 0:width], None, table,
                                             bass.IndirectOffsetOnAxis(ap=idx[:, h, n:n + 1], axis=0)
                                             ).then_inc(gathered[u].sem, 16)


def edge_conv_out_phase(nc, k):
    with ExitStack() as ctx:
        def sb(name, shape, dt=F32):
            return ctx.enter_context(nc.sbuf_tensor(k.own(name), shape, dt))

        def pb(name):
            return ctx.enter_context(nc.psum_tensor(k.own(name), [P, 8, D], F32))
        w_upd = sb("w_upd", [D, 2, D])
        w_out = sb("w_out", [D, D])
        w_f1 = sb("w_f1", [D, 4, D])
        w_f2 = sb("w_f2", [D, 4, D])
        b_upd = sb("b_upd", [D, 1])
        b_f1 = sb("b_f1", [D, 4])
        bc = sb("rows_bc", [P, 6, D])
        w = Scratch(nc, sb, "n1", k.eps5)
        md = sb("max_diff", [P, CH, D])
        gT = sb("gT", [P, CH, D])
        mT = sb("mT", [P, CH, D])
        uT = sb("uT", [P, CH, D])
        x1 = sb("x1", [P, CH, D])
        x1T = sb("x1T", [P, CH, D])
        y = sb("y", [P, CH, D])
        fT = sb("fT", [P, 4, CH, D])
        pA, pB, pC, pD = pb("pA"), pb("pB"), pb("pC"), pb("pD")
        s_w = k.fresh("weights_out")
        (md_made, turned, gT_made, u_prod, uT_made, o_prod, var, sd, x1_made, x1_turned, x1T_made, f_prod, f_made,
         y_prod, chunk_done) = (k.count(n) for n in (
             "h_made", "h_turned", "hT_made", "u_product", "uT_made", "o_product", "var_made", "sd_made",
             "x1_made", "x1_turned", "x1T_made", "ffn_product", "ffn_made", "y_product", "chunk_done"))
        srcs = ((w_upd[:, :, :], k.L0_gnn_W_upd_w.rearrange("(c p) n -> p c n", p=D)),
                (w_out[:, :], k.L0_gnn_W_out_w),
                (w_f1[:, :, :], k.L0_gnn_ffn1_w.rearrange("p (c n) -> p c n", n=D)),
                (w_f2[:, :, :], k.L0_gnn_ffn2_w.rearrange("(c p) n -> p c n", p=D)),
                (b_upd[:, :], k.L0_gnn_W_upd_b.rearrange("(p o) -> p o", o=1)),
                (b_f1[:, :], k.L0_gnn_ffn1_b.rearrange("(c p) -> p c", p=D)))
        rows = (k.L0_gnn_W_out_b, k.L0_gnn_ln1_g, k.L0_gnn_ln1_b, k.L0_gnn_ffn2_b, k.L0_gnn_ln2_g, k.L0_gnn_ln2_b)
        loaded = 16 * (len(srcs) + len(rows))
        with nc.Block() as block:
            @block.sync
            def _(sp):
                with nc.allow_non_contiguous_dma(reason="small columns of biases"):
                    for out, src in srcs:
                        sp.dma_start(out, src).then_inc(s_w, 16)
                for n, row in enumerate(rows):
                    sp.dma_start(bc[:, n, :], row.rearrange("(o n) -> o n", o=1).partition_broadcast(P)).then_inc(s_w, 16)

            @block.vector
            def _(dve):
                v = nc.vector
                acc = k.acc[:, 0:WINDOWS * (D + 1)].rearrange("p (w d) -> p w d", d=D + 1)
                dve.wait_ge(s_w, loaded)
                with dve.Fori(0, CHUNKS) as i:
                    a = acc[:, ds(i * CH, CH), :]
                    v.tensor_tensor(md[:, :, :], chunk(k.G, i), a[:, :, D:D + 1].broadcast_to([P, CH, D]), ALU.mult)
                    v.tensor_copy(y[:, :, :], chunk(k.G, i))
                    dve.drain()
                    v.tensor_tensor(md[:, :, :], a[:, :, 0:D], md[:, :, :], ALU.subtract).then_inc(md_made.sem, 1)
                    dve.wait_ge(*o_prod.done(i + 1))
                    v.tensor_tensor(x1[:, :, :], pA[:, 0:CH, :], over_rows(bc[:, 0, :]), ALU.add)
                    dve.drain()
                    v.tensor_tensor(x1[:, :, :], x1[:, :, :], chunk(k.H, i), ALU.add)
                    dve.drain()
                    norm_head(dve, x1[:, :, :], w, var)
                    norm_tail(dve, w, x1[:, :, :], sd, 2 * i + 1)
                    v.tensor_tensor(x1[:, :, :], x1[:, :, :], over_rows(bc[:, 1, :]), ALU.mult)
                    dve.drain()
                    v.tensor_tensor(x1[:, :, :], x1[:, :, :], over_rows(bc[:, 2, :]), ALU.add).then_inc(x1_made.sem, 1)
                    dve.wait_ge(*y_prod.done(i + 1))
                    v.tensor_tensor(y[:, :, :], pB[:, 0:CH, :], over_rows(bc[:, 3, :]), ALU.add)
                    dve.drain()
                    v.tensor_tensor(y[:, :, :], y[:, :, :], x1[:, :, :], ALU.add)
                    dve.drain()
                    norm_head(dve, y[:, :, :], w, var)
                    norm_tail(dve, w, y[:, :, :], sd, 2 * i + 2)
                    v.tensor_tensor(y[:, :, :], y[:, :, :], over_rows(bc[:, 4, :]), ALU.mult)
                    dve.drain()
                    v.tensor_tensor(y[:, :, :], y[:, :, :], over_rows(bc[:, 5, :]), ALU.add)
                    dve.drain()
                    v.tensor_tensor(chunk(k.X, i), chunk(k.X, i), y[:, :, :], ALU.add)
                    dve.drain().then_inc(chunk_done.sem, 1)

            @block.scalar
            def _(act):
                s = nc.scalar
                with act.Fori(0, CHUNKS) as i:
                    act.wait_ge(*turned.done(i + 1))
                    s.copy(gT[:, :, :], pA[:, 0:CH, :])
                    s.copy(mT[:, :, :], pB[:, 0:CH, :]).then_inc(gT_made.sem, 1)
                    act.wait_ge(*u_prod.done(i + 1))
                    s.activation(uT[:, :, :], pC[:, 0:CH, :], ACT.Identity, bias=b_upd[:, 0:1]).then_inc(uT_made.sem, 1)
                    norm_sqrt(act, nc, w, var, sd, 2 * i + 1)
                    act.wait_ge(*x1_turned.done(i + 1))
                    s.copy(x1T[:, :, :], pA[:, 0:CH, :]).then_inc(x1T_made.sem, 1)
                    for f in range(4):
                        act.wait_ge(*f_prod.done(4 * i + f + 1))
                        s.activation(fT[:, f, :, :], (pC, pD)[f % 2][:, 0:CH, :], ACT.Gelu, bias=b_f1[:, f:f + 1]
                                     ).then_inc(f_made.sem, 1)
                    norm_sqrt(act, nc, w, var, sd, 2 * i + 2)

            @block.tensor
            def _(pe):
                t = nc.tensor

                def wide(out, lhsT, rhs, start, stop):
                    t.matmul(out[:, 0:4, :], lhsT, rhs[:, 0:4, :], start=start, stop=stop)
                    return t.matmul(out[:, 4:CH, :], lhsT, rhs[:, 4:CH, :], start=start, stop=stop)
                pe.wait_ge(s_w, loaded)

                with pe.Fori(0, CHUNKS) as i:
                    pe.wait_ge(*md_made.done(i + 1))
                    for c in range(CH):
                        t.transpose(pA[:, c, :], y[:, c, :], k.ident[:, :])
                        last = t.transpose(pB[:, c, :], md[:, c, :], k.ident[:, :])
                    last.then_inc(turned.sem, 1)
                    pe.wait_ge(*gT_made.done(i + 1))
                    wide(pC, w_upd[:, 0, :], gT, True, False)
                    wide(pC, w_upd[:, 1, :], mT, False, True).then_inc(u_prod.sem, 1)
                    pe.wait_ge(*uT_made.done(i + 1))
                    for c in range(CH):
                        last = t.matmul(pA[:, c, :], uT[:, c, :], w_out[:, :], start=True, stop=True)
                    last.then_inc(o_prod.sem, 1)
                    pe.wait_ge(*x1_made.done(i + 1))
                    for c in range(CH):
                        last = t.transpose(pA[:, c, :], x1[:, c, :], k.ident[:, :])
                    last.then_inc(x1_turned.sem, 1)
                    pe.wait_ge(*x1T_made.done(i + 1))
                    for f in range(4):
                        if f >= 2:
                            pe.wait_ge(*f_made.done(4 * i + f - 1))
                        wide((pC, pD)[f % 2], w_f1[:, f, :], x1T, True, True).then_inc(f_prod.sem, 1)
                    pe.wait_ge(*f_made.done(4 * i + 4))
                    for c in range(CH):
                        for f in range(4):
                            last = t.matmul(pB[:, c, :], fT[:, f, c, :], w_f2[:, f, :], start=(f == 0), stop=(f == 3))
                    last.then_inc(y_prod.sem, 1)
        k.close(CHUNKS, md_made, turned, gT_made, u_prod, uT_made, o_prod, x1_made, x1_turned, x1T_made, y_prod,
                chunk_done)
        k.close(2 * CHUNKS, var, sd)
        k.close(4 * CHUNKS, f_prod, f_made)



def split3(dve, nc, full, hi, mid, lo, rest):
    v = nc.vector
    v.tensor_copy(hi, full)
    dve.drain()
    v.tensor_tensor(rest, full, hi, ALU.subtract)
    dve.drain()
    v.tensor_copy(mid, rest)
    dve.drain()
    return v.tensor_tensor(lo, rest, mid, ALU.subtract)


def conv1_in_phase(nc, k):
    with ExitStack() as ctx:
        def sb(name, shape, dt=F32):
            return ctx.enter_context(nc.sbuf_tensor(k.own(name), shape, dt))

        def pb(name, shape):
            return ctx.enter_context(nc.psum_tensor(k.own(name), shape, F32))
        wq = sb("wq", [D, HEADS, D])
        wk = sb("wk", [D, HEADS, D])
        wkT = sb("wkT", [D, HEADS, D + 1])
        bq = sb("bq", [D, HEADS])
        w = Scratch(nc, sb, "n2", k.eps5)
        h = sb("h", [P, CH, D + 4])
        hT = sb("hT", [P, CH, D])
        qT = sb("qT", [P, HEADS, CH, D])
        rest = sb("rest", [P, HEADS, D + 1])
        pT = pb("pT", [P, 8, D])
        pQ = pb("pQ", [P, 8, D])
        pU = [pb(f"pU{n}", [P, HEADS, 256]) for n in range(2)]
        s_w = k.fresh("weights_conv1")
        s_k = k.fresh("wk_turned")
        s_kT = k.fresh("wkT_made")
        var, sd, h_made, turned, hT_made = (k.count(n) for n in (
            "var_made", "sd_made", "h_made", "h_turned", "hT_made"))
        h_out = k.count("rows_stored_chunk", 1, 16)
        q_prod, qT_made = k.count("q_product"), k.count("qT_made", 1)
        u_prod, u_split = k.count("u_product"), k.count("u_split", 2)
        with nc.Block() as block:
            @block.sync
            def _(sp):
                with nc.allow_non_contiguous_dma(reason="small columns of biases"):
                    sp.dma_start(wq[:, :, :], k.L1_gnn_Wq0.rearrange("p (h n) -> p h n", n=D)).then_inc(s_w, 16)
                    sp.dma_start(wk[:, :, :], k.L1_gnn_Wk0.rearrange("p (h n) -> p h n", n=D)).then_inc(s_w, 16)
                    sp.dma_start(bq[:, :], k.L1_gnn_bq0.rearrange("(h p) -> p h", p=D)).then_inc(s_w, 16)
                    sp.dma_start(wkT[:, :, D], k.L1_gnn_bk0.rearrange("(h p) -> p h", p=D)).then_inc(s_w, 16)
                with sp.Fori(0, CHUNKS) as i:
                    sp.wait_ge(*h_made.done(i + 1))
                    sp.dma_start(rows_of(k.h_dram, i, D + 4), h[:, :, :]).then_inc(h_out.sem, 16)
                sp.wait_ge(*h_out.done(CHUNKS))

            @block.vector
            def _(dve):
                v = nc.vector
                dve.wait_ge(s_w, 64)
                v.memset(h[:, :, D:D + 4], 1.0)
                dve.wait_ge(s_k, 1)
                v.tensor_copy(wkT[:, :, 0:D], pT[:, 0:HEADS, :])
                dve.drain().then_inc(s_kT, 1)
                dve.sem_inc(h_out.sem, 16)
                dve.sem_inc(u_split.sem, 2)
                with dve.Fori(0, CHUNKS) as i:
                    norm_head(dve, chunk(k.X, i), w, var)
                    dve.wait_ge(*h_out.free(i + 1, 1))
                    norm_tail(dve, w, h[:, :, 0:D], sd, i + 1)
                    v.tensor_scalar(h[:, :, 0:D], h[:, :, 0:D], 0.0, None, ALU.max)
                    dve.drain()
                    v.tensor_copy(chunk(k.H, i), h[:, :, 0:D])
                    dve.drain().then_inc(h_made.sem, 1)
                    for c in range(CH):
                        dve.wait_ge(*u_prod.done(CH * i + c + 1))
                        part = [k.U[:, ds(i * (CH * 3 * HW1) + (3 * c + n) * HW1, HW1)]
                                .rearrange("p (h d) -> p h d", h=HEADS) for n in range(3)]
                        split3(dve, nc, pU[c % 2][:, :, 0:D + 1], *part, rest[:, :, :])
                        dve.drain().then_inc(u_split.sem, 1)

            @block.scalar
            def _(act):
                act.sem_inc(qT_made.sem, 1)
                act.wait_ge(s_w, 64)
                with act.Fori(0, CHUNKS) as i:
                    norm_sqrt(act, nc, w, var, sd, i + 1)
                    act.wait_ge(*turned.done(i + 1))
                    nc.scalar.copy(hT[:, :, :], pT[:, 0:CH, :]).then_inc(hT_made.sem, 1)
                    for hh in range(HEADS):
                        act.wait_ge(*q_prod.done(HEADS * i + hh + 1))
                        nc.scalar.activation(qT[:, hh, :, :], pQ[:, 0:CH, :], ACT.Identity, bias=bq[:, hh:hh + 1]
                                             ).then_inc(qT_made.sem, 1)

            @block.tensor
            def _(pe):
                t = nc.tensor
                pe.wait_ge(s_w, 64)
                for hh in range(HEADS):
                    last = t.transpose(pT[:, hh, :], wk[:, hh, :], k.ident[:, :])
                last.then_inc(s_k, 1)
                pe.wait_ge(s_kT, 1)
                with pe.Fori(0, CHUNKS) as i:
                    pe.wait_ge(*h_made.done(i + 1))
                    for c in range(CH):
                        last = t.transpose(pT[:, c, :], h[:, c, 0:D], k.ident[:, :])
                    last.then_inc(turned.sem, 1)
                    pe.wait_ge(*hT_made.done(i + 1))
                    for hh in range(HEADS):
                        pe.wait_ge(*qT_made.free(HEADS * i + hh + 1, 1))
                        t.matmul(pQ[:, 0:4, :], wq[:, hh, :], hT[:, 0:4, :], start=True, stop=True)
                        t.matmul(pQ[:, 4:CH, :], wq[:, hh, :], hT[:, 4:CH, :], start=True, stop=True
                                 ).then_inc(q_prod.sem, 1)
                    pe.wait_ge(*qT_made.done(HEADS * i + HEADS))
                    for c in range(CH):
                        pe.wait_ge(*u_split.free(CH * i + c + 1, 2))
                        for hh in range(HEADS):
                            last = t.matmul(pU[c % 2][:, hh, 0:D + 1], qT[:, hh, c, :], wkT[:, hh, :],
                                            start=True, stop=True)
                        last.then_inc(u_prod.sem, 1)
        k.close(CHUNKS, var, sd, h_made, turned, hT_made, h_out)
        k.close(HEADS * CHUNKS, q_prod, qT_made)
        k.close(WINDOWS, u_prod, u_split)


def edge_logits_phase(nc, k, table, width, per_head, row, mode="dot"):
    per = row // HEADS
    banks = 2 if row > 512 else 1
    bw = row // banks
    with ExitStack() as ctx:
        def sb(name, shape, dt=F32):
            return ctx.enter_context(nc.sbuf_tensor(k.own(name), shape, dt))
        idx = sb("staged_src", [P, 2, 4], I32)
        rows = sb("src_rows", [P, U, 2, width])
        hot = sb("one_hot", [P, 2, 2 * GROUP], BF16)
        prod = sb("products", [P, 2, row])
        msg = sb("messages", [P, 2, row])
        pU = [ctx.enter_context(nc.psum_tensor(k.own(f"dst_rows{n}"), [P, banks, 512], F32)) for n in range(4)]
        staged, picked, dotted, passed = (k.count(n, a) for n, a in (
            ("src_staged", 0), ("dst_rows_picked", 0), ("logits_made", U), ("pool_passed", 0)))
        gathered = [k.count(f"rows_gathered{u}", 0, 32) for u in range(U)]
        loaded = [k.count(f"mask_loaded{v}", 0, 16) for v in range(2)]
        with nc.Block() as block:
            @block.sync
            def _(sp):
                with sp.Fori(0, ITERS) as i:
                    for h in range(2):
                        sp.wait_ge(*dotted.free(U * i + 2 * h + 2, U))
                        sp.dma_start(hot[:, h, :], k.hot_dram[:, ds((2 * i + h) * 2 * GROUP, 2 * GROUP)]
                                     ).then_inc(loaded[h].sem, 16)

            @block.gpsimd
            def _(pool):
                gather_rows(nc, k, pool, idx, rows, width, table, staged, passed, (dotted,), gathered)

            @block.tensor
            def _(pe):
                with pe.Fori(0, ITERS) as i:
                    win = windows_of(pe, k, i)
                    for u in range(U):
                        pe.wait_ge(*dotted.free(U * i + u + 1, 2))
                        if u % 2 == 0:
                            pe.wait_ge(*loaded[u // 2].done(i + 1))
                        for j in range(2):
                            lhsT = hot[:, u // 2, (u % 2) * GROUP + j * P:(u % 2) * GROUP + (j + 1) * P]
                            for part in range(3):
                                for b in range(banks):
                                    last = nc.tensor.matmul(
                                        pU[2 * (u % 2) + j][:, b, 0:bw], lhsT,
                                        k.U[:, ds(win[u] * (3 * row) + (part * row + b * bw), bw)],
                                        start=(part == 0), stop=(part == 2))
                        last.then_inc(picked.sem, 1)

            @block.vector
            def _(dve):
                v = nc.vector
                dve.sem_inc(dotted.sem, U)

                def dot(src_rows, dst_rows, cols):
                    hb = HEADS // banks
                    for j in range(2):
                        for b in range(banks):
                            if per_head:
                                src = src_rows[:, j, b * bw:(b + 1) * bw].rearrange("p (h d) -> p h d", h=hb)
                            else:
                                src = src_rows[:, j, 0:per].unsqueeze(1).broadcast_to([P, hb, per])
                            v.tensor_tensor(prod[:, j, b * bw:(b + 1) * bw].rearrange("p (h d) -> p h d", h=hb),
                                            dst_rows[j][:, b, 0:bw].rearrange("p (h d) -> p h d", h=hb), src, ALU.mult)
                    dve.drain()
                    return v.tensor_reduce(k.logits[:, :, cols].rearrange("p h t -> p t h"),
                                           prod[:, :, :].rearrange("p t (h d) -> p t h d", h=HEADS), AXX, ALU.add)

                def gat(src_rows, dst_rows, cols):
                    for j in range(2):
                        v.tensor_tensor(msg[:, j, 0:D], dst_rows[j][:, 0, 0:D], src_rows[:, j, 0:D], ALU.add)
                        v.tensor_copy(prod[:, j, D:D + 1], dst_rows[j][:, 0, D:D + 1])
                    dve.drain()
                    v.scalar_tensor_tensor(prod[:, :, 0:D], msg[:, :, 0:D], 0.2, msg[:, :, 0:D], ALU.mult, ALU.max)
                    v.tensor_copy(k.selfs[:, cols], prod[:, :, D])
                    dve.drain()
                    v.tensor_tensor(msg[:, :, 0:D], prod[:, :, 0:D], k.att[:, :].unsqueeze(1).broadcast_to([P, 2, D]),
                                    ALU.mult)
                    dve.drain()
                    return v.tensor_reduce(k.logits[:, 0, cols], msg[:, :, 0:D], AXX, ALU.add)

                with dve.Fori(0, ITERS) as i:
                    for u in range(U):
                        dve.drain()
                        dve.wait_ge(*gathered[u].done(i + 1))
                        dve.wait_ge(*picked.done(U * i + u + 1))
                        cols = ds(2 * U * i + 2 * u, 2)
                        dst_rows = [pU[2 * (u % 2) + j] for j in range(2)]
                        if mode == "dot":
                            last = dot(rows[:, u], dst_rows, cols)
                        elif mode == "gat":
                            last = gat(rows[:, u], dst_rows, cols)
                        else:
                            for j in range(2):
                                last = v.tensor_tensor(k.logits[:, 0, ds(2 * U * i + 2 * u + j, 1)], rows[:, u, j, 0:1],
                                                       dst_rows[j][:, 0, 0:1], ALU.add)
                        last.then_inc(dotted.sem, 1)
        k.close(STEPS, picked, dotted)
        k.close(2 * ITERS, staged, passed)
        k.close(ITERS, *gathered, *loaded)


def segment_softmax_phase(nc, k, heads, scale, with_self=False):
    with ExitStack() as ctx:
        def sb(name, shape, dt=F32):
            return ctx.enter_context(nc.sbuf_tensor(k.own(name), shape, dt))

        def pb(name, shape):
            return ctx.enter_context(nc.psum_tensor(k.own(name), shape, F32))
        N = heads + 2 * with_self
        lt = sb("logits_t", [P, N, 2, GROUP])
        m = sb("max_t", [P, heads, 2, GROUP])
        mf = sb("max_fwd_t", [P, heads, 2, GROUP])
        edge = sb("step_ends", [HEADS, 2, STEPS])
        run = sb("running", [HEADS, 2, STEPS])
        carry = sb("carry", [HEADS, 2, STEPS])
        cc = sb("carry_t", [P, 2, 2, HEADS])
        pt = pb("pt", [P, 4, 2, GROUP])
        pr = pb("pr", [P, 512])
        pe_back = pb("pcol", [P, 4, 2, P])
        names = ("sm_turned", "sm_local", "sm_ends", "sm_carry", "sm_carry_turned", "sm_diff", "sm_exp", "sm_exp_turned",
                 "sm_done")
        turned, local, ends, carried, carry_t, diff, exped, exp_turned, back = (k.count(n) for n in names)
        HH = HALF
        with nc.Block() as block:
            @block.tensor
            def _(pe):
                t = nc.tensor
                for n in range(N):
                    src = (k.logits[:, n, :] if n < heads else (k.selfs, k.end_e)[n - heads][:, :])
                    for h in range(2):
                        for j in range(2):
                            last = t.transpose(pt[0:HH, n, h, j * P:(j + 1) * P],
                                               src[:, 2 * HH * h + j:2 * HH * (h + 1):2], k.ident[:, :])
                last.then_inc(turned.sem, 1)
                pe.wait_ge(*local.done(1))
                for a, c in ((0, GROUP - 1), (1, 0)):
                    for h in range(2):
                        last = t.matmul(pr[0:heads, a * STEPS + h * HH:a * STEPS + (h + 1) * HH],
                                        m[0:HH, :, h, c], k.ident[0:HH, 0:HH], start=True, stop=True)
                last.then_inc(ends.sem, 1)
                pe.wait_ge(*carried.done(1))
                for a in range(2):
                    for h in range(2):
                        o = (2 * a + h) * HEADS
                        last = t.matmul(pr[0:HH, o:o + heads], carry[0:heads, a, h * HH:(h + 1) * HH],
                                        k.ident[0:heads, 0:heads], start=True, stop=True)
                last.then_inc(carry_t.sem, 1)
                pe.wait_ge(*exped.done(1))
                M = heads + with_self
                for h in range(2):
                    if h:
                        pe.wait_ge(*back.done(1))
                    for n in range(M):
                        for j in range(2):
                            last = t.transpose(pe_back[:, n, j, 0:HH], lt[0:HH, n, h, j * P:(j + 1) * P],
                                               k.ident[0:HH, 0:HH])
                    last.then_inc(exp_turned.sem, 1)

            @block.vector
            def _(dve):
                v = nc.vector
                dve.wait_ge(*turned.done(1))
                v.tensor_scalar(lt[0:HH], pt[0:HH, 0:N], scale, None, ALU.mult)
                dve.drain()
                top = lt
                if with_self:
                    v.tensor_tensor(mf[0:HH, 0], lt[0:HH, 0], lt[0:HH, 1], ALU.max)
                    dve.drain()
                    v.tensor_copy(m[0:HH, 0], mf[0:HH, 0])
                    dve.drain()
                    top = m
                for n in range(heads):
                    for h in range(2):
                        v.tensor_tensor_scan(mf[0:HH, n, h, :], k.mask_t[0:HH, h, 0:GROUP], top[0:HH, n, h, :], -BIG,
                                             ALU.add, ALU.max)
                dve.drain()
                for n in range(heads):
                    for h in range(2):
                        v.tensor_tensor_scan(m[0:HH, n, h, ::-1], k.mask_t[0:HH, h, GROUP:0:-1], mf[0:HH, n, h, ::-1],
                                             -BIG, ALU.add, ALU.max)
                dve.drain().then_inc(local.sem, 1)
                dve.wait_ge(*ends.done(1))
                v.tensor_copy(edge[0:heads], pr[0:heads, 0:2 * STEPS].rearrange("p (a s) -> p a s", a=2))
                v.memset(carry[0:heads], -BIG)
                dve.drain()
                v.tensor_tensor_scan(run[0:heads, 0, :], k.step_masks[0:heads, 0, :], edge[0:heads, 0, :], -BIG,
                                     ALU.add, ALU.max)
                v.tensor_tensor_scan(run[0:heads, 1, ::-1], k.step_masks[0:heads, 1, ::-1], edge[0:heads, 1, ::-1],
                                     -BIG, ALU.add, ALU.max)
                dve.drain()
                v.tensor_tensor(carry[0:heads, 0, 1:STEPS], run[0:heads, 0, 0:STEPS - 1],
                                k.step_masks[0:heads, 2, 1:STEPS], ALU.add)
                v.tensor_tensor(carry[0:heads, 1, 0:STEPS - 1], run[0:heads, 1, 1:STEPS],
                                k.step_masks[0:heads, 3, 0:STEPS - 1], ALU.add)
                dve.drain().then_inc(carried.sem, 1)
                dve.wait_ge(*carry_t.done(1))
                v.tensor_copy(cc[0:HH, :, :, 0:heads], pr[0:HH, 0:4 * HEADS].rearrange(
                    "p (a h n) -> p a h n", a=2, h=2)[:, :, :, 0:heads])
                for a, seg in enumerate((k.first_t, k.last_t)):
                    dve.drain()
                    for n in range(heads):
                        for h in range(2):
                            v.scalar_tensor_tensor(m[0:HH, n, h, :], seg[0:HH, h, :], cc[0:HH, a, h, n:n + 1],
                                                   m[0:HH, n, h, :], ALU.add, ALU.max)
                dve.drain()
                v.tensor_tensor(lt[0:HH, 0:heads], lt[0:HH, 0:heads], m[0:HH], ALU.subtract)
                if with_self:
                    v.tensor_tensor(lt[0:HH, 1], lt[0:HH, 1], m[0:HH, 0], ALU.subtract)
                dve.drain().then_inc(diff.sem, 1)
                M = heads + with_self
                for h in range(2):
                    dve.wait_ge(*exp_turned.done(h + 1))
                    for n in range(M):
                        out = k.logits[:, n, :] if n < heads else k.selfs[:, :]
                        v.tensor_copy(out[:, 2 * HH * h:2 * HH * (h + 1)].rearrange("p (s j) -> p j s", j=2),
                                      pe_back[:, n, :, 0:HH])
                    dve.drain().then_inc(back.sem, 1)
                if with_self:
                    v.tensor_tensor(k.ends[:, :, 0], k.selfs[:, :], k.end_e[:, :], ALU.mult)
                    v.tensor_copy(k.ends[:, :, 1], k.end_e[:, :])
                    dve.drain()

            @block.scalar
            def _(act):
                act.wait_ge(*diff.done(1))
                nc.scalar.activation(lt[0:HH, 0:heads + with_self], lt[0:HH, 0:heads + with_self], ACT.Exp
                                     ).then_inc(exped.sem, 1)
        k.close(1, turned, local, ends, carried, carry_t, diff, exped)
        k.close(2, back, exp_turned)


def edge_sum_phase(nc, k, table, width, blocks, out_dram):
    size = sum(b[2] for b in blocks)
    banks = -(-size // 512)
    bw = size // banks
    weighted = [b for b in blocks if b[0] is not None]
    plain = [b for b in blocks if b[0] is None]
    on_dve = weighted[:1] if len(weighted) > 1 else []
    on_act = weighted[len(on_dve):]
    wide = sum(b[2] for b in weighted)
    ahead = 2
    with ExitStack() as ctx:
        def sb(name, shape, dt=F32):
            return ctx.enter_context(nc.sbuf_tensor(k.own(name), shape, dt))
        acc = sb("sums", [P, WINDOWS * size])
        sel = sb("selection", [P, U, 2, P])
        if weighted:
            idx = sb("staged_src", [P, 2, 4], I32)
            rows = sb("src_rows", [P, U, 2, width])
            msg = sb("weighted_rows", [P, U, 2, wide])
        pO = [ctx.enter_context(nc.psum_tensor(k.own(f"window_sum{p}"), [P, banks, 512], F32)) for p in range(U)]
        staged, selected, weighed, summed, added, passed, act_passed = (k.count(n, a) for n, a in (
            ("src_staged", 0), ("selection_made", U), ("rows_weighed", U), ("window_summed", U), ("window_added", U),
            ("pool_passed", 0), ("act_passed", 0)))
        gathered = [k.count(f"rows_gathered{u}", 0, 32) for u in range(U)]
        s_out = k.count("sums_stored", 0, 16)
        with nc.Block() as block:
            if weighted:
                @block.gpsimd
                def _(pool):
                    gather_rows(nc, k, pool, idx, rows, width, table, staged, passed,
                                (selected, weighed) if on_dve else (weighed,), gathered)

                @block.scalar
                def _(act):
                    act.sem_inc(weighed.sem, U)
                    with act.Fori(0, ITERS) as i:
                        for u in range(U):
                            act.wait_ge(*gathered[u].done(i + 1))
                            act.wait_ge(*summed.free(U * i + u + 1, U))
                            act.sem_inc(act_passed.sem)
                            for j in range(2):
                                at = sum(b[2] for b in on_dve)
                                for weight, col, n in on_act:
                                    last = nc.scalar.activation(msg[:, u, j, at:at + n], rows[:, u, j, col:col + n],
                                                                ACT.Copy, scale=weight[:, ds(U * 2 * i + 2 * u + j, 1)])
                                    at += n
                            last.then_inc(weighed.sem, 1)

            @block.vector
            def _(dve):
                v = nc.vector
                v.memset(acc[:, :], 0.0)
                dve.sem_inc(selected.sem, U)
                dve.sem_inc(added.sem, U)

                def prepare(i, u):
                    dve.wait_ge(*summed.free(U * i + u + 1, U))
                    for j in range(2):
                        last = v.tensor_scalar(sel[:, u, j, :], k.iota_row[:, :],
                                               k.dloc_e[:, ds(U * 2 * i + 2 * u + j, 1)], None, ALU.is_equal)
                    if on_dve:
                        dve.wait_ge(*gathered[u].done(i + 1))
                        for j in range(2):
                            for weight, col, n in on_dve:
                                last = v.tensor_scalar(msg[:, u, j, 0:n], rows[:, u, j, col:col + n],
                                                       weight[:, ds(U * 2 * i + 2 * u + j, 1)], None, ALU.mult)
                    last.then_inc(selected.sem, 1)

                def add(i, u, win):
                    dve.drain()
                    dve.wait_ge(*summed.done(U * i + u + 1))
                    a = acc[:, ds(win[u] * size, size)].rearrange("p (b n) -> p b n", b=banks)
                    v.tensor_tensor(a, a, pO[u][:, :, 0:bw], ALU.add).then_inc(added.sem, 1)

                for u in range(ahead):
                    prepare(0, u)
                with dve.Fori(0, ITERS - 1) as i:
                    win = windows_of(dve, k, i)
                    for u in range(U):
                        prepare(i + (u + ahead) // U, (u + ahead) % U)
                        add(i, u, win)
                win = windows_of(dve, k, ITERS - 1)
                for u in range(U):
                    if u + ahead < U:
                        prepare(ITERS - 1, u + ahead)
                    add(ITERS - 1, u, win)

            @block.tensor
            def _(pe):
                pe.sem_inc(summed.sem, U)
                with pe.Fori(0, ITERS) as i:
                    for u in range(U):
                        pe.wait_ge(*selected.done(U * i + u + 1))
                        if weighted:
                            pe.wait_ge(*weighed.done(U * i + u + 1))
                        pe.wait_ge(*added.free(U * i + u + 1, U))
                        if weighted:
                            n = wide // banks
                            for b in range(banks):
                                for j in range(2):
                                    last = nc.tensor.matmul(pO[u][:, b, 0:n], sel[:, u, j, :],
                                                            msg[:, u, j, b * n:(b + 1) * n],
                                                            start=(j == 0), stop=(j == 1))
                        at = wide if weighted else 0
                        for _, values, n in plain:
                            for j in range(2):
                                last = nc.tensor.matmul(pO[u][:, 0, at:at + n], sel[:, u, j, :],
                                                        values[:, ds((U * 2 * i + 2 * u + j) * n, n)],
                                                        start=(j == 0), stop=(j == 1))
                            at += n
                        last.then_inc(summed.sem, 1)

            @block.sync
            def _(sp):
                sp.wait_ge(*added.done(STEPS))
                sp.dma_start(out_dram[:, 0:WINDOWS * size], acc[:, :]).then_inc(s_out.sem, 16)
                sp.wait_ge(*s_out.done(1))
        k.close(STEPS, selected, summed, added)
        if weighted:
            k.close(STEPS, weighed, act_passed)
            k.close(2 * ITERS, staged, passed)
            k.close(ITERS, *gathered)
        k.close(1, s_out)


def conv_mid_phase(nc, k):
    H = HEADS
    with ExitStack() as ctx:
        def sb(name, shape, dt=F32):
            return ctx.enter_context(nc.sbuf_tensor(k.own(name), shape, dt))

        def pb(name, shape):
            return ctx.enter_context(nc.psum_tensor(k.own(name), shape, F32))
        wv = sb("wv0", [D, H, D])
        ws = sb("ws0", [D, H, D])
        bs = sb("bs0", [D, H])
        bv = sb("bv0_block", [H, H, D])
        w2 = sb("w_qkv1", [D, 3, H, HD])
        ws1 = sb("ws1", [D, H, D])
        b2 = sb("b_qkv1", [P, 3, HD])
        bs1 = sb("bs1", [P, D])
        agg = sb("agg", [P, CH, H, D + 1])
        den = sb("den", [P, CH, H])
        ratio = sb("ratio", [P, CH, H])
        ratioT = sb("ratioT", [H, CH, D])
        aggT = sb("aggT", [P, CH, D])
        hc = sb("h", [P, CH, D])
        hT = sb("hT", [P, CH, D])
        h1T = sb("h1T", [P, H, CH, D])
        work = k.logits[:, :, :].rearrange("p h t -> p (h t)")
        q = work[:, 0:HD]
        kk = work[:, HD:2 * HD]
        vv = work[:, 2 * HD:2 * HD + HW1].rearrange("p (h d) -> p h d", h=H)
        pA = pb("pA", [P, 8, D])
        pB = pb("pB", [P, 8, D])
        pX = [pb(f"pX{n}", [P, 512]) for n in range(4)]
        s_w = k.fresh("weights_conv2")
        s_bv = k.fresh("bias_block_cleared")
        names = ("agg_scaled", "aggT_ready", "aggT_made", "h1_product", "h1_made", "ratio_turned", "ratio_made")
        scaled, a_turned, aT_made, h1_prod, h1_made, r_turned, r_made = (k.count(n) for n in names)
        done = k.count("chunk_done", 1)
        agg_in = k.count("agg_loaded", 0, 16)
        prods = [k.count(f"proj{n}_product") for n in range(4)]
        used = [k.count(f"proj{n}_used", 1) for n in range(4)]
        stored = [k.count(f"{n}_rows_stored", 1, 16) for n in ("k", "v")]
        with nc.Block() as block:
            @block.sync
            def _(sp):
                with nc.allow_non_contiguous_dma(reason="small columns of biases"):
                    for out, src in (
                            (wv[:, :, :], k.L1_gnn_Wv0.rearrange("p (h n) -> p h n", n=D)),
                            (ws[:, :, :], k.L1_gnn_Ws0.rearrange("p (h n) -> p h n", n=D)),
                            (bs[:, :], k.L1_gnn_bs0.rearrange("(h p) -> p h", p=D)),
                            (ws1[:, :, :], k.L1_gnn_Ws1.rearrange("(c p) n -> p c n", p=D)),
                            (bs1[:, :], k.L1_gnn_bs1.rearrange("(o n) -> o n", o=1).partition_broadcast(P))):
                        sp.dma_start(out, src).then_inc(s_w, 16)
                    for n, (w, b) in enumerate(((k.L1_gnn_Wq1, k.L1_gnn_bq1), (k.L1_gnn_Wk1, k.L1_gnn_bk1),
                                                (k.L1_gnn_Wv1, k.L1_gnn_bv1))):
                        sp.dma_start(w2[:, n, :, :], w.rearrange("(c p) n -> p c n", p=D)).then_inc(s_w, 16)
                        sp.dma_start(b2[:, n, :], b.rearrange("(o n) -> o n", o=1).partition_broadcast(P)).then_inc(s_w, 16)
                    sp.wait_ge(s_bv, 1)
                    for h in range(H):
                        sp.dma_start(bv[h:h + 1, h, :], k.L1_gnn_bv0.rearrange("(h n) -> h n", n=D)[h:h + 1, :])\
                          .then_inc(s_w, 16)
                with sp.Fori(0, CHUNKS) as i:
                    sp.wait_ge(*done.free(i + 1, 1))
                    sp.dma_start(agg[:, :, :, :], k.sums_dram[:, ds(i * CH * HW1, CH * HW1)]).then_inc(agg_in.sem, 16)
                    for c in range(CH):
                        for n, (src, dram) in enumerate(((kk[:, :], k.k_dram), (vv[:, :, :], k.v_dram))):
                            sp.wait_ge(*used[1 + n].done(CH * i + c + 1))
                            sp.dma_start(dram[ds((i * CH + c) * P, P), :], src).then_inc(stored[n].sem, 16)
                for n in range(2):
                    sp.wait_ge(*stored[n].done(WINDOWS))

            @block.vector
            def _(dve):
                v = nc.vector
                v.memset(bv[:, :, :], 0.0).then_inc(s_bv, 1)
                v.memset(vv[:, :, D:D + 1], 1.0)
                dve.sem_inc(done.sem)
                for n in range(2):
                    dve.sem_inc(stored[n].sem, 16)
                for n in range(4):
                    dve.sem_inc(used[n].sem)
                dve.wait_ge(s_w, 16 * 15)
                with dve.Fori(0, CHUNKS) as i:
                    dve.wait_ge(*agg_in.done(i + 1))
                    v.tensor_copy(hc[:, :, :], chunk(k.H, i))
                    v.tensor_scalar(den[:, :, :], agg[:, :, :, D], 1.0e-16, None, ALU.add)
                    dve.drain()
                    v.reciprocal(den[:, :, :], den[:, :, :])
                    dve.drain()
                    v.tensor_tensor(ratio[:, :, :], agg[:, :, :, D], den[:, :, :], ALU.mult)
                    for h in range(H):
                        v.tensor_tensor(agg[:, :, h, 0:D], agg[:, :, h, 0:D],
                                        den[:, :, h:h + 1].broadcast_to([P, CH, D]), ALU.mult)
                    dve.drain().then_inc(scaled.sem, 1)
                    for c in range(CH):
                        dve.wait_ge(*prods[0].done(CH * i + c + 1))
                        v.tensor_tensor(q[:, :], pX[0][:, :], b2[:, 0, :], ALU.add)
                        dve.drain().then_inc(used[0].sem, 1)
                        part = [k.U[:, ds(i * (CH * 3 * HD) + (3 * c + n) * HD, HD)] for n in range(3)]
                        split3(dve, nc, q[:, :], *part, q[:, :])
                        dve.drain()
                        dve.wait_ge(*prods[1].done(CH * i + c + 1))
                        dve.wait_ge(*stored[0].free(CH * i + c + 1, 1))
                        v.tensor_tensor(kk[:, :], pX[1][:, :], b2[:, 1, :], ALU.add).then_inc(used[1].sem, 1)
                        dve.wait_ge(*prods[2].done(CH * i + c + 1))
                        dve.wait_ge(*stored[1].free(CH * i + c + 1, 1))
                        v.tensor_tensor(vv[:, :, 0:D], pX[2][:, :].rearrange("p (h d) -> p h d", h=H),
                                        b2[:, 2, :].rearrange("p (h d) -> p h d", h=H), ALU.add).then_inc(used[2].sem, 1)
                        dve.wait_ge(*prods[3].done(CH * i + c + 1))
                        v.tensor_tensor(k.G[:, ds(i * CH + c, 1), :].rearrange("p o d -> p (o d)"), pX[3][:, 0:D],
                                        bs1[:, :], ALU.add).then_inc(used[3].sem, 1)
                    dve.drain().then_inc(done.sem, 1)

            @block.scalar
            def _(act):
                s = nc.scalar
                act.wait_ge(s_w, 16 * 15)
                with act.Fori(0, CHUNKS) as i:
                    act.wait_ge(*a_turned.done(5 * i + 1))
                    s.copy(hT[:, :, :], pA[:, 0:CH, :]).then_inc(aT_made.sem, 1)
                    act.wait_ge(*r_turned.done(i + 1))
                    s.copy(ratioT[:, :, :], pB[0:H, 0:CH, :]).then_inc(r_made.sem, 1)
                    for h in range(H):
                        act.wait_ge(*a_turned.done(5 * i + h + 2))
                        s.copy(aggT[:, :, :], pA[:, 0:CH, :]).then_inc(aT_made.sem, 1)
                        act.wait_ge(*h1_prod.done(H * i + h + 1))
                        s.activation(h1T[:, h, :, :], pB[:, 0:CH, :], ACT.Relu, bias=bs[:, h:h + 1])\
                         .then_inc(h1_made.sem, 1)

            @block.tensor
            def _(pe):
                t = nc.tensor

                def wide(out, lhsT, rhs, start, stop):
                    t.matmul(out[:, 0:4, :], lhsT, rhs[:, 0:4, :], start=start, stop=stop)
                    return t.matmul(out[:, 4:CH, :], lhsT, rhs[:, 4:CH, :], start=start, stop=stop)
                pe.wait_ge(s_w, 16 * 15)
                with pe.Fori(0, CHUNKS) as i:
                    pe.wait_ge(*scaled.done(i + 1))
                    for c in range(CH):
                        last = t.transpose(pA[:, c, :], hc[:, c, :], k.ident[:, :])
                    last.then_inc(a_turned.sem, 1)
                    for c in range(CH):
                        last = t.matmul(pB[0:H, c, :], ratio[:, c, :], k.ident[:, :], start=True, stop=True)
                    last.then_inc(r_turned.sem, 1)
                    pe.wait_ge(*r_made.done(i + 1))
                    for h in range(H):
                        pe.wait_ge(*aT_made.done(5 * i + h + 1))
                        for c in range(CH):
                            last = t.transpose(pA[:, c, :], agg[:, c, h, 0:D], k.ident[:, :])
                        last.then_inc(a_turned.sem, 1)
                        pe.wait_ge(*aT_made.done(5 * i + h + 2))
                        wide(pB, wv[:, h, :], aggT, True, False)
                        wide(pB, ws[:, h, :], hT, False, False)
                        wide(pB, bv[:, h, :], ratioT, False, True).then_inc(h1_prod.sem, 1)
                        pe.wait_ge(*h1_made.done(H * i + h + 1))
                    for c in range(CH):
                        for n in range(4):
                            pe.wait_ge(*used[n].free(CH * i + c + 1, 1))
                            for kc in range(H):
                                rhs = w2[:, n, kc, :] if n < 3 else ws1[:, kc, :]
                                last = t.matmul(pX[n][:, 0:rhs.shape[1]], h1T[:, kc, c, :], rhs,
                                                start=(kc == 0), stop=(kc == H - 1))
                            last.then_inc(prods[n].sem, 1)
        k.close(CHUNKS, scaled, r_turned, r_made, agg_in, done)
        k.close(5 * CHUNKS, a_turned, aT_made)
        k.close(H * CHUNKS, h1_prod, h1_made)
        k.close(WINDOWS, *prods, *used, *stored)


def conv2_out_phase(nc, k):
    H = HEADS
    with ExitStack() as ctx:
        agg = ctx.enter_context(nc.sbuf_tensor(k.own("agg"), [P, CH, H, D + 1], F32))
        den = ctx.enter_context(nc.sbuf_tensor(k.own("den"), [P, CH, H], F32))
        agg_in, done = k.count("agg_loaded", 0, 16), k.count("chunk_done", 1)
        with nc.Block() as block:
            @block.sync
            def _(sp):
                with sp.Fori(0, CHUNKS) as i:
                    sp.wait_ge(*done.free(i + 1, 1))
                    sp.dma_start(agg[:, :, :, :], k.sums_dram[:, ds(i * CH * HW1, CH * HW1)]).then_inc(agg_in.sem, 16)

            @block.vector
            def _(dve):
                v = nc.vector
                dve.sem_inc(done.sem)
                with dve.Fori(0, CHUNKS) as i:
                    dve.wait_ge(*agg_in.done(i + 1))
                    v.tensor_scalar(den[:, :, :], agg[:, :, :, D], 1.0e-16, None, ALU.add)
                    dve.drain()
                    v.reciprocal(den[:, :, :], den[:, :, :])
                    dve.drain()
                    v.tensor_scalar(den[:, :, :], den[:, :, :], 1.0 / H, None, ALU.mult)
                    dve.drain()
                    for h in range(H):
                        v.tensor_tensor(agg[:, :, h, 0:D], agg[:, :, h, 0:D],
                                        den[:, :, h:h + 1].broadcast_to([P, CH, D]), ALU.mult)
                    dve.drain()
                    for a, b in ((0, 1), (2, 3), (0, 2)):
                        v.tensor_tensor(agg[:, :, a, 0:D], agg[:, :, a, 0:D], agg[:, :, b, 0:D], ALU.add)
                        dve.drain()
                    v.tensor_tensor(agg[:, :, 0, 0:D], agg[:, :, 0, 0:D], chunk(k.G, i), ALU.add)
                    dve.drain()
                    v.tensor_tensor(chunk(k.X, i), chunk(k.X, i), agg[:, :, 0, 0:D], ALU.add)
                    dve.drain().then_inc(done.sem, 1)
        k.close(CHUNKS, agg_in, done)


def gat_in_phase(nc, k):
    with ExitStack() as ctx:
        def sb(name, shape, dt=F32):
            return ctx.enter_context(nc.sbuf_tensor(k.own(name), shape, dt))

        def pb(name):
            return ctx.enter_context(nc.psum_tensor(k.own(name), [P, 8, D], F32))
        wl = sb("wl", [D, D])
        wr = sb("wr", [D, D])
        w = Scratch(nc, sb, "n3", k.eps5)
        h = sb("h", [P, CH, D])
        hT = sb("hT", [P, CH, D])
        xl = sb("xl", [P, CH, D + 4])
        xr = sb("xr", [P, CH, D + 1])
        m = sb("m", [P, CH, D])
        lk = sb("lk", [P, CH, D])
        rest = sb("rest", [P, CH, D + 1])
        pT, pL, pR = pb("pT"), pb("pL"), pb("pR")
        s_w = k.fresh("weights_gat")
        var, sd, h_made, turned, hT_made, prod, made = (k.count(n) for n in (
            "var_made", "sd_made", "h_made", "h_turned", "hT_made", "g_product", "g_made"))
        out = k.count("rows_stored_chunk", 1, 16)
        with nc.Block() as block:
            @block.sync
            def _(sp):
                sp.dma_start(wl[:, :], k.L2_gnn_W_l).then_inc(s_w, 16)
                sp.dma_start(wr[:, :], k.L2_gnn_W_r).then_inc(s_w, 16)
                sp.dma_start(k.att[:, :], k.L2_gnn_att.rearrange("(o n) -> o n", o=1).partition_broadcast(P)).then_inc(s_w, 16)
                with sp.Fori(0, CHUNKS) as i:
                    sp.wait_ge(*made.done(i + 1))
                    sp.dma_start(rows_of(k.h_dram, i, D + 4), xl[:, :, :]).then_inc(out.sem, 16)
                sp.wait_ge(*out.done(CHUNKS))

            @block.vector
            def _(dve):
                v = nc.vector
                dve.wait_ge(s_w, 48)
                dve.sem_inc(out.sem, 16)
                v.memset(xl[:, :, D:D + 4], 1.0)
                with dve.Fori(0, CHUNKS) as i:
                    norm_head(dve, chunk(k.X, i), w, var)
                    norm_tail(dve, w, h[:, :, :], sd, i + 1)
                    v.tensor_scalar(h[:, :, :], h[:, :, :], 0.0, None, ALU.max).then_inc(h_made.sem, 1)
                    dve.wait_ge(*prod.done(i + 1))
                    dve.wait_ge(*out.free(i + 1, 1))
                    v.tensor_copy(xl[:, :, 0:D], pL[:, 0:CH, :])
                    v.tensor_copy(xr[:, :, 0:D], pR[:, 0:CH, :])
                    dve.drain().then_inc(made.sem, 1)
                    v.tensor_copy(chunk(k.H, i), xl[:, :, 0:D])
                    v.tensor_tensor(m[:, :, :], xl[:, :, 0:D], xr[:, :, 0:D], ALU.add)
                    dve.drain()
                    v.scalar_tensor_tensor(lk[:, :, :], m[:, :, :], 0.2, m[:, :, :], ALU.mult, ALU.max)
                    dve.drain()
                    v.tensor_tensor(m[:, :, :], lk[:, :, :], over_rows(k.att[:, :]), ALU.mult)
                    dve.drain()
                    v.tensor_reduce(xr[:, :, D], m[:, :, :], AXX, ALU.add)
                    dve.drain()
                    u = k.U[:, ds(i * (CH * 3 * (D + 1)), CH * 3 * (D + 1))].rearrange("p (c n d) -> p c n d", c=CH, n=3)
                    split3(dve, nc, xr[:, :, :], u[:, :, 0, :], u[:, :, 1, :], u[:, :, 2, :], rest[:, :, :])
                    dve.drain()

            @block.scalar
            def _(act):
                with act.Fori(0, CHUNKS) as i:
                    norm_sqrt(act, nc, w, var, sd, i + 1)
                    act.wait_ge(*turned.done(i + 1))
                    nc.scalar.copy(hT[:, :, :], pT[:, 0:CH, :]).then_inc(hT_made.sem, 1)

            @block.tensor
            def _(pe):
                pe.wait_ge(s_w, 48)
                with pe.Fori(0, CHUNKS) as i:
                    pe.wait_ge(*h_made.done(i + 1))
                    for c in range(CH):
                        last = nc.tensor.transpose(pT[:, c, :], h[:, c, :], k.ident[:, :])
                    last.then_inc(turned.sem, 1)
                    pe.wait_ge(*hT_made.done(i + 1))
                    for c in range(CH):
                        nc.tensor.matmul(pL[:, c, :], hT[:, c, :], wl[:, :], start=True, stop=True)
                        last = nc.tensor.matmul(pR[:, c, :], hT[:, c, :], wr[:, :], start=True, stop=True)
                    last.then_inc(prod.sem, 1)
        k.close(CHUNKS, var, sd, h_made, turned, hT_made, prod, made, out)


def gat_out_phase(nc, k):
    S = D + 3
    with ExitStack() as ctx:
        def sb(name, shape, dt=F32):
            return ctx.enter_context(nc.sbuf_tensor(k.own(name), shape, dt))
        sums = sb("sums_gat", [P, WINDOWS, S])
        bc = sb("rows_bc", [P, 3, D])
        own = sb("own", [P, WINDOWS])
        den = sb("den", [P, WINDOWS])
        o = sb("o", [P, WINDOWS, D])
        t = sb("t", [P, WINDOWS, D])
        part = sb("part", [P, WINDOWS])
        tot = sb("tot", [P, 1])
        valid = sb("valid", [P, 1])
        ones = sb("ones", [P, P])
        mu = sb("mu", [P, 1])
        sd = sb("sd_all", [P, 1])
        pS = ctx.enter_context(nc.psum_tensor(k.own("pS"), [P, 512], F32))
        s_in = k.fresh("gat_out_loaded")
        s_part = k.fresh("partition_sums")
        s_all = k.fresh("whole_sums")
        s_sd = k.fresh("whole_sd")
        over = lambda row: row.unsqueeze(1).broadcast_to([P, WINDOWS, D])
        each = lambda col: col.unsqueeze(2).broadcast_to([P, WINDOWS, D])
        with nc.Block() as block:
            @block.sync
            def _(sp):
                sp.dma_start(sums[:, :, :], k.sums_dram[:, 0:WINDOWS * S]).then_inc(s_in, 16)
                for n, row in enumerate((k.L2_gnn_bias, k.L2_gnn_ln_w, k.L2_gnn_ln_b)):
                    sp.dma_start(bc[:, n, :], row.rearrange("(o n) -> o n", o=1).partition_broadcast(P)).then_inc(s_in, 16)

            @block.vector
            def _(dve):
                v = nc.vector

                def total(src, value):
                    v.tensor_reduce(part[:, :], src, AXX, ALU.add)
                    dve.drain()
                    v.tensor_tensor(part[:, WINDOWS - 1:WINDOWS], part[:, WINDOWS - 1:WINDOWS], valid[:, :], ALU.mult)
                    dve.drain()
                    v.tensor_reduce(tot[:, :], part[:, :], AXX, ALU.add).then_inc(s_part, 1)
                    dve.wait_ge(s_all, value)
                v.memset(ones[:, :], 1.0)
                v.tensor_scalar(valid[:, :], k.iota_p[:, :], float(LAST), None, ALU.is_lt)
                dve.wait_ge(s_in, 64)
                v.tensor_scalar(own[:, :], sums[:, :, D + 2], -1.0, 1.0, ALU.mult, ALU.add)
                dve.drain()
                v.tensor_tensor(own[:, :], own[:, :], sums[:, :, D + 1], ALU.add)
                dve.drain()
                v.tensor_tensor(den[:, :], own[:, :], sums[:, :, D], ALU.add)
                v.tensor_tensor(t[:, :, :], k.H[:, :, :], each(own[:, :]), ALU.mult)
                dve.drain()
                v.reciprocal(den[:, :], den[:, :])
                v.tensor_tensor(t[:, :, :], t[:, :, :], sums[:, :, 0:D], ALU.add)
                dve.drain()
                v.tensor_tensor(t[:, :, :], t[:, :, :], each(den[:, :]), ALU.mult)
                dve.drain()
                v.tensor_tensor(t[:, :, :], t[:, :, :], over(bc[:, 0, :]), ALU.add)
                dve.drain()
                v.scalar_tensor_tensor(o[:, :, :], t[:, :, :], 0.01, t[:, :, :], ALU.mult, ALU.max)
                dve.drain()
                total(o[:, :, :], 1)
                v.tensor_scalar(mu[:, :], pS[:, 0:1], 1.0 / (NODES * D), None, ALU.mult)
                dve.drain()
                v.tensor_scalar(o[:, :, :], o[:, :, :], mu[:, 0:1], None, ALU.subtract)
                dve.drain()
                v.tensor_tensor(t[:, :, :], o[:, :, :], o[:, :, :], ALU.mult)
                dve.drain()
                total(t[:, :, :], 2)
                dve.wait_ge(s_sd, 1)
                v.tensor_scalar(sd[:, :], sd[:, :], 1.0e-5, None, ALU.add)
                dve.drain()
                v.reciprocal(sd[:, :], sd[:, :])
                dve.drain()
                v.scalar_tensor_tensor(t[:, :, :], o[:, :, :], sd[:, 0:1], over(bc[:, 1, :]), ALU.mult, ALU.mult)
                dve.drain()
                v.tensor_tensor(t[:, :, :], t[:, :, :], over(bc[:, 2, :]), ALU.add)
                dve.drain()
                v.tensor_tensor(k.X[:, :, :], k.X[:, :, :], t[:, :, :], ALU.add)
                dve.drain()

            @block.tensor
            def _(pe):
                for n in range(2):
                    pe.wait_ge(s_part, n + 1)
                    nc.tensor.matmul(pS[:, n:n + 1], ones[:, :], tot[:, :], start=True, stop=True).then_inc(s_all, 1)

            @block.scalar
            def _(act):
                act.wait_ge(s_all, 2)
                nc.scalar.activation(sd[:, :], pS[:, 1:2], ACT.Sqrt, scale=1.0 / (NODES * D)).then_inc(s_sd, 1)


def last_in_phase(nc, k):
    with ExitStack() as ctx:
        def sb(name, shape, dt=F32):
            return ctx.enter_context(nc.sbuf_tensor(k.own(name), shape, dt))

        def pb(name):
            return ctx.enter_context(nc.psum_tensor(k.own(name), [P, 8, D], F32))
        w3 = sb("w3", [D, D])
        w3T = sb("w3T", [D, D])
        bc = sb("rows_bc", [P, 3, D])
        w = Scratch(nc, sb, "n4", k.eps5)
        h = sb("h", [P, CH, D])
        hT = sb("hT", [P, CH, D])
        tt = sb("tt", [P, CH, D])
        m = sb("m", [P, CH, 2, D])
        vals = sb("vals", [P, CH, 2])
        vs = sb("src_values", [P, CH])
        rest = sb("rest", [P, CH])
        pT, pL = pb("pT"), pb("pL")
        s_w = k.fresh("weights_last")
        s_t = k.fresh("w3_turned")
        s_wT = k.fresh("w3T_made")
        var, sd, h_made, turned, hT_made, prod, made = (k.count(n) for n in (
            "var_made", "sd_made", "h_made", "h_turned", "hT_made", "g_product", "g_made"))
        out = k.count("rows_stored_chunk", 1, 16)
        with nc.Block() as block:
            @block.sync
            def _(sp):
                sp.dma_start(w3[:, :], k.L3_gnn_W).then_inc(s_w, 16)
                for n, row in enumerate((k.L3_gnn_b.rearrange("(o n) -> o n", o=1), k.L3_gnn_att_w[:, 0:D],
                                         k.L3_gnn_att_w[:, D:2 * D])):
                    sp.dma_start(bc[:, n, :], row.partition_broadcast(P)).then_inc(s_w, 16)
                with nc.allow_non_contiguous_dma(reason="one value per node"):
                    with sp.Fori(0, CHUNKS) as i:
                        sp.wait_ge(*made.done(i + 1))
                        sp.dma_start(k.val_dram.rearrange("(w p) o -> p (w o)", p=P)[:, ds(i * CH, CH)], vs[:, :]
                                     ).then_inc(out.sem, 16)
                sp.wait_ge(*out.done(CHUNKS))

            @block.vector
            def _(dve):
                v = nc.vector
                dve.sem_inc(out.sem, 16)
                dve.wait_ge(s_t, 1)
                v.tensor_copy(w3T[:, :], pT[:, 0, :]).then_inc(s_wT, 1)
                with dve.Fori(0, CHUNKS) as i:
                    norm_head(dve, chunk(k.X, i), w, var)
                    norm_tail(dve, w, h[:, :, :], sd, i + 1)
                    v.tensor_scalar(h[:, :, :], h[:, :, :], 0.0, None, ALU.max).then_inc(h_made.sem, 1)
                    dve.drain()
                    v.tensor_copy(chunk(k.H, i), h[:, :, :])
                    dve.wait_ge(*prod.done(i + 1))
                    v.tensor_tensor(tt[:, :, :], pL[:, 0:CH, :], over_rows(bc[:, 0, :]), ALU.add)
                    dve.drain()
                    for n in range(2):
                        v.tensor_tensor(m[:, :, n, :], tt[:, :, :], over_rows(bc[:, 1 + n, :]), ALU.mult)
                    dve.drain()
                    v.tensor_reduce(vals[:, :, :], m[:, :, :, :], AXX, ALU.add)
                    dve.drain()
                    dve.wait_ge(*out.free(i + 1, 1))
                    v.tensor_copy(vs[:, :], vals[:, :, 0]).then_inc(made.sem, 1)
                    u = k.U[:, ds(i * (CH * 3), CH * 3)].rearrange("p (c n) -> p c n", c=CH)
                    split3(dve, nc, vals[:, :, 1], u[:, :, 0], u[:, :, 1], u[:, :, 2], rest[:, :])
                    dve.drain()

            @block.scalar
            def _(act):
                with act.Fori(0, CHUNKS) as i:
                    norm_sqrt(act, nc, w, var, sd, i + 1)
                    act.wait_ge(*turned.done(i + 1))
                    nc.scalar.copy(hT[:, :, :], pT[:, 0:CH, :]).then_inc(hT_made.sem, 1)

            @block.tensor
            def _(pe):
                pe.wait_ge(s_w, 64)
                nc.tensor.transpose(pT[:, 0, :], w3[:, :], k.ident[:, :]).then_inc(s_t, 1)
                pe.wait_ge(s_wT, 1)
                with pe.Fori(0, CHUNKS) as i:
                    pe.wait_ge(*h_made.done(i + 1))
                    for c in range(CH):
                        last = nc.tensor.transpose(pT[:, c, :], h[:, c, :], k.ident[:, :])
                    last.then_inc(turned.sem, 1)
                    pe.wait_ge(*hT_made.done(i + 1))
                    for c in range(CH):
                        last = nc.tensor.matmul(pL[:, c, :], hT[:, c, :], w3T[:, :], start=True, stop=True)
                    last.then_inc(prod.sem, 1)
        k.close(CHUNKS, var, sd, h_made, turned, hT_made, prod, made, out)


CAP = 1.0e36
TINY = 1.1754944e-38
SHRINK = 2.0 ** -30


def last_weights_phase(nc, k):
    with ExitStack() as ctx:
        a = ctx.enter_context(nc.sbuf_tensor(k.own("leaky"), [P, TILES], F32))
        z = ctx.enter_context(nc.sbuf_tensor(k.own("normal"), [P, TILES], F32))
        s_l = k.fresh("leaky_made")
        s_e = k.fresh("weights_made")
        with nc.Block() as block:
            @block.vector
            def _(dve):
                v = nc.vector
                lg = k.logits[:, 0, :]
                v.scalar_tensor_tensor(a[:, :], lg, 0.2, lg, ALU.mult, ALU.max)
                dve.drain()
                v.tensor_scalar(a[:, :], a[:, :], 88.0, -100.0, ALU.min, ALU.max).then_inc(s_l, 1)
                dve.wait_ge(s_e, 1)
                v.tensor_scalar(z[:, :], a[:, :], TINY, None, ALU.is_ge)
                v.tensor_scalar(a[:, :], a[:, :], CAP, None, ALU.min)
                dve.drain()
                v.tensor_tensor(lg, a[:, :], z[:, :], ALU.mult)
                dve.drain()

            @block.scalar
            def _(act):
                act.wait_ge(s_l, 1)
                nc.scalar.activation(a[:, :], a[:, :], ACT.Exp).then_inc(s_e, 1)


def last_out_phase(nc, k, out):
    with ExitStack() as ctx:
        def sb(name, shape, dt=F32):
            return ctx.enter_context(nc.sbuf_tensor(k.own(name), shape, dt))
        n = sb("n_sum", [P, WINDOWS])
        z = sb("n_zero", [P, WINDOWS])
        y = sb("y", [P, WINDOWS, D])
        t = sb("t", [P, WINDOWS, D])
        ms = sb("ms", [P, WINDOWS])
        ok = sb("ok", [P, WINDOWS])
        sd = sb("sd_last", [P, WINDOWS])
        bc = sb("rows_bc", [P, 2, D])
        s_in = k.fresh("last_loaded_sums")
        s_ms = k.fresh("mean_square_made")
        s_sd = k.fresh("rms_made")
        s_y = k.fresh("result_made")
        s_out = k.fresh("result_stored")
        over = lambda row: row.unsqueeze(1).broadcast_to([P, WINDOWS, D])
        each = lambda col: col.unsqueeze(2).broadcast_to([P, WINDOWS, D])
        with nc.Block() as block:
            @block.sync
            def _(sp):
                sp.dma_start(n[:, :], k.sums_dram[:, 0:WINDOWS]).then_inc(s_in, 16)
                for j, row in enumerate((k.L3_gnn_norm_w, k.L3_gnn_norm_b)):
                    sp.dma_start(bc[:, j, :], row.rearrange("(o n) -> o n", o=1).partition_broadcast(P)).then_inc(s_in, 16)
                sp.wait_ge(s_y, 1)
                sp.dma_start(out[0:(WINDOWS - 1) * P, :].rearrange("(w p) d -> p w d", p=P), y[:, 0:WINDOWS - 1, :])\
                  .then_inc(s_out, 16)
                sp.dma_start(out[(WINDOWS - 1) * P:NODES, :], y[0:LAST, WINDOWS - 1, :]).then_inc(s_out, 16)
                sp.wait_ge(s_out, 32)

            @block.vector
            def _(dve):
                v = nc.vector
                dve.wait_ge(s_in, 48)
                v.tensor_scalar(z[:, :], n[:, :], 0.0, None, ALU.is_equal)
                v.tensor_scalar(n[:, :], n[:, :], CAP, None, ALU.min)
                dve.drain()
                v.tensor_tensor(n[:, :], n[:, :], z[:, :], ALU.add)
                dve.drain()
                v.reciprocal(n[:, :], n[:, :])
                dve.drain()
                v.tensor_scalar(n[:, :], n[:, :], SHRINK, None, ALU.mult)
                v.tensor_scalar(y[:, :, :], k.H[:, :, :], SHRINK, None, ALU.mult)
                dve.drain()
                v.tensor_tensor(t[:, :, :], k.H[:, :, :], each(n[:, :]), ALU.mult)
                dve.drain()
                v.scalar_tensor_tensor(t[:, :, :], t[:, :, :], 0.0, y[:, :, :], ALU.max, ALU.add)
                dve.drain()
                v.tensor_scalar(y[:, :, :], t[:, :, :], 1.0e15, None, ALU.min)
                dve.drain()
                v.tensor_tensor(t[:, :, :], y[:, :, :], y[:, :, :], ALU.mult)
                dve.drain()
                v.tensor_reduce(ms[:, :], t[:, :, :], AXX, ALU.add)
                dve.drain()
                v.tensor_scalar(ok[:, :], ms[:, :], 3.4028235e38 * SHRINK * SHRINK, None, ALU.is_le)
                v.tensor_scalar(sd[:, :], ms[:, :], 1.0 / D, 1.0e-6 * SHRINK * SHRINK, ALU.mult, ALU.add)
                dve.drain().then_inc(s_ms, 1)
                dve.wait_ge(s_sd, 1)
                v.reciprocal(sd[:, :], sd[:, :])
                dve.drain()
                v.tensor_tensor(sd[:, :], sd[:, :], ok[:, :], ALU.mult)
                dve.drain()
                v.tensor_tensor(y[:, :, :], y[:, :, :], each(sd[:, :]), ALU.mult)
                dve.drain()
                v.tensor_tensor(y[:, :, :], y[:, :, :], over(bc[:, 0, :]), ALU.mult)
                dve.drain()
                v.tensor_tensor(y[:, :, :], y[:, :, :], over(bc[:, 1, :]), ALU.add)
                dve.drain()
                v.tensor_tensor(y[:, :, :], y[:, :, :], k.X[:, :, :], ALU.add).then_inc(s_y, 1)

            @block.scalar
            def _(act):
                act.wait_ge(s_ms, 1)
                nc.scalar.activation(sd[:, :], sd[:, :], ACT.Sqrt).then_inc(s_sd, 1)


def program(nc, arrays, out):
    with ExitStack() as ctx:
        k = Shared(nc, ctx, arrays)

        def sbuf(name, shape, dt=F32):
            return nc.sbuf_tensor(name, shape, dt)

        def sb(name, shape, dt=F32):
            return ctx.enter_context(sbuf(name, shape, dt))

        def dram(name, shape, dt=F32):
            return nc.dram_tensor(name, shape, dt).ap()
        k.ones_row = sb("ones_row", [1, P])
        k.ident = sb("ident", [P, P])
        k.iota_row = sb("iota_row", [P, P])
        k.iota_p = sb("iota_p", [P, 1])
        k.eps5 = sb("eps5", [P, 1])
        k.mask_t = sb("mask_t", [P, 2, GROUP + 1])
        k.first_t = sb("first_t", [P, 2, GROUP])
        k.last_t = sb("last_t", [P, 2, GROUP])
        k.step_masks = sb("step_masks", [HEADS, 4, STEPS])
        k.dloc_e = sb("dloc_e", [P, TILES])
        k.end_e = sb("end_e", [P, TILES])
        k.src_e = sb("src_e", [P, TILES], I32)
        k.win = sb("win", [1, ITERS], I32)
        k.X = sb("X", [P, WINDOWS, D])
        k.H = sb("H", [P, WINDOWS, D])
        k.G = sb("G", [P, WINDOWS, D])
        k.att = sb("att", [P, D])
        k.dloc_dram = dram("dloc_dram", [STEPS, GROUP], BF16)
        k.mask_dram = dram("mask_dram", [STEPS, GROUP], BF16)
        k.hot_dram = dram("hot_dram", [P, STEPS * GROUP], BF16)
        k.g_dram = dram("g_dram", [ROWS, D])
        k.h_dram = dram("h_dram", [ROWS, D + 4])
        k.k_dram = dram("k_dram", [ROWS, HD])
        k.v_dram = dram("v_dram", [ROWS, HW1])
        k.val_dram = dram("val_dram", [ROWS, 1])
        k.sums_dram = dram("sums_dram", [P, WINDOWS * HW1])
        graph_phase(nc, k)
        onehot_phase(nc, k)
        load_phase(nc, k)

        edge_conv_in_phase(nc, k)
        with sbuf("acc", [P, WINDOWS * (D + 1)]) as k.acc:
            edge_max_phase(nc, k)
            edge_conv_out_phase(nc, k)

        with sbuf("logits_conv", [P, HEADS, TILES]) as k.logits:
            with sbuf("u_table", [P, WINDOWS * 3 * HW1], BF16) as k.U:
                conv1_in_phase(nc, k)
                edge_logits_phase(nc, k, k.h_dram, D + 4, False, HW1)
            segment_softmax_phase(nc, k, HEADS, float(D) ** -0.5)
            edge_sum_phase(nc, k, k.h_dram, D + 4, [(k.logits[:, h, :], 0, D + 1) for h in range(HEADS)],
                           k.sums_dram)
            with sbuf("q_table", [P, WINDOWS * 3 * HD], BF16) as k.U:
                conv_mid_phase(nc, k)
                edge_logits_phase(nc, k, k.k_dram, HD, True, HD)
            segment_softmax_phase(nc, k, HEADS, float(D) ** -0.5)
            edge_sum_phase(nc, k, k.v_dram, HW1, [(k.logits[:, h, :], h * (D + 1), D + 1) for h in range(HEADS)],
                           k.sums_dram)
            conv2_out_phase(nc, k)

        k.logits, k.selfs, k.ends = sb("logits3", [P, 1, TILES]), sb("selfs", [P, TILES]), sb("ends", [P, TILES, 2])
        with sbuf("r_table", [P, WINDOWS * 3 * (D + 1)], BF16) as k.U:
            gat_in_phase(nc, k)
            edge_logits_phase(nc, k, k.h_dram, D + 4, False, D + 1, "gat")
        segment_softmax_phase(nc, k, 1, 1.0, with_self=True)
        edge_sum_phase(nc, k, k.h_dram, D + 4, [(k.logits[:, 0, :], 0, D + 1),
                                                (None, k.ends[:, :, :].rearrange("p t n -> p (t n)"), 2)], k.sums_dram)
        gat_out_phase(nc, k)

        with sbuf("s_table", [P, WINDOWS * 3], BF16) as k.U:
            last_in_phase(nc, k)
            edge_logits_phase(nc, k, k.val_dram, 1, False, 1, "sum")
        last_weights_phase(nc, k)
        edge_sum_phase(nc, k, None, 0, [(None, k.logits[:, 0, :], 1)], k.sums_dram)
        last_out_phase(nc, k, out)


def kernel(**inputs):
    import numpy as _np
    import concourse.bacc as _bacc
    from concourse import mybir as _mybir
    from concourse.bass_utils import run_bass_kernel_spmd as _run

    nc = _bacc.Bacc("TRN2", target_bir_lowering=False, num_devices=1)
    host = {n: _np.ascontiguousarray(v) for n, v in inputs.items()}
    pad = SLOTS - EDGES
    host["src"] = _np.concatenate([host["src"], _np.zeros(pad, host["src"].dtype)])
    host["dst"] = _np.concatenate([host["dst"], _np.full(pad, ROWS - 1, host["dst"].dtype)])
    arrays = {f"in_{n}": a for n, a in host.items()}
    aps = {n: nc.dram_tensor(f"in_{n}", a.shape, _mybir.dt.from_np(a.dtype), kind="ExternalInput").ap()
           for n, a in host.items()}
    out = nc.dram_tensor("out_0", [NODES, D], _mybir.dt.float32, kind="ExternalOutput").ap()
    program(nc, aps, out)
    r = _run(nc, [arrays], core_ids=[0])
    return r.results[0]["out_0"]
```

```python
import numpy as np
import concourse.bass as bass
from concourse import mybir
from contextlib import ExitStack

F32, I32, BF16 = mybir.dt.float32, mybir.dt.int32, mybir.dt.bfloat16
ALU = mybir.AluOpType
ACT = mybir.ActivationFunctionType
AXX = mybir.AxisListType.X

NODES, EDGES, D = 3125, 50000, 128
HEADS = 4
FFN = 4 * D
HD = HEADS * D
HW1 = HEADS * (D + 1)
P = 128
WINDOWS = -(-NODES // P)
ROWS = WINDOWS * P
LAST = NODES - (WINDOWS - 1) * P
GROUP = 256
GROUPS = -(-EDGES // GROUP)
SLOTS = GROUPS * GROUP
STEPS = GROUPS + WINDOWS - 1
HALF = STEPS // 2
TILES = 2 * STEPS
U = 4
ITERS = STEPS // U
WBITS = 5
CH = 5
CHUNKS = WINDOWS // CH
BIG = 1.0e30
ds = bass.ds


class Count:

    def __init__(self, sem, ahead, unit):
        self.sem, self.ahead, self.unit, self.base = sem, ahead, unit, 0

    def done(self, n):
        return self.sem, n * self.unit + (self.base + self.ahead * self.unit)

    def free(self, n, depth):
        return self.sem, n * self.unit + (self.base + (self.ahead - depth) * self.unit)


def windows_of(eng, k, i):
    packed = eng.value_load(k.win[0:1, ds(i, 1)], min_val=0, max_val=(1 << (U * WBITS)) - 1)
    return [((packed >> (u * WBITS)) & ((1 << WBITS) - 1)).with_bounds(min_val=0, max_val=WINDOWS - 1) for u in range(U)]


def graph_phase(nc, k):
    with ExitStack() as ctx:
        def sb(name, shape, dt=F32):
            return ctx.enter_context(nc.sbuf_tensor(k.own(name), shape, dt))

        def pb(name, shape):
            return ctx.enter_context(nc.psum_tensor(k.own(name), shape, F32))

        def sem(name):
            return ctx.enter_context(nc.semaphore(k.own(name)))

        last_i = sb("last_i", [1, GROUPS], I32)
        lastw_i = sb("lastw_i", [1, GROUPS], I32)
        lastw = sb("lastw", [1, GROUPS])
        grp_i = sb("grp_i", [1, GROUPS], I32)
        grp = sb("grp", [1, GROUPS])
        key = sb("key", [1, GROUPS])
        step_col = sb("step_col", [P, 2])
        hits = sb("hits", [P, GROUPS])
        gcol = sb("gcol", [P, 2])
        gcol_i = sb("gcol_i", [P, 2], I32)
        wcol = sb("wcol", [P, 2])
        base = sb("base", [P, 2])
        it_i = sb("it_i", [P, P], I32)
        ip_i = sb("ip_i", [P, 1], I32)
        dst_i = sb("dst_i", [P, 2, GROUP], I32)
        src_i = sb("src_i", [P, 2, GROUP], I32)
        dst = sb("dst", [P, 2, GROUP])
        srcf = sb("srcf", [P, 2, GROUP])
        lo_i = sb("lo_i", [P, 2, GROUP], I32)
        lo_b = sb("lo_b", [P, 2, GROUP], BF16)
        dloc = sb("dloc", [P, 2, GROUP])
        dloc_b = sb("dloc_b", [P, 2, GROUP], BF16)
        same = sb("same", [P, 2, GROUP])
        end = sb("end", [P, 2, GROUP])
        mask_b = sb("mask_b", [P, 2, GROUP], BF16)
        rows = sb("rows", [1, 2, STEPS])
        cont = sb("cont", [1, STEPS + 1])
        whole = sb("whole", [1, STEPS])
        mrows = sb("mrows", [1, 4, STEPS])
        wpack = sb("packed_windows", [1, ITERS])
        cont_c = sb("cont_c", [P, 2, 2])

        pa = pb("pa", [P, 512])
        pc = pb("pc", [P, 512])
        pd = pb("pd", [P, 12, P])

        s_last = sem("last_loaded")
        s_iota = sem("iotas_made")
        s_const = sem("consts_made")
        s_key = sem("key_made")
        s_keyb = sem("key_broadcast")
        s_g = sem("group_index_made")
        s_edges = sem("edges_gathered")
        s_winrow = sem("window_row_made")
        s_dst = sem("dst_floats_made")
        s_rows = sem("first_last_rows")
        s_mrow = sem("mask_rows_made")
        s_mrowb = sem("mask_rows_spread")
        s_end = sem("end_flags_made")
        s_cols = sem("edge_major_made")
        s_stored = sem("rows_stored")

        block = ctx.enter_context(nc.Block())

        @block.sync
        def _(sp):
            with nc.allow_non_contiguous_dma(reason="one value of each group"):
                sp.dma_start(last_i[:, :], k.dst.rearrange("(o g e) -> o g e", o=1, e=GROUP)[:, :, GROUP - 1])\
                  .then_inc(s_last, 16)
            sp.wait_ge(s_end, 1)
            for h in range(2):
                sp.dma_start(k.dloc_dram[h * HALF:(h + 1) * HALF, :], dloc_b[0:HALF, h, :]).then_inc(s_stored, 16)
                sp.dma_start(k.mask_dram[h * HALF:(h + 1) * HALF, :], mask_b[0:HALF, h, :]).then_inc(s_stored, 16)
                sp.dma_start(k.lo_dram[h * HALF:(h + 1) * HALF, :], lo_b[0:HALF, h, :]).then_inc(s_stored, 16)
            sp.wait_ge(s_stored, 96)

        @block.gpsimd
        def _(pool):
            nc.gpsimd.iota(it_i[:, :], [[1, P]], base=0, channel_multiplier=0)
            nc.gpsimd.iota(ip_i[:, :], [[1, 1]], base=0, channel_multiplier=1)
            nc.gpsimd.iota(grp_i[:, :], [[1, GROUPS]], base=0, channel_multiplier=0)
            nc.gpsimd.memset(k.ones_row[:, :], 1.0)
            nc.gpsimd.memset(k.ident[:, :], 0.0)
            pool.drain().then_inc(s_iota, 1)
            nc.gpsimd.affine_select(out=k.ident[:, :], in_=k.ident[:, :], compare_op=ALU.not_equal, fill=1.0,
                                    base=0, pattern=[[-1, P]], channel_multiplier=1).then_inc(s_const, 1)
            pool.wait_ge(s_g, 1)
            for h in range(2):
                for rows_i, table in ((dst_i, k.dst), (src_i, k.src)):
                    nc.gpsimd.indirect_dma_start(
                        rows_i[0:HALF, h, :], None, table.rearrange("(g e) -> g e", e=GROUP),
                        bass.IndirectOffsetOnAxis(ap=gcol_i[0:HALF, h:h + 1], axis=0)).then_inc(s_edges, 16)

        @block.vector
        def _(dve):
            v = nc.vector
            dve.wait_ge(s_last, 16)
            v.tensor_scalar(lastw_i[:, :], last_i[:, :], 7, None, ALU.arith_shift_right)
            dve.wait_ge(s_iota, 1)
            v.tensor_copy(k.iota_row[:, :], it_i[:, :])
            v.tensor_copy(k.iota_p[:, :], ip_i[:, :])
            v.tensor_copy(grp[:, :], grp_i[:, :])
            dve.drain()
            v.tensor_copy(lastw[:, :], lastw_i[:, :])
            v.tensor_copy(step_col[:, 0:1], k.iota_p[:, :])
            v.tensor_scalar(step_col[:, 1:2], k.iota_p[:, :], float(HALF), None, ALU.add)
            dve.drain()
            v.tensor_tensor(key[:, :], lastw[:, :], grp[:, :], ALU.add).then_inc(s_key, 1)
            dve.wait_ge(s_keyb, 1)
            for h in range(2):
                v.tensor_scalar(hits[:, :], pa[:, 0:GROUPS], step_col[:, h:h + 1], None, ALU.is_lt, ALU.add,
                                accum_out=gcol[:, h:h + 1])
                dve.drain()
            v.tensor_copy(gcol_i[:, :], gcol[:, :]).then_inc(s_g, 1)
            v.tensor_tensor(wcol[:, :], step_col[:, :], gcol[:, :], ALU.subtract)
            dve.drain()
            v.tensor_scalar(base[:, :], wcol[:, :], float(P), None, ALU.mult)
            dve.wait_ge(s_edges, 64)
            v.tensor_copy(dst[0:HALF], dst_i[0:HALF])
            v.tensor_copy(srcf[0:HALF], src_i[0:HALF])
            v.tensor_scalar(lo_i[0:HALF], src_i[0:HALF], P - 1, None, ALU.bitwise_and)
            for h in range(2):
                v.tensor_scalar(k.win_hot[:, h, :], k.iota_row[:, 0:WINDOWS], wcol[:, h:h + 1], None, ALU.is_equal)
            dve.drain().then_inc(s_dst, 1)
            for h in range(2):
                v.tensor_scalar(dloc[0:HALF, h, :], dst[0:HALF, h, :], base[0:HALF, h:h + 1], None, ALU.subtract)
            dve.drain()
            v.tensor_scalar(dloc[0:HALF], dloc[0:HALF], -1.0, float(P), ALU.max, ALU.min)
            v.tensor_tensor(same[0:HALF, :, 1:GROUP], dst[0:HALF, :, 1:GROUP], dst[0:HALF, :, 0:GROUP - 1],
                            ALU.is_equal)
            dve.drain()
            v.tensor_copy(dloc_b[0:HALF], dloc[0:HALF])
            v.tensor_copy(lo_b[0:HALF], lo_i[0:HALF])
            v.memset(k.mask_t[:, :, 0:1], -BIG)
            v.memset(k.mask_t[:, :, GROUP:GROUP + 1], -BIG)
            v.tensor_scalar(k.mask_t[0:HALF, :, 1:GROUP], same[0:HALF, :, 1:GROUP], -1.0, BIG, ALU.add, ALU.mult)
            v.tensor_scalar(end[0:HALF, :, 0:GROUP - 1], same[0:HALF, :, 1:GROUP], -1.0, 1.0, ALU.mult, ALU.add)
            for h in range(2):
                for out, c in ((k.first_t, 0), (k.last_t, GROUP - 1)):
                    v.tensor_scalar(out[0:HALF, h, :], dst[0:HALF, h, :], dst[0:HALF, h, c:c + 1], None, ALU.is_equal)
            dve.drain()
            for out in (k.first_t, k.last_t):
                v.tensor_scalar(out[0:HALF], out[0:HALF], -1.0, BIG, ALU.add, ALU.mult)
            v.tensor_copy(mask_b[0:HALF, :, 1:GROUP], k.mask_t[0:HALF, :, 1:GROUP])
            dve.wait_ge(s_rows, 1)
            v.tensor_copy(rows[:, :, :], pc[0:1, 0:2 * STEPS].rearrange("o (a s) -> o a s", a=2))
            v.memset(cont[:, :], 0.0)
            dve.drain()
            v.tensor_tensor(cont[:, 1:STEPS], rows[:, 0, 1:STEPS], rows[:, 1, 0:STEPS - 1], ALU.is_equal)
            v.tensor_tensor(whole[:, :], rows[:, 0, :], rows[:, 1, :], ALU.is_equal)
            dve.drain()
            v.tensor_tensor(mrows[:, 0, :], whole[:, :], cont[:, 0:STEPS], ALU.mult)
            v.tensor_tensor(mrows[:, 1, :], whole[:, :], cont[:, 1:STEPS + 1], ALU.mult)
            v.tensor_copy(mrows[:, 2, :], cont[:, 0:STEPS])
            v.tensor_copy(mrows[:, 3, :], cont[:, 1:STEPS + 1])
            dve.drain()
            v.tensor_scalar(mrows[:, :, :], mrows[:, :, :], -1.0, BIG, ALU.add, ALU.mult).then_inc(s_mrow, 1)
            dve.wait_ge(s_mrowb, 1)
            v.tensor_copy(cont_c[0:HALF, :, :], pc[0:HALF, 0:4].rearrange("p (a h) -> p a h", a=2))
            v.tensor_copy(k.step_masks[:, 0:2, :], pa[0:HEADS, 0:2 * STEPS].rearrange("o (a s) -> o a s", a=2))
            dve.wait_ge(s_mrowb, 2)
            v.tensor_copy(k.step_masks[:, 2:4, :], pd[0:HEADS, 0:4, :].rearrange("o a s -> o (a s)")[:, 0:2 * STEPS]
                          .rearrange("o (a s) -> o a s", a=2))
            dve.drain()
            for h in range(2):
                v.tensor_scalar(mask_b[0:HALF, h, 0:1], cont_c[0:HALF, 0, h:h + 1], -1.0, BIG, ALU.add, ALU.mult)
                v.tensor_scalar(end[0:HALF, h, GROUP - 1:GROUP], cont_c[0:HALF, 1, h:h + 1], -1.0, 1.0,
                                ALU.mult, ALU.add)
            dve.drain().then_inc(s_end, 1)
            dve.wait_ge(s_cols, 1)
            for n, out in enumerate((k.dloc_e, k.end_e, k.src_e)):
                for h in range(2):
                    for j in range(2):
                        v.tensor_copy(out[:, 2 * HALF * h + j:2 * HALF * (h + 1):2], pd[:, 4 * n + 2 * h + j, 0:HALF])
            dve.wait_ge(s_winrow, 1)
            winrow = pc[0:1, 8:8 + STEPS].rearrange("o (i u) -> o i u", u=U)
            v.tensor_copy(wpack[:, :], winrow[:, :, U - 1])
            for u in reversed(range(U - 1)):
                dve.drain()
                v.scalar_tensor_tensor(wpack[:, :], wpack[:, :], float(1 << WBITS), winrow[:, :, u], ALU.mult, ALU.add)
            dve.drain()
            v.tensor_copy(k.win[:, :], wpack[:, :])
            dve.drain()

        @block.tensor
        def _(pe):
            t = nc.tensor
            pe.wait_ge(s_const, 1)
            pe.wait_ge(s_key, 1)
            t.matmul(pa[:, 0:GROUPS], k.ones_row[:, :], key[:, :], start=True, stop=True).then_inc(s_keyb, 1)
            pe.wait_ge(s_dst, 1)
            for a, c in ((0, 0), (1, GROUP - 1)):
                for h in range(2):
                    last = t.matmul(pc[0:1, a * STEPS + h * HALF:a * STEPS + (h + 1) * HALF],
                                    dst[0:HALF, h, c:c + 1], k.ident[0:HALF, 0:HALF], start=True, stop=True)
            last.then_inc(s_rows, 1)
            pe.wait_ge(s_mrow, 1)
            for a in range(2):
                for h in range(2):
                    t.matmul(pc[0:HALF, 2 * a + h:2 * a + h + 1], cont[:, a + h * HALF:a + (h + 1) * HALF],
                             k.ones_row[0:1, 0:1], start=True, stop=True)
            t.matmul(pa[0:HEADS, 0:2 * STEPS], k.ones_row[0:1, 0:HEADS], mrows[:, 0:2, :],
                     start=True, stop=True).then_inc(s_mrowb, 1)
            pm = pd[:, 0:4, :].rearrange("o a s -> o (a s)")
            t.matmul(pm[0:HEADS, 0:2 * STEPS], k.ones_row[0:1, 0:HEADS], mrows[:, 2:4, :],
                     start=True, stop=True).then_inc(s_mrowb, 1)
            pe.wait_ge(s_end, 1)
            for n, tt in enumerate((dloc, end, srcf)):
                for h in range(2):
                    for j in range(2):
                        last = t.transpose(pd[:, 4 * n + 2 * h + j, 0:HALF], tt[0:HALF, h, j * P:(j + 1) * P],
                                           k.ident[0:HALF, 0:HALF])
            last.then_inc(s_cols, 1)
            for h in range(2):
                last = t.matmul(pc[0:1, 8 + h * HALF:8 + (h + 1) * HALF], wcol[0:HALF, h:h + 1],
                                k.ident[0:HALF, 0:HALF], start=True, stop=True)
            last.then_inc(s_winrow, 1)


class Shared:

    def __init__(self, nc, ctx, arrays):
        self.x = arrays["x"]
        self.src = arrays["src"]
        self.dst = arrays["dst"]
        self.L0_gnn_W_in_b = arrays["L0_gnn_W_in_b"]
        self.L0_gnn_W_in_w = arrays["L0_gnn_W_in_w"]
        self.L0_gnn_W_out_b = arrays["L0_gnn_W_out_b"]
        self.L0_gnn_W_out_w = arrays["L0_gnn_W_out_w"]
        self.L0_gnn_W_upd_b = arrays["L0_gnn_W_upd_b"]
        self.L0_gnn_W_upd_w = arrays["L0_gnn_W_upd_w"]
        self.L0_gnn_ffn1_b = arrays["L0_gnn_ffn1_b"]
        self.L0_gnn_ffn1_w = arrays["L0_gnn_ffn1_w"]
        self.L0_gnn_ffn2_b = arrays["L0_gnn_ffn2_b"]
        self.L0_gnn_ffn2_w = arrays["L0_gnn_ffn2_w"]
        self.L0_gnn_ln1_b = arrays["L0_gnn_ln1_b"]
        self.L0_gnn_ln1_g = arrays["L0_gnn_ln1_g"]
        self.L0_gnn_ln2_b = arrays["L0_gnn_ln2_b"]
        self.L0_gnn_ln2_g = arrays["L0_gnn_ln2_g"]
        self.L1_gnn_Wk0 = arrays["L1_gnn_Wk0"]
        self.L1_gnn_Wk1 = arrays["L1_gnn_Wk1"]
        self.L1_gnn_Wq0 = arrays["L1_gnn_Wq0"]
        self.L1_gnn_Wq1 = arrays["L1_gnn_Wq1"]
        self.L1_gnn_Ws0 = arrays["L1_gnn_Ws0"]
        self.L1_gnn_Ws1 = arrays["L1_gnn_Ws1"]
        self.L1_gnn_Wv0 = arrays["L1_gnn_Wv0"]
        self.L1_gnn_Wv1 = arrays["L1_gnn_Wv1"]
        self.L1_gnn_bk0 = arrays["L1_gnn_bk0"]
        self.L1_gnn_bk1 = arrays["L1_gnn_bk1"]
        self.L1_gnn_bq0 = arrays["L1_gnn_bq0"]
        self.L1_gnn_bq1 = arrays["L1_gnn_bq1"]
        self.L1_gnn_bs0 = arrays["L1_gnn_bs0"]
        self.L1_gnn_bs1 = arrays["L1_gnn_bs1"]
        self.L1_gnn_bv0 = arrays["L1_gnn_bv0"]
        self.L1_gnn_bv1 = arrays["L1_gnn_bv1"]
        self.L2_gnn_W_l = arrays["L2_gnn_W_l"]
        self.L2_gnn_W_r = arrays["L2_gnn_W_r"]
        self.L2_gnn_att = arrays["L2_gnn_att"]
        self.L2_gnn_bias = arrays["L2_gnn_bias"]
        self.L2_gnn_ln_b = arrays["L2_gnn_ln_b"]
        self.L2_gnn_ln_w = arrays["L2_gnn_ln_w"]
        self.L3_gnn_W = arrays["L3_gnn_W"]
        self.L3_gnn_att_w = arrays["L3_gnn_att_w"]
        self.L3_gnn_b = arrays["L3_gnn_b"]
        self.L3_gnn_norm_b = arrays["L3_gnn_norm_b"]
        self.L3_gnn_norm_w = arrays["L3_gnn_norm_w"]
        self.nc, self.ctx, self.counts, self.names = nc, ctx, {}, {}

    def own(self, name):
        self.names[name] = self.names.get(name, -1) + 1
        return f"{name}_{self.names[name]}" if self.names[name] else name

    def fresh(self, name):
        return self.ctx.enter_context(self.nc.semaphore(name))

    def count(self, name, ahead=0, unit=1):
        if name not in self.counts:
            self.counts[name] = Count(self.fresh(name), ahead, unit)
        c = self.counts[name]
        c.ahead, c.unit = ahead, unit
        return c

    def close(self, n, *counts):
        for c in counts:
            c.base += (n + c.ahead) * c.unit


class OneHotWriter:
    UO = 5
    W = 4 * GROUP
    N = (STEPS * GROUP) // W

    def __init__(self, nc, ctx, k):
        self.nc, self.k = nc, k
        self.local = ctx.enter_context(nc.sbuf_tensor(k.own("local_dst"), [P, self.UO, self.W], BF16))
        self.hot = ctx.enter_context(nc.sbuf_tensor(k.own("one_hot"), [P, self.UO, self.W], BF16))
        self.loaded = [k.fresh(f"local_loaded{u}") for u in range(self.UO)]
        self.made = [k.fresh(f"one_hot_made{u}") for u in range(self.UO)]
        self.stored = [k.fresh(f"one_hot_stored{u}") for u in range(self.UO)]
        self.passed = k.fresh("one_hot_passed")

    def load(self, sp):
        UO, W = self.UO, self.W
        flat = self.k.dloc_dram.rearrange("s (o e) -> o (s e)", o=1)
        with sp.Fori(0, self.N // UO) as i:
            for u in range(UO):
                sp.wait_ge(self.made[u], i + 1)
                sp.dma_start(self.local[:, u, :], flat[:, ds((i * UO + u) * W, W)].partition_broadcast(P)
                             ).then_inc(self.loaded[u], 16)

    def write(self, pool):
        UO, W = self.UO, self.W

        def chunk_out(i, u, first=False):
            pool.wait_ge(self.loaded[u], i * 16 + 16)
            if not first:
                pool.wait_ge(self.stored[u], i * 16)
            pool.sem_inc(self.passed)
            self.nc.gpsimd.tensor_scalar(self.hot[:, u, :], self.local[:, u, :], self.k.iota_p[:, 0:1], None,
                                         ALU.is_equal).then_inc(self.made[u], 1)
            pool.wait_ge(self.made[u], i + 2)
            pool.sem_inc(self.passed)
            pool.dma_start(self.k.hot_dram[:, ds((i * UO + u) * W, W)], self.hot[:, u, :]).then_inc(self.stored[u], 16)
        for u in range(UO):
            pool.sem_inc(self.made[u], 1)
        for u in range(UO):
            chunk_out(0, u, first=True)
        with pool.Fori(1, self.N // UO) as i:
            for u in range(UO):
                chunk_out(i, u)
        for u in range(UO):
            pool.wait_ge(self.stored[u], 16 * (self.N // UO))



def norm_head(dve, x, w, var_made):
    v = w.vector
    v.tensor_reduce(w.mean[:, :], x, AXX, ALU.add)
    dve.drain()
    v.tensor_scalar(w.mean[:, :], w.mean[:, :], 1.0 / D, None, ALU.mult)
    dve.drain()
    v.tensor_tensor(w.c[:, :, :], x, w.mean[:, :].unsqueeze(2).broadcast_to([P, CH, D]), ALU.subtract)
    dve.drain()
    v.tensor_tensor(w.sq[:, :, :], w.c[:, :, :], w.c[:, :, :], ALU.mult)
    dve.drain()
    v.tensor_reduce(w.var[:, :], w.sq[:, :, :], AXX, ALU.add).then_inc(var_made.sem, 1)


def norm_sqrt(act, nc, w, var_made, sd_made, n):
    act.wait_ge(*var_made.done(n))
    nc.scalar.activation(w.sd[:, :], w.var[:, :], ACT.Sqrt, bias=w.eps[:, 0:1], scale=1.0 / D)\
      .then_inc(sd_made.sem, 1)


def norm_tail(dve, w, out, sd_made, n):
    v = w.vector
    dve.wait_ge(*sd_made.done(n))
    v.reciprocal(w.rstd[:, :], w.sd[:, :])
    dve.drain()
    v.tensor_tensor(out, w.c[:, :, :], w.rstd[:, :].unsqueeze(2).broadcast_to([P, CH, D]), ALU.mult)
    dve.drain()


def over_rows(row):
    return row.unsqueeze(1).broadcast_to([P, CH, D])


class Scratch:

    def __init__(self, nc, sb, name, eps):
        self.vector = nc.vector
        self.mean = sb(name + "_mean", [P, CH])
        self.var = sb(name + "_var", [P, CH])
        self.sd = sb(name + "_sd", [P, CH])
        self.rstd = sb(name + "_rstd", [P, CH])
        self.c = sb(name + "_c", [P, CH, D])
        self.sq = sb(name + "_sq", [P, CH, D])
        self.eps = eps


def chunk(t, i):
    return t[:, ds(i * CH, CH), :]


def rows_of(dram, i, width):
    return dram.rearrange("(w p) d -> p w d", p=P)[:, ds(i * CH, CH), 0:width]


def load_phase(nc, k):
    with ExitStack() as ctx:
        s_pad = ctx.enter_context(nc.semaphore(k.own("x_padding_cleared")))
        s_x = ctx.enter_context(nc.semaphore(k.own("x_loaded")))
        block = ctx.enter_context(nc.Block())

        @block.vector
        def _(dve):
            nc.vector.memset(k.X[:, WINDOWS - 1, :], 0.0).then_inc(s_pad, 1)
            nc.vector.memset(k.eps5[:, :], 1.0e-5)
            dve.drain()

        @block.sync
        def _(sp):
            sp.dma_start(k.X[:, 0:WINDOWS - 1, :], k.x[0:(WINDOWS - 1) * P, :].rearrange("(w p) d -> p w d", p=P))\
              .then_inc(s_x, 16)
            sp.wait_ge(s_pad, 1)
            sp.dma_start(k.X[0:LAST, WINDOWS - 1, :], k.x[(WINDOWS - 1) * P:NODES, :]).then_inc(s_x, 16)
            sp.wait_ge(s_x, 32)


def edge_conv_in_phase(nc, k):
    with ExitStack() as ctx:
        def sb(name, shape, dt=F32):
            return ctx.enter_context(nc.sbuf_tensor(k.own(name), shape, dt))
        wts = sb("w_in", [D, D])
        b = sb("b_in", [P, D])
        w = Scratch(nc, sb, "n0", k.eps5)
        h = sb("h", [P, CH, D])
        hT = sb("hT", [P, CH, D])
        g = sb("g", [P, CH, D])
        pT = ctx.enter_context(nc.psum_tensor(k.own("pT"), [P, 8, D], F32))
        pG = ctx.enter_context(nc.psum_tensor(k.own("pG"), [P, 8, D], F32))
        s_w = k.fresh("weights_in")
        var, sd, h_made, turned, hT_made, g_prod, g_made = (k.count(n) for n in (
            "var_made", "sd_made", "h_made", "h_turned", "hT_made", "g_product", "g_made"))
        g_out = k.count("rows_stored_chunk", 1, 16)
        with nc.Block() as block:
            @block.sync
            def _(sp):
                sp.dma_start(wts[:, :], k.L0_gnn_W_in_w).then_inc(s_w, 16)
                sp.dma_start(b[:, :], k.L0_gnn_W_in_b.rearrange("(o n) -> o n", o=1).partition_broadcast(P)).then_inc(s_w, 16)
                with sp.Fori(0, CHUNKS) as i:
                    sp.wait_ge(*g_made.done(i + 1))
                    sp.dma_start(rows_of(k.g_dram, i, D), g[:, :, :]).then_inc(g_out.sem, 16)
                sp.wait_ge(*g_out.done(CHUNKS))

            @block.vector
            def _(dve):
                v = nc.vector
                dve.wait_ge(s_w, 32)
                dve.sem_inc(g_out.sem, 16)
                with dve.Fori(0, CHUNKS) as i:
                    norm_head(dve, chunk(k.X, i), w, var)
                    norm_tail(dve, w, h[:, :, :], sd, i + 1)
                    v.tensor_scalar(h[:, :, :], h[:, :, :], 0.0, None, ALU.max)
                    dve.drain()
                    v.tensor_copy(chunk(k.H, i), h[:, :, :])
                    dve.drain().then_inc(h_made.sem, 1)
                    dve.wait_ge(*g_prod.done(i + 1))
                    dve.wait_ge(*g_out.free(i + 1, 1))
                    v.tensor_tensor(g[:, :, :], pG[:, 0:CH, :], over_rows(b[:, :]), ALU.add)
                    dve.drain().then_inc(g_made.sem, 1)
                    v.tensor_copy(chunk(k.G, i), g[:, :, :])
                    dve.drain()

            @block.scalar
            def _(act):
                with act.Fori(0, CHUNKS) as i:
                    norm_sqrt(act, nc, w, var, sd, i + 1)
                    act.wait_ge(*turned.done(i + 1))
                    nc.scalar.copy(hT[:, :, :], pT[:, 0:CH, :]).then_inc(hT_made.sem, 1)

            @block.tensor
            def _(pe):
                pe.wait_ge(s_w, 32)
                with pe.Fori(0, CHUNKS) as i:
                    pe.wait_ge(*h_made.done(i + 1))
                    for c in range(CH):
                        last = nc.tensor.transpose(pT[:, c, :], h[:, c, :], k.ident[:, :])
                    last.then_inc(turned.sem, 1)
                    pe.wait_ge(*hT_made.done(i + 1))
                    for c in range(CH):
                        last = nc.tensor.matmul(pG[:, c, :], hT[:, c, :], wts[:, :], start=True, stop=True)
                    last.then_inc(g_prod.sem, 1)
        k.close(CHUNKS, var, sd, h_made, turned, hT_made, g_prod, g_made, g_out)


def edge_max_phase(nc, k):
    with ExitStack() as ctx:
        def sb(name, shape, dt=F32):
            return ctx.enter_context(nc.sbuf_tensor(k.own(name), shape, dt))

        def pb(name):
            return ctx.enter_context(nc.psum_tensor(k.own(name), [P, 512], F32))
        idx = sb("staged_src", [P, 2, 4], I32)
        rows = sb("g_rows", [P, U, 2, D])
        mask = sb("mask_all", [P, 2, 2 * GROUP], BF16)
        scan = sb("running_max", [P, 2, GROUP])
        msg = sb("max_rows", [P, 2, 2, D + 4])
        sel = sb("select_end", [P, 2, 2, P])
        pT = [pb(f"gT{p}") for p in range(2)]
        pB = [pb(f"back{p}") for p in range(2)]
        pO = [pb(f"picked{p}") for p in range(2)]
        staged, turned, scanned, back, moved, selected, summed, added, passed = (k.count(n, a) for n, a in (
            ("src_staged", 0), ("rows_turned", U), ("max_scanned", U), ("max_turned_back", U),
            ("max_moved", U), ("selection_made", 0), ("window_summed", U), ("window_added", U), ("pool_passed", 0)))
        gathered = [k.count(f"rows_gathered{u}", 0, 32) for u in range(U)]
        masked = [k.count(f"mask_loaded{v}", 0, 16) for v in range(2)]
        flat = k.mask_dram.rearrange("s (o e) -> o (s e)", o=1)
        with nc.Block() as block:
            @block.sync
            def _(sp):
                with sp.Fori(0, ITERS) as i:
                    for h in range(2):
                        sp.wait_ge(*scanned.free(U * i + 2 * h + 2, U))
                        sp.dma_start(mask[:, h, :], flat[:, ds((2 * i + h) * 2 * GROUP, 2 * GROUP)].partition_broadcast(P)
                                     ).then_inc(masked[h].sem, 16)

            @block.gpsimd
            def _(pool):
                gather_rows(nc, k, pool, idx, rows, D, k.g_dram, staged, passed, (turned,), gathered)

            @block.tensor
            def _(pe):
                t = nc.tensor
                for c in (turned, back, summed):
                    pe.sem_inc(c.sem, U)

                def turn(i, u):
                    pe.wait_ge(*gathered[u].done(i + 1))
                    pe.wait_ge(*scanned.free(U * i + u + 1, 2))
                    for j in range(2):
                        last = t.transpose(pT[u % 2][:, j * P:(j + 1) * P], rows[:, u, j, :], k.ident[:, :])
                    last.then_inc(turned.sem, 1)

                def turn_back(i, u):
                    pe.wait_ge(*scanned.done(U * i + u + 1))
                    pe.wait_ge(*moved.free(U * i + u + 1, 2))
                    for j in range(2):
                        last = t.transpose(pB[u % 2][:, j * P:(j + 1) * P], scan[:, u % 2, j * P:(j + 1) * P],
                                           k.ident[:, :])
                    last.then_inc(back.sem, 1)

                def pick(i, u):
                    pe.wait_ge(*moved.done(U * i + u + 1))
                    pe.wait_ge(*selected.done(U * i + u + 1))
                    pe.wait_ge(*added.free(U * i + u + 1, 2))
                    for j in range(2):
                        last = t.matmul(pO[u % 2][:, 0:D + 1], sel[:, u % 2, j, :], msg[:, u % 2, j, 0:D + 1],
                                        start=(j == 0), stop=(j == 1))
                    last.then_inc(summed.sem, 1)

                def slot(i, u, to_come):
                    if to_come > 2:
                        turn(i + (u + 2) // U, (u + 2) % U)
                    if to_come > 1:
                        turn_back(i + (u + 1) // U, (u + 1) % U)
                    pick(i, u)
                turn(0, 0)
                turn(0, 1)
                turn_back(0, 0)
                with pe.Fori(0, ITERS - 1) as i:
                    for u in range(U):
                        slot(i, u, U)
                for u in range(U):
                    slot(ITERS - 1, u, U - u)

            @block.scalar
            def _(act):
                act.sem_inc(moved.sem, U)
                with act.Fori(0, ITERS) as i:
                    for u in range(U):
                        act.wait_ge(*back.done(U * i + u + 1))
                        act.wait_ge(*summed.free(U * i + u + 1, 2))
                        nc.scalar.copy(msg[:, u % 2, :, 0:D], pB[u % 2][:, 0:2 * P].rearrange("p (j d) -> p j d", j=2)
                                       ).then_inc(moved.sem, 1)

            @block.vector
            def _(dve):
                v = nc.vector
                v.memset(k.acc[:, 0:WINDOWS * (D + 1)], 0.0)
                v.memset(msg[:, :, :, D:D + 1], 1.0)
                v.memset(scan[:, 1, GROUP - 1:GROUP], -BIG)
                dve.drain()
                dve.sem_inc(scanned.sem, U)
                dve.sem_inc(added.sem, U)

                def run_max(i, u):
                    dve.drain()
                    dve.wait_ge(*turned.done(U * i + u + 1))
                    dve.wait_ge(*back.free(U * i + u + 1, 2))
                    if u % 2 == 0:
                        dve.wait_ge(*masked[u // 2].done(i + 1))
                    v.tensor_tensor_scan(scan[:, u % 2, :], mask[:, u // 2, (u % 2) * GROUP:(u % 2 + 1) * GROUP],
                                         pT[u % 2][:, 0:GROUP], scan[:, 1 - u % 2, GROUP - 1:GROUP], ALU.add, ALU.max
                                         ).then_inc(scanned.sem, 1)

                def select(i, u):
                    dve.wait_ge(*summed.free(U * i + u + 1, 2))
                    for j in range(2):
                        col = U * 2 * i + 2 * u + j
                        last = v.tensor_scalar(sel[:, u % 2, j, :], k.iota_row[:, :], k.dloc_e[:, ds(col, 1)],
                                               k.end_e[:, ds(col, 1)], ALU.is_equal, ALU.mult)
                    last.then_inc(selected.sem, 1)

                def add(i, u, win):
                    dve.drain()
                    dve.wait_ge(*summed.done(U * i + u + 1))
                    acc = k.acc[:, ds(win[u] * (D + 1), D + 1)]
                    v.tensor_tensor(acc, acc, pO[u % 2][:, 0:D + 1], ALU.add).then_inc(added.sem, 1)

                def slot(i, u, win, to_come):
                    if to_come > 2:
                        run_max(i + (u + 2) // U, (u + 2) % U)
                    if to_come > 1:
                        select(i + (u + 1) // U, (u + 1) % U)
                    add(i, u, win)
                run_max(0, 0)
                run_max(0, 1)
                select(0, 0)
                with dve.Fori(0, ITERS - 1) as i:
                    win = windows_of(dve, k, i)
                    for u in range(U):
                        slot(i, u, win, U)
                win = windows_of(dve, k, ITERS - 1)
                for u in range(U):
                    slot(ITERS - 1, u, win, U - u)
        k.close(STEPS, turned, scanned, back, moved, selected, summed, added)
        k.close(2 * ITERS, staged, passed)
        k.close(ITERS, *gathered, *masked)


def gather_rows(nc, k, pool, idx, rows, width, table, staged, passed, taken, gathered, kept=()):
    with pool.Fori(0, ITERS) as i:
        for h in range(2):
            for c in taken:
                pool.wait_ge(*c.free(U * i + 2 * h + 2, U))
            for c in kept[2 * h:2 * h + 2]:
                pool.wait_ge(*c.free(i + 1, 1))
            pool.sem_inc(passed.sem)
            nc.gpsimd.tensor_copy(idx[:, h, :], k.src_e[:, ds(2 * U * i + 4 * h, 4)]).then_inc(staged.sem, 1)
            pool.wait_ge(*staged.done(2 * i + h + 1))
            pool.sem_inc(passed.sem)
            for n in range(4):
                u, j = 2 * h + n // 2, n % 2
                nc.gpsimd.indirect_dma_start(rows[:, u, j, 0:width], None, table,
                                             bass.IndirectOffsetOnAxis(ap=idx[:, h, n:n + 1], axis=0)
                                             ).then_inc(gathered[u].sem, 16)


def edge_conv_out_phase(nc, k):
    with ExitStack() as ctx:
        def sb(name, shape, dt=F32):
            return ctx.enter_context(nc.sbuf_tensor(k.own(name), shape, dt))

        def pb(name):
            return ctx.enter_context(nc.psum_tensor(k.own(name), [P, 8, D], F32))
        w_upd = sb("w_upd", [D, 2, D])
        w_out = sb("w_out", [D, D])
        w_f1 = sb("w_f1", [D, 4, D])
        w_f2 = sb("w_f2", [D, 4, D])
        b_upd = sb("b_upd", [D, 1])
        b_f1 = sb("b_f1", [D, 4])
        bc = sb("rows_bc", [P, 6, D])
        w = Scratch(nc, sb, "n1", k.eps5)
        one_hots = OneHotWriter(nc, ctx, k)
        md = sb("max_diff", [P, CH, D])
        gT = sb("gT", [P, CH, D])
        mT = sb("mT", [P, CH, D])
        uT = sb("uT", [P, CH, D])
        x1 = sb("x1", [P, CH, D])
        x1T = sb("x1T", [P, CH, D])
        y = sb("y", [P, CH, D])
        fT = sb("fT", [P, 4, CH, D])
        pA, pB, pC, pD = pb("pA"), pb("pB"), pb("pC"), pb("pD")
        s_w = k.fresh("weights_out")
        (md_made, turned, gT_made, u_prod, uT_made, o_prod, var, sd, x1_made, x1_turned, x1T_made, f_prod, f_made,
         y_prod, chunk_done) = (k.count(n) for n in (
             "h_made", "h_turned", "hT_made", "u_product", "uT_made", "o_product", "var_made", "sd_made",
             "x1_made", "x1_turned", "x1T_made", "ffn_product", "ffn_made", "y_product", "chunk_done"))
        srcs = ((w_upd[:, :, :], k.L0_gnn_W_upd_w.rearrange("(c p) n -> p c n", p=D)),
                (w_out[:, :], k.L0_gnn_W_out_w),
                (w_f1[:, :, :], k.L0_gnn_ffn1_w.rearrange("p (c n) -> p c n", n=D)),
                (w_f2[:, :, :], k.L0_gnn_ffn2_w.rearrange("(c p) n -> p c n", p=D)),
                (b_upd[:, :], k.L0_gnn_W_upd_b.rearrange("(p o) -> p o", o=1)),
                (b_f1[:, :], k.L0_gnn_ffn1_b.rearrange("(c p) -> p c", p=D)))
        rows = (k.L0_gnn_W_out_b, k.L0_gnn_ln1_g, k.L0_gnn_ln1_b, k.L0_gnn_ffn2_b, k.L0_gnn_ln2_g, k.L0_gnn_ln2_b)
        loaded = 16 * (len(srcs) + len(rows))
        with nc.Block() as block:
            @block.sync
            def _(sp):
                with nc.allow_non_contiguous_dma(reason="small columns of biases"):
                    for out, src in srcs:
                        sp.dma_start(out, src).then_inc(s_w, 16)
                for n, row in enumerate(rows):
                    sp.dma_start(bc[:, n, :], row.rearrange("(o n) -> o n", o=1).partition_broadcast(P)).then_inc(s_w, 16)
                one_hots.load(sp)

            @block.gpsimd
            def _(pool):
                one_hots.write(pool)

            @block.vector
            def _(dve):
                v = nc.vector
                acc = k.acc[:, 0:WINDOWS * (D + 1)].rearrange("p (w d) -> p w d", d=D + 1)
                dve.wait_ge(s_w, loaded)
                with dve.Fori(0, CHUNKS) as i:
                    a = acc[:, ds(i * CH, CH), :]
                    v.tensor_tensor(md[:, :, :], chunk(k.G, i), a[:, :, D:D + 1].broadcast_to([P, CH, D]), ALU.mult)
                    v.tensor_copy(y[:, :, :], chunk(k.G, i))
                    dve.drain()
                    v.tensor_tensor(md[:, :, :], a[:, :, 0:D], md[:, :, :], ALU.subtract).then_inc(md_made.sem, 1)
                    dve.wait_ge(*o_prod.done(i + 1))
                    v.tensor_tensor(x1[:, :, :], pA[:, 0:CH, :], over_rows(bc[:, 0, :]), ALU.add)
                    dve.drain()
                    v.tensor_tensor(x1[:, :, :], x1[:, :, :], chunk(k.H, i), ALU.add)
                    dve.drain()
                    norm_head(dve, x1[:, :, :], w, var)
                    norm_tail(dve, w, x1[:, :, :], sd, 2 * i + 1)
                    v.tensor_tensor(x1[:, :, :], x1[:, :, :], over_rows(bc[:, 1, :]), ALU.mult)
                    dve.drain()
                    v.tensor_tensor(x1[:, :, :], x1[:, :, :], over_rows(bc[:, 2, :]), ALU.add).then_inc(x1_made.sem, 1)
                    dve.wait_ge(*y_prod.done(i + 1))
                    v.tensor_tensor(y[:, :, :], pB[:, 0:CH, :], over_rows(bc[:, 3, :]), ALU.add)
                    dve.drain()
                    v.tensor_tensor(y[:, :, :], y[:, :, :], x1[:, :, :], ALU.add)
                    dve.drain()
                    norm_head(dve, y[:, :, :], w, var)
                    norm_tail(dve, w, y[:, :, :], sd, 2 * i + 2)
                    v.tensor_tensor(y[:, :, :], y[:, :, :], over_rows(bc[:, 4, :]), ALU.mult)
                    dve.drain()
                    v.tensor_tensor(y[:, :, :], y[:, :, :], over_rows(bc[:, 5, :]), ALU.add)
                    dve.drain()
                    v.tensor_tensor(chunk(k.X, i), chunk(k.X, i), y[:, :, :], ALU.add)
                    dve.drain().then_inc(chunk_done.sem, 1)

            @block.scalar
            def _(act):
                s = nc.scalar
                with act.Fori(0, CHUNKS) as i:
                    act.wait_ge(*turned.done(i + 1))
                    s.copy(gT[:, :, :], pA[:, 0:CH, :])
                    s.copy(mT[:, :, :], pB[:, 0:CH, :]).then_inc(gT_made.sem, 1)
                    act.wait_ge(*u_prod.done(i + 1))
                    s.activation(uT[:, :, :], pC[:, 0:CH, :], ACT.Identity, bias=b_upd[:, 0:1]).then_inc(uT_made.sem, 1)
                    norm_sqrt(act, nc, w, var, sd, 2 * i + 1)
                    act.wait_ge(*x1_turned.done(i + 1))
                    s.copy(x1T[:, :, :], pA[:, 0:CH, :]).then_inc(x1T_made.sem, 1)
                    for f in range(4):
                        act.wait_ge(*f_prod.done(4 * i + f + 1))
                        s.activation(fT[:, f, :, :], (pC, pD)[f % 2][:, 0:CH, :], ACT.Gelu, bias=b_f1[:, f:f + 1]
                                     ).then_inc(f_made.sem, 1)
                    norm_sqrt(act, nc, w, var, sd, 2 * i + 2)

            @block.tensor
            def _(pe):
                t = nc.tensor

                def wide(out, lhsT, rhs, start, stop):
                    t.matmul(out[:, 0:4, :], lhsT, rhs[:, 0:4, :], start=start, stop=stop)
                    return t.matmul(out[:, 4:CH, :], lhsT, rhs[:, 4:CH, :], start=start, stop=stop)
                pe.wait_ge(s_w, loaded)

                with pe.Fori(0, CHUNKS) as i:
                    pe.wait_ge(*md_made.done(i + 1))
                    for c in range(CH):
                        t.transpose(pA[:, c, :], y[:, c, :], k.ident[:, :])
                        last = t.transpose(pB[:, c, :], md[:, c, :], k.ident[:, :])
                    last.then_inc(turned.sem, 1)
                    pe.wait_ge(*gT_made.done(i + 1))
                    wide(pC, w_upd[:, 0, :], gT, True, False)
                    wide(pC, w_upd[:, 1, :], mT, False, True).then_inc(u_prod.sem, 1)
                    pe.wait_ge(*uT_made.done(i + 1))
                    for c in range(CH):
                        last = t.matmul(pA[:, c, :], uT[:, c, :], w_out[:, :], start=True, stop=True)
                    last.then_inc(o_prod.sem, 1)
                    pe.wait_ge(*x1_made.done(i + 1))
                    for c in range(CH):
                        last = t.transpose(pA[:, c, :], x1[:, c, :], k.ident[:, :])
                    last.then_inc(x1_turned.sem, 1)
                    pe.wait_ge(*x1T_made.done(i + 1))
                    for f in range(4):
                        if f >= 2:
                            pe.wait_ge(*f_made.done(4 * i + f - 1))
                        wide((pC, pD)[f % 2], w_f1[:, f, :], x1T, True, True).then_inc(f_prod.sem, 1)
                    pe.wait_ge(*f_made.done(4 * i + 4))
                    for c in range(CH):
                        for f in range(4):
                            last = t.matmul(pB[:, c, :], fT[:, f, c, :], w_f2[:, f, :], start=(f == 0), stop=(f == 3))
                    last.then_inc(y_prod.sem, 1)
        k.close(CHUNKS, md_made, turned, gT_made, u_prod, uT_made, o_prod, x1_made, x1_turned, x1T_made, y_prod,
                chunk_done)
        k.close(2 * CHUNKS, var, sd)
        k.close(4 * CHUNKS, f_prod, f_made)



def split3(dve, nc, full, hi, mid, lo, rest):
    v = nc.vector
    v.tensor_copy(hi, full)
    dve.drain()
    v.tensor_tensor(rest, full, hi, ALU.subtract)
    dve.drain()
    v.tensor_copy(mid, rest)
    dve.drain()
    return v.tensor_tensor(lo, rest, mid, ALU.subtract)


def conv1_in_phase(nc, k):
    with ExitStack() as ctx:
        def sb(name, shape, dt=F32):
            return ctx.enter_context(nc.sbuf_tensor(k.own(name), shape, dt))

        def pb(name, shape):
            return ctx.enter_context(nc.psum_tensor(k.own(name), shape, F32))
        wq = sb("wq", [D, HEADS, D])
        wk = sb("wk", [D, HEADS, D])
        wkT = sb("wkT", [D, HEADS, D + 1])
        bq = sb("bq", [D, HEADS])
        w = Scratch(nc, sb, "n2", k.eps5)
        h = sb("h", [P, CH, D + 4])
        hT = sb("hT", [P, CH, D])
        qT = sb("qT", [P, HEADS, CH, D])
        rest = sb("rest", [P, HEADS, D + 1])
        pT = pb("pT", [P, 8, D])
        pQ = pb("pQ", [P, 8, D])
        pU = [pb(f"pU{n}", [P, HEADS, 256]) for n in range(2)]
        s_w = k.fresh("weights_conv1")
        s_k = k.fresh("wk_turned")
        s_kT = k.fresh("wkT_made")
        var, sd, h_made, turned, hT_made = (k.count(n) for n in (
            "var_made", "sd_made", "h_made", "h_turned", "hT_made"))
        h_out = k.count("rows_stored_chunk", 1, 16)
        q_prod, qT_made = k.count("q_product"), k.count("qT_made", 1)
        u_prod, u_split = k.count("u_product"), k.count("u_split", 2)
        with nc.Block() as block:
            @block.sync
            def _(sp):
                with nc.allow_non_contiguous_dma(reason="small columns of biases"):
                    sp.dma_start(wq[:, :, :], k.L1_gnn_Wq0.rearrange("p (h n) -> p h n", n=D)).then_inc(s_w, 16)
                    sp.dma_start(wk[:, :, :], k.L1_gnn_Wk0.rearrange("p (h n) -> p h n", n=D)).then_inc(s_w, 16)
                    sp.dma_start(bq[:, :], k.L1_gnn_bq0.rearrange("(h p) -> p h", p=D)).then_inc(s_w, 16)
                    sp.dma_start(wkT[:, :, D], k.L1_gnn_bk0.rearrange("(h p) -> p h", p=D)).then_inc(s_w, 16)
                with sp.Fori(0, CHUNKS) as i:
                    sp.wait_ge(*h_made.done(i + 1))
                    sp.dma_start(rows_of(k.h_dram, i, D + 4), h[:, :, :]).then_inc(h_out.sem, 16)
                sp.wait_ge(*h_out.done(CHUNKS))

            @block.vector
            def _(dve):
                v = nc.vector
                dve.wait_ge(s_w, 64)
                v.memset(h[:, :, D:D + 4], 1.0)
                dve.wait_ge(s_k, 1)
                v.tensor_copy(wkT[:, :, 0:D], pT[:, 0:HEADS, :])
                dve.drain().then_inc(s_kT, 1)
                dve.sem_inc(h_out.sem, 16)
                dve.sem_inc(u_split.sem, 2)
                with dve.Fori(0, CHUNKS) as i:
                    norm_head(dve, chunk(k.X, i), w, var)
                    dve.wait_ge(*h_out.free(i + 1, 1))
                    norm_tail(dve, w, h[:, :, 0:D], sd, i + 1)
                    v.tensor_scalar(h[:, :, 0:D], h[:, :, 0:D], 0.0, None, ALU.max)
                    dve.drain()
                    v.tensor_copy(chunk(k.H, i), h[:, :, 0:D])
                    dve.drain().then_inc(h_made.sem, 1)
                    for c in range(CH):
                        dve.wait_ge(*u_prod.done(CH * i + c + 1))
                        part = [k.U[:, ds(i * (CH * 3 * HW1) + (3 * c + n) * HW1, HW1)]
                                .rearrange("p (h d) -> p h d", h=HEADS) for n in range(3)]
                        split3(dve, nc, pU[c % 2][:, :, 0:D + 1], *part, rest[:, :, :])
                        dve.drain().then_inc(u_split.sem, 1)

            @block.scalar
            def _(act):
                act.sem_inc(qT_made.sem, 1)
                act.wait_ge(s_w, 64)
                with act.Fori(0, CHUNKS) as i:
                    norm_sqrt(act, nc, w, var, sd, i + 1)
                    act.wait_ge(*turned.done(i + 1))
                    nc.scalar.copy(hT[:, :, :], pT[:, 0:CH, :]).then_inc(hT_made.sem, 1)
                    for hh in range(HEADS):
                        act.wait_ge(*q_prod.done(HEADS * i + hh + 1))
                        nc.scalar.activation(qT[:, hh, :, :], pQ[:, 0:CH, :], ACT.Identity, bias=bq[:, hh:hh + 1]
                                             ).then_inc(qT_made.sem, 1)

            @block.tensor
            def _(pe):
                t = nc.tensor
                pe.wait_ge(s_w, 64)
                for hh in range(HEADS):
                    last = t.transpose(pT[:, hh, :], wk[:, hh, :], k.ident[:, :])
                last.then_inc(s_k, 1)
                pe.wait_ge(s_kT, 1)
                with pe.Fori(0, CHUNKS) as i:
                    pe.wait_ge(*h_made.done(i + 1))
                    for c in range(CH):
                        last = t.transpose(pT[:, c, :], h[:, c, 0:D], k.ident[:, :])
                    last.then_inc(turned.sem, 1)
                    pe.wait_ge(*hT_made.done(i + 1))
                    for hh in range(HEADS):
                        pe.wait_ge(*qT_made.free(HEADS * i + hh + 1, 1))
                        t.matmul(pQ[:, 0:4, :], wq[:, hh, :], hT[:, 0:4, :], start=True, stop=True)
                        t.matmul(pQ[:, 4:CH, :], wq[:, hh, :], hT[:, 4:CH, :], start=True, stop=True
                                 ).then_inc(q_prod.sem, 1)
                    pe.wait_ge(*qT_made.done(HEADS * i + HEADS))
                    for c in range(CH):
                        pe.wait_ge(*u_split.free(CH * i + c + 1, 2))
                        for hh in range(HEADS):
                            last = t.matmul(pU[c % 2][:, hh, 0:D + 1], qT[:, hh, c, :], wkT[:, hh, :],
                                            start=True, stop=True)
                        last.then_inc(u_prod.sem, 1)
        k.close(CHUNKS, var, sd, h_made, turned, hT_made, h_out)
        k.close(HEADS * CHUNKS, q_prod, qT_made)
        k.close(WINDOWS, u_prod, u_split)


def edge_logits_phase(nc, k, table, width, per_head, row, gat=False, keep=False):
    per = row // HEADS
    banks = 2 if row > 512 else 1
    bw = row // banks
    terms = D if gat else per
    dots = 1 if gat else HEADS
    on_dve = 0 if gat else 1
    with ExitStack() as ctx:
        def sb(name, shape, dt=F32):
            return ctx.enter_context(nc.sbuf_tensor(k.own(name), shape, dt))
        idx = sb("staged_src", [P, 2, 4], I32)
        rows = sb("src_rows", [P, U, 2, width])
        hot = sb("one_hot", [P, 2, 2 * GROUP], BF16)
        prod = sb("products", [P, U, 2, dots * terms])
        msg = sb("messages", [P, 2, 2, D if gat else 1])
        pU = [ctx.enter_context(nc.psum_tensor(k.own(f"dst_rows{n}"), [P, banks, 512], F32)) for n in range(4)]
        staged, picked, read, made, dotted, passed, act_passed = (k.count(n, a) for n, a in (
            ("src_staged", 0), ("dst_rows_picked", 0), ("edge_rows_read", U), ("products_made", 0),
            ("logits_made", U), ("pool_passed", 0), ("act_passed", 0)))
        gathered = [k.count(f"rows_gathered{u}", 0, 32) for u in range(U)]
        loaded = [k.count(f"mask_loaded{v}", 0, 16) for v in range(2)]
        kept = [k.count(f"slot_rows_kept{u}", 1, 16) for u in range(U)] if keep else ()
        with nc.Block() as block:
            if keep:
                @block.sync
                def _(sp):
                    for c in kept:
                        sp.sem_inc(c.sem, 16)
                    with sp.Fori(0, ITERS) as i:
                        for u in range(U):
                            sp.wait_ge(*gathered[u].done(i + 1))
                            sp.dma_start(k.slots_dram[:, ds((U * i + u) * 2 * width, 2 * width)],
                                         rows[:, u].rearrange("p j d -> p (j d)")).then_inc(kept[u].sem, 16)
                    for c in kept:
                        sp.wait_ge(*c.done(ITERS))

            @block.gpsimd
            def _(pool):
                gather_rows(nc, k, pool, idx, rows, width, table, staged, passed, (read,), gathered, kept)

            @block.tensor
            def _(pe):
                with pe.Fori(0, ITERS) as i:
                    win = windows_of(pe, k, i)
                    for u in range(U):
                        pe.wait_ge(*read.free(U * i + u + 1, 2))
                        if u % 2 == 0:
                            pe.wait_ge(*loaded[u // 2].done(i + 1))
                        for j in range(2):
                            lhsT = hot[:, u // 2, (u % 2) * GROUP + j * P:(u % 2) * GROUP + (j + 1) * P]
                            for part in range(3):
                                for b in range(banks):
                                    last = nc.tensor.matmul(
                                        pU[2 * (u % 2) + j][:, b, 0:bw], lhsT,
                                        k.U[:, ds(win[u] * (3 * row) + (part * row + b * bw), bw)],
                                        start=(part == 0), stop=(part == 2))
                        last.then_inc(picked.sem, 1)

            @block.vector
            def _(dve):
                v = nc.vector
                dve.sem_inc(read.sem, U)

                def head_products(src_rows, dst_rows, out):
                    hb = HEADS // banks
                    for j in range(2):
                        for b in range(banks):
                            if per_head:
                                src = src_rows[:, j, b * bw:(b + 1) * bw].rearrange("p (h d) -> p h d", h=hb)
                            else:
                                src = src_rows[:, j, 0:per].unsqueeze(1).broadcast_to([P, hb, per])
                            last = v.tensor_tensor(out[:, j, b * bw:(b + 1) * bw].rearrange("p (h d) -> p h d", h=hb),
                                                   dst_rows[j][:, b, 0:bw].rearrange("p (h d) -> p h d", h=hb),
                                                   src, ALU.mult)
                    return last

                with dve.Fori(0, ITERS) as i:
                    for u in range(U):
                        dve.wait_ge(*gathered[u].done(i + 1))
                        dve.wait_ge(*picked.done(U * i + u + 1))
                        dve.wait_ge(*dotted.free(U * i + u + 1, U))
                        dst_rows = [pU[2 * (u % 2) + j] for j in range(2)]
                        if gat:
                            m = msg[:, u % 2]
                            for j in range(2):
                                v.tensor_copy(k.selfs[:, ds(2 * U * i + 2 * u + j, 1)], dst_rows[j][:, 0, D:D + 1])
                                last = v.tensor_tensor(m[:, j], dst_rows[j][:, 0, 0:D], rows[:, u, j, 0:D], ALU.add)
                            last.then_inc(read.sem, 1)
                            dve.drain()
                            v.scalar_tensor_tensor(prod[:, u], m, 0.2, m, ALU.mult, ALU.max)
                            dve.drain()
                            v.tensor_tensor(prod[:, u], prod[:, u], k.att[:, :].unsqueeze(1).broadcast_to([P, 2, D]),
                                            ALU.mult).then_inc(made.sem, 1)
                        else:
                            head_products(rows[:, u], dst_rows, prod[:, u]).then_inc(read.sem, 1)
                            dve.drain().then_inc(made.sem, 1)
                            v.tensor_reduce(k.logits[:, 0, ds(2 * U * i + 2 * u, 2)], prod[:, u, :, 0:terms],
                                            AXX, ALU.add)

            @block.scalar
            def _(act):
                act.sem_inc(dotted.sem, U)

                def load_hot(i, h):
                    act.dma_start(hot[:, h, :], k.hot_dram[:, ds((2 * i + h) * 2 * GROUP, 2 * GROUP)]
                                  ).then_inc(loaded[h].sem, 16)

                def sum_terms(i, u):
                    act.wait_ge(*made.done(U * i + u + 1))
                    act.sem_inc(act_passed.sem)
                    for j in range(2):
                        for h in range(on_dve, dots):
                            part = prod[:, u, j, h * terms:(h + 1) * terms]
                            last = nc.scalar.activation(part, part, ACT.Copy,
                                                        accum_out=k.logits[:, h, ds(2 * U * i + 2 * u + j, 1)])
                    last.then_inc(dotted.sem, 1)
                load_hot(0, 0)
                load_hot(0, 1)
                with act.Fori(0, ITERS - 1) as i:
                    for u in range(U):
                        if u % 2:
                            act.wait_ge(*picked.done(U * i + u + 1))
                            load_hot(i + 1, u // 2)
                        sum_terms(i, u)
                for u in range(U):
                    sum_terms(ITERS - 1, u)
        k.close(STEPS, picked, read, made, dotted, act_passed)
        k.close(2 * ITERS, staged, passed)
        k.close(ITERS, *gathered, *loaded, *kept)


def value_logits_phase(nc, k):
    T = 2 * U
    W = WINDOWS + 1
    with ExitStack() as ctx:
        def sb(name, shape, dt=F32):
            return ctx.enter_context(nc.sbuf_tensor(k.own(name), shape, dt))
        hot = sb("one_hot", [P, 2, U * GROUP], BF16)
        lo = sb("src_lo", [P, 2, U * GROUP], BF16)
        lo_hot = sb("one_hot_lo", [P, 2, U * GROUP], BF16)
        hi = sb("src_hi", [P, TILES], I32)
        hi_f = sb("src_hi_f", [P, TILES])
        hi_hot = sb("one_hot_hi", [P, T, WINDOWS])
        found = sb("found", [P, T, WINDOWS])
        vals = sb("src_values", [P, T])
        pV = [ctx.enter_context(nc.psum_tensor(k.own(f"looked_up{n}"), [P, T, 64], F32)) for n in range(2)]
        loaded = [k.count(f"lookup_loaded{n}", 0, 32) for n in range(2)]
        lo_made, looked, used = k.count("one_hot_lo_made"), k.count("values_looked_up", 2), k.count("values_used", 2)
        lo_flat = k.lo_dram.rearrange("s (o e) -> o (s e)", o=1)
        N = U * GROUP
        with nc.Block() as block:
            @block.sync
            def _(sp):
                def load(i, n):
                    sp.wait_ge(*looked.free(2 * i + n + 1, 2))
                    sp.dma_start(lo[:, n, :], lo_flat[:, ds((2 * i + n) * N, N)].partition_broadcast(P)
                                 ).then_inc(loaded[n].sem, 16)
                    sp.dma_start(hot[:, n, :], k.hot_dram[:, ds((2 * i + n) * N, N)]).then_inc(loaded[n].sem, 16)
                with sp.Fori(0, ITERS // 2) as i:
                    load(i, 0)
                    load(i, 1)
                load(ITERS // 2, 0)

            @block.vector
            def _(dve):
                v = nc.vector
                v.tensor_scalar(hi[:, :], k.src_e[:, :], 7, None, ALU.arith_shift_right)
                dve.drain()
                v.tensor_copy(hi_f[:, :], hi[:, :])
                dve.drain()
                dve.sem_inc(used.sem, 2)

                def find_lo(i, n):
                    dve.wait_ge(*loaded[n].done(i + 1))
                    v.tensor_scalar(lo_hot[:, n, :], lo[:, n, :], k.iota_p[:, 0:1], None, ALU.is_equal
                                    ).then_inc(lo_made.sem, 1)

                def take(i, n):
                    v.tensor_tensor(hi_hot[:, :, :], k.iota_row[:, 0:WINDOWS].unsqueeze(1).broadcast_to([P, T, WINDOWS]),
                                    hi_f[:, ds((2 * i + n) * T, T)].unsqueeze(2).broadcast_to([P, T, WINDOWS]),
                                    ALU.is_equal)
                    dve.drain()
                    dve.wait_ge(*looked.done(2 * i + n + 1))
                    v.tensor_tensor(found[:, :, :], pV[n][:, :, 0:WINDOWS], hi_hot[:, :, :], ALU.mult)
                    dve.drain()
                    v.tensor_reduce(vals[:, :], found[:, :, :], AXX, ALU.add)
                    dve.drain()
                    v.tensor_tensor(k.logits[:, 0, ds((2 * i + n) * T, T)], vals[:, :], pV[n][:, :, WINDOWS], ALU.add
                                    ).then_inc(used.sem, 1)
                find_lo(0, 0)
                with dve.Fori(0, ITERS // 2) as i:
                    find_lo(i, 1)
                    take(i, 0)
                    find_lo(i + 1, 0)
                    take(i, 1)
                take(ITERS // 2, 0)

            @block.tensor
            def _(pe):
                pe.sem_inc(looked.sem, 2)

                def look_up(i, n):
                    win = windows_of(pe, k, 2 * i + n)
                    pe.wait_ge(*lo_made.done(2 * i + n + 1))
                    pe.wait_ge(*used.free(2 * i + n + 1, 2))
                    for t in range(T):
                        for part in range(3):
                            nc.tensor.matmul(pV[n][:, t, 0:WINDOWS], lo_hot[:, n, t * P:(t + 1) * P], k.V[:, part, :],
                                             start=(part == 0), stop=(part == 2))
                        for part in range(3):
                            last = nc.tensor.matmul(pV[n][:, t, WINDOWS:W], hot[:, n, t * P:(t + 1) * P],
                                                    k.U[:, ds(win[t // 2] * 3 + part, 1)],
                                                    start=(part == 0), stop=(part == 2))
                    last.then_inc(looked.sem, 1)
                with pe.Fori(0, ITERS // 2) as i:
                    look_up(i, 0)
                    look_up(i, 1)
                look_up(ITERS // 2, 0)
        k.close(ITERS, lo_made, looked, used)
        k.close(ITERS // 2 + 1, loaded[0])
        k.close(ITERS // 2, loaded[1])


def value_sums_phase(nc, k):
    with ExitStack() as ctx:
        def sb(name, shape, dt=F32):
            return ctx.enter_context(nc.sbuf_tensor(k.own(name), shape, dt))
        sel = sb("selection", [P, 2, U, 2, P], BF16)
        cols = sb("step_sums", [P, STEPS])
        colsT = sb("step_sums_t", [P, 2, P])
        pS = ctx.enter_context(nc.psum_tensor(k.own("step_sum"), [P, 256, 4], F32))
        pT = ctx.enter_context(nc.psum_tensor(k.own("step_sum_t"), [P, 4, P], F32))
        selected, summed = k.count("selection_made", 0), k.count("window_summed", 2)
        s_cols, s_turned, s_colsT, s_sums = (k.fresh(n) for n in (
            "step_sums_moved", "step_sums_turned", "step_sums_t_moved", "node_sums_made"))
        with nc.Block() as block:
            @block.vector
            def _(dve):
                v = nc.vector

                def select(i, n):
                    dve.wait_ge(*summed.free(2 * i + n + 1, 2))
                    at = (2 * i + n) * 2 * U
                    v.tensor_tensor(sel[:, n, :, :, :], k.iota_row[:, :].unsqueeze(1).broadcast_to([P, 2 * U, P]),
                                    k.dloc_e[:, ds(at, 2 * U)].unsqueeze(2).broadcast_to([P, 2 * U, P]),
                                    ALU.is_equal).then_inc(selected.sem, 1)
                with dve.Fori(0, ITERS // 2) as i:
                    select(i, 0)
                    select(i, 1)
                select(ITERS // 2, 0)
                dve.wait_ge(*summed.done(ITERS))
                v.tensor_reduce(cols[:, :], pS[:, 0:STEPS, 0:3], AXX, ALU.add).then_inc(s_cols, 1)
                dve.wait_ge(s_turned, 1)
                v.tensor_copy(colsT[0:HALF, :, :], pT[0:HALF, 0:2, :]).then_inc(s_colsT, 1)
                dve.wait_ge(s_sums, 1)
                v.tensor_copy(k.node_sums[:, :], pT[:, 2, 0:WINDOWS])
                dve.drain()

            @block.tensor
            def _(pe):
                pe.sem_inc(summed.sem, 2)

                def total(i, n):
                    pe.wait_ge(*selected.done(2 * i + n + 1))
                    for u in range(U):
                        s = (2 * i + n) * U + u
                        for j in range(2):
                            last = nc.tensor.matmul(pS[:, ds(s, 1), 0:3], sel[:, n, u, j, :],
                                                    k.parts[:, ds(2 * s + j, 1), :], start=(j == 0), stop=(j == 1))
                    last.then_inc(summed.sem, 1)
                with pe.Fori(0, ITERS // 2) as i:
                    total(i, 0)
                    total(i, 1)
                total(ITERS // 2, 0)
                pe.wait_ge(s_cols, 1)
                for h in range(2):
                    last = nc.tensor.transpose(pT[0:HALF, h, :], cols[:, h * HALF:(h + 1) * HALF], k.ident[:, :])
                last.then_inc(s_turned, 1)
                pe.wait_ge(s_colsT, 1)
                for h in range(2):
                    last = nc.tensor.matmul(pT[:, 2, 0:WINDOWS], colsT[0:HALF, h, :], k.win_hot[0:HALF, h, :],
                                            start=(h == 0), stop=(h == 1))
                last.then_inc(s_sums, 1)
        k.close(ITERS, selected, summed)


def segment_softmax_phase(nc, k, heads, scale, with_self=False):
    with ExitStack() as ctx:
        def sb(name, shape, dt=F32):
            return ctx.enter_context(nc.sbuf_tensor(k.own(name), shape, dt))

        def pb(name, shape):
            return ctx.enter_context(nc.psum_tensor(k.own(name), shape, F32))
        N = heads + 2 * with_self
        lt = sb("logits_t", [P, N, 2, GROUP])
        m = sb("max_t", [P, heads, 2, GROUP])
        mf = sb("max_fwd_t", [P, heads, 2, GROUP])
        edge = sb("step_ends", [HEADS, 2, STEPS])
        run = sb("running", [HEADS, 2, STEPS])
        carry = sb("carry", [HEADS, 2, STEPS])
        cc = sb("carry_t", [P, 2, 2, HEADS])
        pt = pb("pt", [P, 4, 2, GROUP])
        pr = pb("pr", [P, 512])
        pe_back = pb("pcol", [P, 4, 2, P])
        names = ("sm_turned", "sm_local", "sm_ends", "sm_carry", "sm_carry_turned", "sm_diff", "sm_exp", "sm_exp_turned",
                 "sm_done")
        turned, local, ends, carried, carry_t, diff, exped, exp_turned, back = (k.count(n) for n in names)
        HH = HALF
        with nc.Block() as block:
            @block.tensor
            def _(pe):
                t = nc.tensor
                for n in range(N):
                    src = (k.logits[:, n, :] if n < heads else (k.selfs, k.end_e)[n - heads][:, :])
                    for h in range(2):
                        for j in range(2):
                            last = t.transpose(pt[0:HH, n, h, j * P:(j + 1) * P],
                                               src[:, 2 * HH * h + j:2 * HH * (h + 1):2], k.ident[:, :])
                last.then_inc(turned.sem, 1)
                pe.wait_ge(*local.done(1))
                for a, c in ((0, GROUP - 1), (1, 0)):
                    for h in range(2):
                        last = t.matmul(pr[0:heads, a * STEPS + h * HH:a * STEPS + (h + 1) * HH],
                                        m[0:HH, :, h, c], k.ident[0:HH, 0:HH], start=True, stop=True)
                last.then_inc(ends.sem, 1)
                pe.wait_ge(*carried.done(1))
                for a in range(2):
                    for h in range(2):
                        o = (2 * a + h) * HEADS
                        last = t.matmul(pr[0:HH, o:o + heads], carry[0:heads, a, h * HH:(h + 1) * HH],
                                        k.ident[0:heads, 0:heads], start=True, stop=True)
                last.then_inc(carry_t.sem, 1)
                pe.wait_ge(*exped.done(1))
                M = heads + with_self
                for h in range(2):
                    if h:
                        pe.wait_ge(*back.done(1))
                    for n in range(M):
                        for j in range(2):
                            last = t.transpose(pe_back[:, n, j, 0:HH], lt[0:HH, n, h, j * P:(j + 1) * P],
                                               k.ident[0:HH, 0:HH])
                    last.then_inc(exp_turned.sem, 1)

            @block.vector
            def _(dve):
                v = nc.vector
                dve.wait_ge(*turned.done(1))
                v.tensor_scalar(lt[0:HH], pt[0:HH, 0:N], scale, None, ALU.mult)
                dve.drain()
                top = lt
                if with_self:
                    v.tensor_tensor(mf[0:HH, 0], lt[0:HH, 0], lt[0:HH, 1], ALU.max)
                    dve.drain()
                    v.tensor_copy(m[0:HH, 0], mf[0:HH, 0])
                    dve.drain()
                    top = m
                for n in range(heads):
                    for h in range(2):
                        v.tensor_tensor_scan(mf[0:HH, n, h, :], k.mask_t[0:HH, h, 0:GROUP], top[0:HH, n, h, :], -BIG,
                                             ALU.add, ALU.max)
                dve.drain()
                for n in range(heads):
                    for h in range(2):
                        v.tensor_tensor_scan(m[0:HH, n, h, ::-1], k.mask_t[0:HH, h, GROUP:0:-1], mf[0:HH, n, h, ::-1],
                                             -BIG, ALU.add, ALU.max)
                dve.drain().then_inc(local.sem, 1)
                dve.wait_ge(*ends.done(1))
                v.tensor_copy(edge[0:heads], pr[0:heads, 0:2 * STEPS].rearrange("p (a s) -> p a s", a=2))
                v.memset(carry[0:heads], -BIG)
                dve.drain()
                v.tensor_tensor_scan(run[0:heads, 0, :], k.step_masks[0:heads, 0, :], edge[0:heads, 0, :], -BIG,
                                     ALU.add, ALU.max)
                v.tensor_tensor_scan(run[0:heads, 1, ::-1], k.step_masks[0:heads, 1, ::-1], edge[0:heads, 1, ::-1],
                                     -BIG, ALU.add, ALU.max)
                dve.drain()
                v.tensor_tensor(carry[0:heads, 0, 1:STEPS], run[0:heads, 0, 0:STEPS - 1],
                                k.step_masks[0:heads, 2, 1:STEPS], ALU.add)
                v.tensor_tensor(carry[0:heads, 1, 0:STEPS - 1], run[0:heads, 1, 1:STEPS],
                                k.step_masks[0:heads, 3, 0:STEPS - 1], ALU.add)
                dve.drain().then_inc(carried.sem, 1)
                dve.wait_ge(*carry_t.done(1))
                v.tensor_copy(cc[0:HH, :, :, 0:heads], pr[0:HH, 0:4 * HEADS].rearrange(
                    "p (a h n) -> p a h n", a=2, h=2)[:, :, :, 0:heads])
                for a, seg in enumerate((k.first_t, k.last_t)):
                    dve.drain()
                    for n in range(heads):
                        for h in range(2):
                            v.scalar_tensor_tensor(m[0:HH, n, h, :], seg[0:HH, h, :], cc[0:HH, a, h, n:n + 1],
                                                   m[0:HH, n, h, :], ALU.add, ALU.max)
                dve.drain()
                v.tensor_tensor(lt[0:HH, 0:heads], lt[0:HH, 0:heads], m[0:HH], ALU.subtract)
                if with_self:
                    v.tensor_tensor(lt[0:HH, 1], lt[0:HH, 1], m[0:HH, 0], ALU.subtract)
                dve.drain().then_inc(diff.sem, 1)
                M = heads + with_self
                for h in range(2):
                    dve.wait_ge(*exp_turned.done(h + 1))
                    for n in range(M):
                        out = k.logits[:, n, :] if n < heads else k.selfs[:, :]
                        v.tensor_copy(out[:, 2 * HH * h:2 * HH * (h + 1)].rearrange("p (s j) -> p j s", j=2),
                                      pe_back[:, n, :, 0:HH])
                    dve.drain().then_inc(back.sem, 1)
                if with_self:
                    v.tensor_tensor(k.ends[:, :, 0], k.selfs[:, :], k.end_e[:, :], ALU.mult)
                    v.tensor_copy(k.ends[:, :, 1], k.end_e[:, :])
                    dve.drain()

            @block.scalar
            def _(act):
                act.wait_ge(*diff.done(1))
                nc.scalar.activation(lt[0:HH, 0:heads + with_self], lt[0:HH, 0:heads + with_self], ACT.Exp
                                     ).then_inc(exped.sem, 1)
        k.close(1, turned, local, ends, carried, carry_t, diff, exped)
        k.close(2, back, exp_turned)


def edge_sum_phase(nc, k, table, width, blocks, out_dram):
    size = sum(b[2] for b in blocks)
    banks = -(-size // 512)
    bw = size // banks
    weighted = [b for b in blocks if b[0] is not None]
    plain = [b for b in blocks if b[0] is None]
    on_dve = weighted[:1] if len(weighted) > 1 else []
    on_act = weighted[len(on_dve):]
    wide = sum(b[2] for b in weighted)
    ahead = 2
    with ExitStack() as ctx:
        def sb(name, shape, dt=F32):
            return ctx.enter_context(nc.sbuf_tensor(k.own(name), shape, dt))
        acc = sb("sums", [P, WINDOWS * size])
        sel = sb("selection", [P, U, 2, P])
        idx = sb("staged_src", [P, 2, 4], I32)
        rows = sb("src_rows", [P, U, 2, width])
        msg = sb("weighted_rows", [P, U, 2, wide])
        pO = [ctx.enter_context(nc.psum_tensor(k.own(f"window_sum{p}"), [P, banks, 512], F32)) for p in range(U)]
        staged, selected, weighed, summed, added, passed, act_passed = (k.count(n, a) for n, a in (
            ("src_staged", 0), ("selection_made", U), ("rows_weighed", U), ("window_summed", U), ("window_added", U),
            ("pool_passed", 0), ("act_passed", 0)))
        if table is not None:
            arrived = [k.count(f"rows_gathered{u}", 0, 32) for u in range(U)]
        else:
            arrived = [k.count(f"slot_rows_loaded{u}", 0, 16) for u in range(U)]
        sp_passed = k.count("sp_passed")
        readers = (selected, weighed) if on_dve else (weighed,)
        s_out = k.count("sums_stored", 0, 16)
        with nc.Block() as block:
            if table is not None:
                @block.gpsimd
                def _(pool):
                    gather_rows(nc, k, pool, idx, rows, width, table, staged, passed, readers, arrived)

            @block.scalar
            def _(act):
                act.sem_inc(weighed.sem, U)
                with act.Fori(0, ITERS) as i:
                    for u in range(U):
                        act.wait_ge(*arrived[u].done(i + 1))
                        act.wait_ge(*summed.free(U * i + u + 1, U))
                        act.sem_inc(act_passed.sem)
                        for j in range(2):
                            at = sum(b[2] for b in on_dve)
                            for weight, col, n in on_act:
                                last = nc.scalar.activation(msg[:, u, j, at:at + n], rows[:, u, j, col:col + n],
                                                            ACT.Copy, scale=weight[:, ds(U * 2 * i + 2 * u + j, 1)])
                                at += n
                        last.then_inc(weighed.sem, 1)

            @block.vector
            def _(dve):
                v = nc.vector
                v.memset(acc[:, :], 0.0)
                dve.sem_inc(selected.sem, U)
                dve.sem_inc(added.sem, U)

                def prepare(i, u):
                    dve.wait_ge(*summed.free(U * i + u + 1, U))
                    for j in range(2):
                        last = v.tensor_scalar(sel[:, u, j, :], k.iota_row[:, :],
                                               k.dloc_e[:, ds(U * 2 * i + 2 * u + j, 1)], None, ALU.is_equal)
                    if on_dve:
                        dve.wait_ge(*arrived[u].done(i + 1))
                        for j in range(2):
                            for weight, col, n in on_dve:
                                last = v.tensor_scalar(msg[:, u, j, 0:n], rows[:, u, j, col:col + n],
                                                       weight[:, ds(U * 2 * i + 2 * u + j, 1)], None, ALU.mult)
                    last.then_inc(selected.sem, 1)

                def add(i, u, win):
                    dve.drain()
                    dve.wait_ge(*summed.done(U * i + u + 1))
                    a = acc[:, ds(win[u] * size, size)].rearrange("p (b n) -> p b n", b=banks)
                    v.tensor_tensor(a, a, pO[u][:, :, 0:bw], ALU.add).then_inc(added.sem, 1)

                for u in range(ahead):
                    prepare(0, u)
                with dve.Fori(0, ITERS - 1) as i:
                    win = windows_of(dve, k, i)
                    for u in range(U):
                        prepare(i + (u + ahead) // U, (u + ahead) % U)
                        add(i, u, win)
                win = windows_of(dve, k, ITERS - 1)
                for u in range(U):
                    if u + ahead < U:
                        prepare(ITERS - 1, u + ahead)
                    add(ITERS - 1, u, win)

            @block.tensor
            def _(pe):
                pe.sem_inc(summed.sem, U)
                with pe.Fori(0, ITERS) as i:
                    for u in range(U):
                        pe.wait_ge(*selected.done(U * i + u + 1))
                        pe.wait_ge(*weighed.done(U * i + u + 1))
                        pe.wait_ge(*added.free(U * i + u + 1, U))
                        n = wide // banks
                        for b in range(banks):
                            for j in range(2):
                                last = nc.tensor.matmul(pO[u][:, b, 0:n], sel[:, u, j, :],
                                                        msg[:, u, j, b * n:(b + 1) * n],
                                                        start=(j == 0), stop=(j == 1))
                        at = wide
                        for _, values, n in plain:
                            for j in range(2):
                                last = nc.tensor.matmul(pO[u][:, 0, at:at + n], sel[:, u, j, :],
                                                        values[:, ds((U * 2 * i + 2 * u + j) * n, n)],
                                                        start=(j == 0), stop=(j == 1))
                            at += n
                        last.then_inc(summed.sem, 1)

            @block.sync
            def _(sp):
                if table is None:
                    with sp.Fori(0, ITERS) as i:
                        for u in range(U):
                            for c in readers:
                                sp.wait_ge(*c.free(U * i + u + 1, U))
                                sp.sem_inc(sp_passed.sem)
                            sp.dma_start(rows[:, u].rearrange("p j d -> p (j d)"),
                                         k.slots_dram[:, ds((U * i + u) * 2 * width, 2 * width)]
                                         ).then_inc(arrived[u].sem, 16)
                sp.wait_ge(*added.done(STEPS))
                sp.dma_start(out_dram[:, 0:WINDOWS * size], acc[:, :]).then_inc(s_out.sem, 16)
                sp.wait_ge(*s_out.done(1))
        k.close(STEPS, selected, summed, added, weighed, act_passed)
        if table is not None:
            k.close(2 * ITERS, staged, passed)
        k.close(ITERS, *arrived)
        k.close(1, s_out)


def conv_mid_phase(nc, k):
    H = HEADS
    with ExitStack() as ctx:
        def sb(name, shape, dt=F32):
            return ctx.enter_context(nc.sbuf_tensor(k.own(name), shape, dt))

        def pb(name, shape):
            return ctx.enter_context(nc.psum_tensor(k.own(name), shape, F32))
        wv = sb("wv0", [D, H, D])
        ws = sb("ws0", [D, H, D])
        bs = sb("bs0", [D, H])
        bv = sb("bv0_block", [H, H, D])
        w2 = sb("w_qkv1", [D, 3, H, HD])
        ws1 = sb("ws1", [D, H, D])
        b2 = sb("b_qkv1", [P, 3, HD])
        bs1 = sb("bs1", [P, D])
        agg = sb("agg", [P, CH, H, D + 1])
        den = sb("den", [P, CH, H])
        ratio = sb("ratio", [P, CH, H])
        ratioT = sb("ratioT", [H, CH, D])
        aggT = sb("aggT", [P, CH, D])
        hc = sb("h", [P, CH, D])
        hT = sb("hT", [P, CH, D])
        h1T = sb("h1T", [P, H, CH, D])
        work = k.logits[:, :, :].rearrange("p h t -> p (h t)")
        q = work[:, 0:HD]
        kk = work[:, HD:2 * HD]
        vv = work[:, 2 * HD:2 * HD + HW1].rearrange("p (h d) -> p h d", h=H)
        pA = pb("pA", [P, 8, D])
        pB = pb("pB", [P, 8, D])
        pX = [pb(f"pX{n}", [P, 512]) for n in range(4)]
        s_w = k.fresh("weights_conv2")
        s_bv = k.fresh("bias_block_cleared")
        names = ("agg_scaled", "aggT_ready", "aggT_made", "h1_product", "h1_made", "ratio_turned", "ratio_made")
        scaled, a_turned, aT_made, h1_prod, h1_made, r_turned, r_made = (k.count(n) for n in names)
        done = k.count("chunk_done", 1)
        agg_in = k.count("agg_loaded", 0, 16)
        prods = [k.count(f"proj{n}_product") for n in range(4)]
        used = [k.count(f"proj{n}_used", 1) for n in range(4)]
        stored = [k.count(f"{n}_rows_stored", 1, 16) for n in ("k", "v")]
        with nc.Block() as block:
            @block.sync
            def _(sp):
                with nc.allow_non_contiguous_dma(reason="small columns of biases"):
                    for out, src in (
                            (wv[:, :, :], k.L1_gnn_Wv0.rearrange("p (h n) -> p h n", n=D)),
                            (ws[:, :, :], k.L1_gnn_Ws0.rearrange("p (h n) -> p h n", n=D)),
                            (bs[:, :], k.L1_gnn_bs0.rearrange("(h p) -> p h", p=D)),
                            (ws1[:, :, :], k.L1_gnn_Ws1.rearrange("(c p) n -> p c n", p=D)),
                            (bs1[:, :], k.L1_gnn_bs1.rearrange("(o n) -> o n", o=1).partition_broadcast(P))):
                        sp.dma_start(out, src).then_inc(s_w, 16)
                    for n, (w, b) in enumerate(((k.L1_gnn_Wq1, k.L1_gnn_bq1), (k.L1_gnn_Wk1, k.L1_gnn_bk1),
                                                (k.L1_gnn_Wv1, k.L1_gnn_bv1))):
                        sp.dma_start(w2[:, n, :, :], w.rearrange("(c p) n -> p c n", p=D)).then_inc(s_w, 16)
                        sp.dma_start(b2[:, n, :], b.rearrange("(o n) -> o n", o=1).partition_broadcast(P)).then_inc(s_w, 16)
                    sp.wait_ge(s_bv, 1)
                    for h in range(H):
                        sp.dma_start(bv[h:h + 1, h, :], k.L1_gnn_bv0.rearrange("(h n) -> h n", n=D)[h:h + 1, :])\
                          .then_inc(s_w, 16)
                with sp.Fori(0, CHUNKS) as i:
                    sp.wait_ge(*done.free(i + 1, 1))
                    sp.dma_start(agg[:, :, :, :], k.sums_dram[:, ds(i * CH * HW1, CH * HW1)]).then_inc(agg_in.sem, 16)
                    for c in range(CH):
                        for n, (src, dram) in enumerate(((kk[:, :], k.k_dram), (vv[:, :, :], k.v_dram))):
                            sp.wait_ge(*used[1 + n].done(CH * i + c + 1))
                            sp.dma_start(dram[ds((i * CH + c) * P, P), :], src).then_inc(stored[n].sem, 16)
                for n in range(2):
                    sp.wait_ge(*stored[n].done(WINDOWS))

            @block.vector
            def _(dve):
                v = nc.vector
                v.memset(bv[:, :, :], 0.0).then_inc(s_bv, 1)
                v.memset(vv[:, :, D:D + 1], 1.0)
                dve.sem_inc(done.sem)
                for n in range(2):
                    dve.sem_inc(stored[n].sem, 16)
                for n in range(4):
                    dve.sem_inc(used[n].sem)
                dve.wait_ge(s_w, 16 * 15)
                with dve.Fori(0, CHUNKS) as i:
                    dve.wait_ge(*agg_in.done(i + 1))
                    v.tensor_copy(hc[:, :, :], chunk(k.H, i))
                    v.tensor_scalar(den[:, :, :], agg[:, :, :, D], 1.0e-16, None, ALU.add)
                    dve.drain()
                    v.reciprocal(den[:, :, :], den[:, :, :])
                    dve.drain()
                    v.tensor_tensor(ratio[:, :, :], agg[:, :, :, D], den[:, :, :], ALU.mult)
                    for h in range(H):
                        v.tensor_tensor(agg[:, :, h, 0:D], agg[:, :, h, 0:D],
                                        den[:, :, h:h + 1].broadcast_to([P, CH, D]), ALU.mult)
                    dve.drain().then_inc(scaled.sem, 1)
                    for c in range(CH):
                        dve.wait_ge(*prods[0].done(CH * i + c + 1))
                        v.tensor_tensor(q[:, :], pX[0][:, :], b2[:, 0, :], ALU.add)
                        dve.drain().then_inc(used[0].sem, 1)
                        part = [k.U[:, ds(i * (CH * 3 * HD) + (3 * c + n) * HD, HD)] for n in range(3)]
                        split3(dve, nc, q[:, :], *part, q[:, :])
                        dve.drain()
                        dve.wait_ge(*prods[1].done(CH * i + c + 1))
                        dve.wait_ge(*stored[0].free(CH * i + c + 1, 1))
                        v.tensor_tensor(kk[:, :], pX[1][:, :], b2[:, 1, :], ALU.add).then_inc(used[1].sem, 1)
                        dve.wait_ge(*prods[2].done(CH * i + c + 1))
                        dve.wait_ge(*stored[1].free(CH * i + c + 1, 1))
                        v.tensor_tensor(vv[:, :, 0:D], pX[2][:, :].rearrange("p (h d) -> p h d", h=H),
                                        b2[:, 2, :].rearrange("p (h d) -> p h d", h=H), ALU.add).then_inc(used[2].sem, 1)
                        dve.wait_ge(*prods[3].done(CH * i + c + 1))
                        v.tensor_tensor(k.G[:, ds(i * CH + c, 1), :].rearrange("p o d -> p (o d)"), pX[3][:, 0:D],
                                        bs1[:, :], ALU.add).then_inc(used[3].sem, 1)
                    dve.drain().then_inc(done.sem, 1)

            @block.scalar
            def _(act):
                s = nc.scalar
                act.wait_ge(s_w, 16 * 15)
                with act.Fori(0, CHUNKS) as i:
                    act.wait_ge(*a_turned.done(5 * i + 1))
                    s.copy(hT[:, :, :], pA[:, 0:CH, :]).then_inc(aT_made.sem, 1)
                    act.wait_ge(*r_turned.done(i + 1))
                    s.copy(ratioT[:, :, :], pB[0:H, 0:CH, :]).then_inc(r_made.sem, 1)
                    for h in range(H):
                        act.wait_ge(*a_turned.done(5 * i + h + 2))
                        s.copy(aggT[:, :, :], pA[:, 0:CH, :]).then_inc(aT_made.sem, 1)
                        act.wait_ge(*h1_prod.done(H * i + h + 1))
                        s.activation(h1T[:, h, :, :], pB[:, 0:CH, :], ACT.Relu, bias=bs[:, h:h + 1])\
                         .then_inc(h1_made.sem, 1)

            @block.tensor
            def _(pe):
                t = nc.tensor

                def wide(out, lhsT, rhs, start, stop):
                    t.matmul(out[:, 0:4, :], lhsT, rhs[:, 0:4, :], start=start, stop=stop)
                    return t.matmul(out[:, 4:CH, :], lhsT, rhs[:, 4:CH, :], start=start, stop=stop)
                pe.wait_ge(s_w, 16 * 15)
                with pe.Fori(0, CHUNKS) as i:
                    pe.wait_ge(*scaled.done(i + 1))
                    for c in range(CH):
                        last = t.transpose(pA[:, c, :], hc[:, c, :], k.ident[:, :])
                    last.then_inc(a_turned.sem, 1)
                    for c in range(CH):
                        last = t.matmul(pB[0:H, c, :], ratio[:, c, :], k.ident[:, :], start=True, stop=True)
                    last.then_inc(r_turned.sem, 1)
                    pe.wait_ge(*r_made.done(i + 1))
                    for h in range(H):
                        pe.wait_ge(*aT_made.done(5 * i + h + 1))
                        for c in range(CH):
                            last = t.transpose(pA[:, c, :], agg[:, c, h, 0:D], k.ident[:, :])
                        last.then_inc(a_turned.sem, 1)
                        pe.wait_ge(*aT_made.done(5 * i + h + 2))
                        wide(pB, wv[:, h, :], aggT, True, False)
                        wide(pB, ws[:, h, :], hT, False, False)
                        wide(pB, bv[:, h, :], ratioT, False, True).then_inc(h1_prod.sem, 1)
                        pe.wait_ge(*h1_made.done(H * i + h + 1))
                    for c in range(CH):
                        for n in range(4):
                            pe.wait_ge(*used[n].free(CH * i + c + 1, 1))
                            for kc in range(H):
                                rhs = w2[:, n, kc, :] if n < 3 else ws1[:, kc, :]
                                last = t.matmul(pX[n][:, 0:rhs.shape[1]], h1T[:, kc, c, :], rhs,
                                                start=(kc == 0), stop=(kc == H - 1))
                            last.then_inc(prods[n].sem, 1)
        k.close(CHUNKS, scaled, r_turned, r_made, agg_in, done)
        k.close(5 * CHUNKS, a_turned, aT_made)
        k.close(H * CHUNKS, h1_prod, h1_made)
        k.close(WINDOWS, *prods, *used, *stored)


def conv2_out_phase(nc, k):
    H = HEADS
    with ExitStack() as ctx:
        agg = ctx.enter_context(nc.sbuf_tensor(k.own("agg"), [P, CH, H, D + 1], F32))
        den = ctx.enter_context(nc.sbuf_tensor(k.own("den"), [P, CH, H], F32))
        agg_in, done = k.count("agg_loaded", 0, 16), k.count("chunk_done", 1)
        with nc.Block() as block:
            @block.sync
            def _(sp):
                with sp.Fori(0, CHUNKS) as i:
                    sp.wait_ge(*done.free(i + 1, 1))
                    sp.dma_start(agg[:, :, :, :], k.sums_dram[:, ds(i * CH * HW1, CH * HW1)]).then_inc(agg_in.sem, 16)

            @block.vector
            def _(dve):
                v = nc.vector
                dve.sem_inc(done.sem)
                with dve.Fori(0, CHUNKS) as i:
                    dve.wait_ge(*agg_in.done(i + 1))
                    v.tensor_scalar(den[:, :, :], agg[:, :, :, D], 1.0e-16, None, ALU.add)
                    dve.drain()
                    v.reciprocal(den[:, :, :], den[:, :, :])
                    dve.drain()
                    v.tensor_scalar(den[:, :, :], den[:, :, :], 1.0 / H, None, ALU.mult)
                    dve.drain()
                    for h in range(H):
                        v.tensor_tensor(agg[:, :, h, 0:D], agg[:, :, h, 0:D],
                                        den[:, :, h:h + 1].broadcast_to([P, CH, D]), ALU.mult)
                    dve.drain()
                    for a, b in ((0, 1), (2, 3), (0, 2)):
                        v.tensor_tensor(agg[:, :, a, 0:D], agg[:, :, a, 0:D], agg[:, :, b, 0:D], ALU.add)
                        dve.drain()
                    v.tensor_tensor(agg[:, :, 0, 0:D], agg[:, :, 0, 0:D], chunk(k.G, i), ALU.add)
                    dve.drain()
                    v.tensor_tensor(chunk(k.X, i), chunk(k.X, i), agg[:, :, 0, 0:D], ALU.add)
                    dve.drain().then_inc(done.sem, 1)
        k.close(CHUNKS, agg_in, done)


def gat_in_phase(nc, k):
    with ExitStack() as ctx:
        def sb(name, shape, dt=F32):
            return ctx.enter_context(nc.sbuf_tensor(k.own(name), shape, dt))

        def pb(name):
            return ctx.enter_context(nc.psum_tensor(k.own(name), [P, 8, D], F32))
        wl = sb("wl", [D, D])
        wr = sb("wr", [D, D])
        w = Scratch(nc, sb, "n3", k.eps5)
        h = sb("h", [P, CH, D])
        hT = sb("hT", [P, CH, D])
        xl = sb("xl", [P, CH, D + 4])
        xr = sb("xr", [P, CH, D + 1])
        m = sb("m", [P, CH, D])
        lk = sb("lk", [P, CH, D])
        rest = sb("rest", [P, CH, D + 1])
        pT, pL, pR = pb("pT"), pb("pL"), pb("pR")
        s_w = k.fresh("weights_gat")
        var, sd, h_made, turned, hT_made, prod, made = (k.count(n) for n in (
            "var_made", "sd_made", "h_made", "h_turned", "hT_made", "g_product", "g_made"))
        out = k.count("rows_stored_chunk", 1, 16)
        with nc.Block() as block:
            @block.sync
            def _(sp):
                sp.dma_start(wl[:, :], k.L2_gnn_W_l).then_inc(s_w, 16)
                sp.dma_start(wr[:, :], k.L2_gnn_W_r).then_inc(s_w, 16)
                sp.dma_start(k.att[:, :], k.L2_gnn_att.rearrange("(o n) -> o n", o=1).partition_broadcast(P)).then_inc(s_w, 16)
                with sp.Fori(0, CHUNKS) as i:
                    sp.wait_ge(*made.done(i + 1))
                    sp.dma_start(rows_of(k.h_dram, i, D + 4), xl[:, :, :]).then_inc(out.sem, 16)
                sp.wait_ge(*out.done(CHUNKS))

            @block.vector
            def _(dve):
                v = nc.vector
                dve.wait_ge(s_w, 48)
                dve.sem_inc(out.sem, 16)
                v.memset(xl[:, :, D:D + 4], 1.0)
                with dve.Fori(0, CHUNKS) as i:
                    norm_head(dve, chunk(k.X, i), w, var)
                    norm_tail(dve, w, h[:, :, :], sd, i + 1)
                    v.tensor_scalar(h[:, :, :], h[:, :, :], 0.0, None, ALU.max).then_inc(h_made.sem, 1)
                    dve.wait_ge(*prod.done(i + 1))
                    dve.wait_ge(*out.free(i + 1, 1))
                    v.tensor_copy(xl[:, :, 0:D], pL[:, 0:CH, :])
                    v.tensor_copy(xr[:, :, 0:D], pR[:, 0:CH, :])
                    dve.drain().then_inc(made.sem, 1)
                    v.tensor_copy(chunk(k.H, i), xl[:, :, 0:D])
                    v.tensor_tensor(m[:, :, :], xl[:, :, 0:D], xr[:, :, 0:D], ALU.add)
                    dve.drain()
                    v.scalar_tensor_tensor(lk[:, :, :], m[:, :, :], 0.2, m[:, :, :], ALU.mult, ALU.max)
                    dve.drain()
                    v.tensor_tensor(m[:, :, :], lk[:, :, :], over_rows(k.att[:, :]), ALU.mult)
                    dve.drain()
                    v.tensor_reduce(xr[:, :, D], m[:, :, :], AXX, ALU.add)
                    dve.drain()
                    u = k.U[:, ds(i * (CH * 3 * (D + 1)), CH * 3 * (D + 1))].rearrange("p (c n d) -> p c n d", c=CH, n=3)
                    split3(dve, nc, xr[:, :, :], u[:, :, 0, :], u[:, :, 1, :], u[:, :, 2, :], rest[:, :, :])
                    dve.drain()

            @block.scalar
            def _(act):
                with act.Fori(0, CHUNKS) as i:
                    norm_sqrt(act, nc, w, var, sd, i + 1)
                    act.wait_ge(*turned.done(i + 1))
                    nc.scalar.copy(hT[:, :, :], pT[:, 0:CH, :]).then_inc(hT_made.sem, 1)

            @block.tensor
            def _(pe):
                pe.wait_ge(s_w, 48)
                with pe.Fori(0, CHUNKS) as i:
                    pe.wait_ge(*h_made.done(i + 1))
                    for c in range(CH):
                        last = nc.tensor.transpose(pT[:, c, :], h[:, c, :], k.ident[:, :])
                    last.then_inc(turned.sem, 1)
                    pe.wait_ge(*hT_made.done(i + 1))
                    for c in range(CH):
                        nc.tensor.matmul(pL[:, c, :], hT[:, c, :], wl[:, :], start=True, stop=True)
                        last = nc.tensor.matmul(pR[:, c, :], hT[:, c, :], wr[:, :], start=True, stop=True)
                    last.then_inc(prod.sem, 1)
        k.close(CHUNKS, var, sd, h_made, turned, hT_made, prod, made, out)


def gat_out_phase(nc, k):
    S = D + 3
    with ExitStack() as ctx:
        def sb(name, shape, dt=F32):
            return ctx.enter_context(nc.sbuf_tensor(k.own(name), shape, dt))
        sums = sb("sums_gat", [P, WINDOWS, S])
        bc = sb("rows_bc", [P, 3, D])
        own = sb("own", [P, WINDOWS])
        den = sb("den", [P, WINDOWS])
        o = sb("o", [P, WINDOWS, D])
        t = sb("t", [P, WINDOWS, D])
        part = sb("part", [P, WINDOWS])
        tot = sb("tot", [P, 1])
        valid = sb("valid", [P, 1])
        ones = sb("ones", [P, P])
        mu = sb("mu", [P, 1])
        sd = sb("sd_all", [P, 1])
        pS = ctx.enter_context(nc.psum_tensor(k.own("pS"), [P, 512], F32))
        s_in = k.fresh("gat_out_loaded")
        s_part = k.fresh("partition_sums")
        s_all = k.fresh("whole_sums")
        s_sd = k.fresh("whole_sd")
        over = lambda row: row.unsqueeze(1).broadcast_to([P, WINDOWS, D])
        each = lambda col: col.unsqueeze(2).broadcast_to([P, WINDOWS, D])
        with nc.Block() as block:
            @block.sync
            def _(sp):
                sp.dma_start(sums[:, :, :], k.sums_dram[:, 0:WINDOWS * S]).then_inc(s_in, 16)
                for n, row in enumerate((k.L2_gnn_bias, k.L2_gnn_ln_w, k.L2_gnn_ln_b)):
                    sp.dma_start(bc[:, n, :], row.rearrange("(o n) -> o n", o=1).partition_broadcast(P)).then_inc(s_in, 16)

            @block.vector
            def _(dve):
                v = nc.vector

                def total(src, value):
                    v.tensor_reduce(part[:, :], src, AXX, ALU.add)
                    dve.drain()
                    v.tensor_tensor(part[:, WINDOWS - 1:WINDOWS], part[:, WINDOWS - 1:WINDOWS], valid[:, :], ALU.mult)
                    dve.drain()
                    v.tensor_reduce(tot[:, :], part[:, :], AXX, ALU.add).then_inc(s_part, 1)
                    dve.wait_ge(s_all, value)
                v.memset(ones[:, :], 1.0)
                v.tensor_scalar(valid[:, :], k.iota_p[:, :], float(LAST), None, ALU.is_lt)
                dve.wait_ge(s_in, 64)
                v.tensor_scalar(own[:, :], sums[:, :, D + 2], -1.0, 1.0, ALU.mult, ALU.add)
                dve.drain()
                v.tensor_tensor(own[:, :], own[:, :], sums[:, :, D + 1], ALU.add)
                dve.drain()
                v.tensor_tensor(den[:, :], own[:, :], sums[:, :, D], ALU.add)
                v.tensor_tensor(t[:, :, :], k.H[:, :, :], each(own[:, :]), ALU.mult)
                dve.drain()
                v.reciprocal(den[:, :], den[:, :])
                v.tensor_tensor(t[:, :, :], t[:, :, :], sums[:, :, 0:D], ALU.add)
                dve.drain()
                v.tensor_tensor(t[:, :, :], t[:, :, :], each(den[:, :]), ALU.mult)
                dve.drain()
                v.tensor_tensor(t[:, :, :], t[:, :, :], over(bc[:, 0, :]), ALU.add)
                dve.drain()
                v.scalar_tensor_tensor(o[:, :, :], t[:, :, :], 0.01, t[:, :, :], ALU.mult, ALU.max)
                dve.drain()
                total(o[:, :, :], 1)
                v.tensor_scalar(mu[:, :], pS[:, 0:1], 1.0 / (NODES * D), None, ALU.mult)
                dve.drain()
                v.tensor_scalar(o[:, :, :], o[:, :, :], mu[:, 0:1], None, ALU.subtract)
                dve.drain()
                v.tensor_tensor(t[:, :, :], o[:, :, :], o[:, :, :], ALU.mult)
                dve.drain()
                total(t[:, :, :], 2)
                dve.wait_ge(s_sd, 1)
                v.tensor_scalar(sd[:, :], sd[:, :], 1.0e-5, None, ALU.add)
                dve.drain()
                v.reciprocal(sd[:, :], sd[:, :])
                dve.drain()
                v.scalar_tensor_tensor(t[:, :, :], o[:, :, :], sd[:, 0:1], over(bc[:, 1, :]), ALU.mult, ALU.mult)
                dve.drain()
                v.tensor_tensor(t[:, :, :], t[:, :, :], over(bc[:, 2, :]), ALU.add)
                dve.drain()
                v.tensor_tensor(k.X[:, :, :], k.X[:, :, :], t[:, :, :], ALU.add)
                dve.drain()

            @block.tensor
            def _(pe):
                for n in range(2):
                    pe.wait_ge(s_part, n + 1)
                    nc.tensor.matmul(pS[:, n:n + 1], ones[:, :], tot[:, :], start=True, stop=True).then_inc(s_all, 1)

            @block.scalar
            def _(act):
                act.wait_ge(s_all, 2)
                nc.scalar.activation(sd[:, :], pS[:, 1:2], ACT.Sqrt, scale=1.0 / (NODES * D)).then_inc(s_sd, 1)


def last_in_phase(nc, k):
    with ExitStack() as ctx:
        def sb(name, shape, dt=F32):
            return ctx.enter_context(nc.sbuf_tensor(k.own(name), shape, dt))

        def pb(name):
            return ctx.enter_context(nc.psum_tensor(k.own(name), [P, 8, D], F32))
        w3 = sb("w3", [D, D])
        w3T = sb("w3T", [D, D])
        bc = sb("rows_bc", [P, 3, D])
        w = Scratch(nc, sb, "n4", k.eps5)
        h = sb("h", [P, CH, D])
        hT = sb("hT", [P, CH, D])
        tt = sb("tt", [P, CH, D])
        m = sb("m", [P, CH, 2, D])
        vals = sb("vals", [P, CH, 2])
        rest = sb("rest", [P, CH])
        pT, pL = pb("pT"), pb("pL")
        s_w = k.fresh("weights_last")
        s_t = k.fresh("w3_turned")
        s_wT = k.fresh("w3T_made")
        var, sd, h_made, turned, hT_made, prod = (k.count(n) for n in (
            "var_made", "sd_made", "h_made", "h_turned", "hT_made", "g_product"))
        with nc.Block() as block:
            @block.sync
            def _(sp):
                sp.dma_start(w3[:, :], k.L3_gnn_W).then_inc(s_w, 16)
                for n, row in enumerate((k.L3_gnn_b.rearrange("(o n) -> o n", o=1), k.L3_gnn_att_w[:, 0:D],
                                         k.L3_gnn_att_w[:, D:2 * D])):
                    sp.dma_start(bc[:, n, :], row.partition_broadcast(P)).then_inc(s_w, 16)

            @block.vector
            def _(dve):
                v = nc.vector
                dve.wait_ge(s_t, 1)
                v.tensor_copy(w3T[:, :], pT[:, 0, :]).then_inc(s_wT, 1)
                with dve.Fori(0, CHUNKS) as i:
                    norm_head(dve, chunk(k.X, i), w, var)
                    norm_tail(dve, w, h[:, :, :], sd, i + 1)
                    v.tensor_scalar(h[:, :, :], h[:, :, :], 0.0, None, ALU.max).then_inc(h_made.sem, 1)
                    dve.drain()
                    v.tensor_copy(chunk(k.H, i), h[:, :, :])
                    dve.wait_ge(*prod.done(i + 1))
                    v.tensor_tensor(tt[:, :, :], pL[:, 0:CH, :], over_rows(bc[:, 0, :]), ALU.add)
                    dve.drain()
                    for n in range(2):
                        v.tensor_tensor(m[:, :, n, :], tt[:, :, :], over_rows(bc[:, 1 + n, :]), ALU.mult)
                    dve.drain()
                    v.tensor_reduce(vals[:, :, :], m[:, :, :, :], AXX, ALU.add)
                    dve.drain()
                    split3(dve, nc, vals[:, :, 0], *(k.V[:, n, ds(i * CH, CH)] for n in range(3)), rest[:, :])
                    dve.drain()
                    u = k.U[:, ds(i * (CH * 3), CH * 3)].rearrange("p (c n) -> p c n", c=CH)
                    split3(dve, nc, vals[:, :, 1], u[:, :, 0], u[:, :, 1], u[:, :, 2], rest[:, :])
                    dve.drain()

            @block.scalar
            def _(act):
                with act.Fori(0, CHUNKS) as i:
                    norm_sqrt(act, nc, w, var, sd, i + 1)
                    act.wait_ge(*turned.done(i + 1))
                    nc.scalar.copy(hT[:, :, :], pT[:, 0:CH, :]).then_inc(hT_made.sem, 1)

            @block.tensor
            def _(pe):
                pe.wait_ge(s_w, 64)
                nc.tensor.transpose(pT[:, 0, :], w3[:, :], k.ident[:, :]).then_inc(s_t, 1)
                pe.wait_ge(s_wT, 1)
                with pe.Fori(0, CHUNKS) as i:
                    pe.wait_ge(*h_made.done(i + 1))
                    for c in range(CH):
                        last = nc.tensor.transpose(pT[:, c, :], h[:, c, :], k.ident[:, :])
                    last.then_inc(turned.sem, 1)
                    pe.wait_ge(*hT_made.done(i + 1))
                    for c in range(CH):
                        last = nc.tensor.matmul(pL[:, c, :], hT[:, c, :], w3T[:, :], start=True, stop=True)
                    last.then_inc(prod.sem, 1)
        k.close(CHUNKS, var, sd, h_made, turned, hT_made, prod)


CAP = 1.0e36
TINY = 1.1754944e-38
SHRINK = 2.0 ** -30


def last_weights_phase(nc, k):
    with ExitStack() as ctx:
        a = ctx.enter_context(nc.sbuf_tensor(k.own("leaky"), [P, TILES], F32))
        z = ctx.enter_context(nc.sbuf_tensor(k.own("normal"), [P, TILES], F32))
        s_l = k.fresh("leaky_made")
        s_e = k.fresh("weights_made")
        with nc.Block() as block:
            @block.vector
            def _(dve):
                v = nc.vector
                lg = k.logits[:, 0, :]
                v.scalar_tensor_tensor(a[:, :], lg, 0.2, lg, ALU.mult, ALU.max)
                dve.drain()
                v.tensor_scalar(a[:, :], a[:, :], 88.0, -100.0, ALU.min, ALU.max).then_inc(s_l, 1)
                dve.wait_ge(s_e, 1)
                v.tensor_scalar(z[:, :], a[:, :], TINY, None, ALU.is_ge)
                v.tensor_scalar(a[:, :], a[:, :], CAP, None, ALU.min)
                dve.drain()
                v.tensor_tensor(a[:, :], a[:, :], z[:, :], ALU.mult)
                dve.drain()
                split3(dve, nc, a[:, :], k.parts[:, :, 0], k.parts[:, :, 1], k.parts[:, :, 2], a[:, :])
                dve.drain()

            @block.scalar
            def _(act):
                act.wait_ge(s_l, 1)
                nc.scalar.activation(a[:, :], a[:, :], ACT.Exp).then_inc(s_e, 1)


def last_out_phase(nc, k, out):
    with ExitStack() as ctx:
        def sb(name, shape, dt=F32):
            return ctx.enter_context(nc.sbuf_tensor(k.own(name), shape, dt))
        n = sb("n_sum", [P, WINDOWS])
        z = sb("n_zero", [P, WINDOWS])
        y = sb("y", [P, WINDOWS, D])
        t = sb("t", [P, WINDOWS, D])
        ms = sb("ms", [P, WINDOWS])
        ok = sb("ok", [P, WINDOWS])
        sd = sb("sd_last", [P, WINDOWS])
        bc = sb("rows_bc", [P, 2, D])
        s_in = k.fresh("last_loaded_sums")
        s_ms = k.fresh("mean_square_made")
        s_sd = k.fresh("rms_made")
        s_y = k.fresh("result_made")
        s_out = k.fresh("result_stored")
        over = lambda row: row.unsqueeze(1).broadcast_to([P, WINDOWS, D])
        each = lambda col: col.unsqueeze(2).broadcast_to([P, WINDOWS, D])
        with nc.Block() as block:
            @block.sync
            def _(sp):
                for j, row in enumerate((k.L3_gnn_norm_w, k.L3_gnn_norm_b)):
                    sp.dma_start(bc[:, j, :], row.rearrange("(o n) -> o n", o=1).partition_broadcast(P)).then_inc(s_in, 16)
                sp.wait_ge(s_y, 1)
                sp.dma_start(out[0:(WINDOWS - 1) * P, :].rearrange("(w p) d -> p w d", p=P), y[:, 0:WINDOWS - 1, :])\
                  .then_inc(s_out, 16)
                sp.dma_start(out[(WINDOWS - 1) * P:NODES, :], y[0:LAST, WINDOWS - 1, :]).then_inc(s_out, 16)
                sp.wait_ge(s_out, 32)

            @block.vector
            def _(dve):
                v = nc.vector
                dve.wait_ge(s_in, 32)
                v.tensor_scalar(z[:, :], k.node_sums[:, :], 0.0, None, ALU.is_equal)
                v.tensor_scalar(n[:, :], k.node_sums[:, :], CAP, None, ALU.min)
                dve.drain()
                v.tensor_tensor(n[:, :], n[:, :], z[:, :], ALU.add)
                dve.drain()
                v.reciprocal(n[:, :], n[:, :])
                dve.drain()
                v.tensor_scalar(n[:, :], n[:, :], SHRINK, None, ALU.mult)
                v.tensor_scalar(y[:, :, :], k.H[:, :, :], SHRINK, None, ALU.mult)
                dve.drain()
                v.tensor_tensor(t[:, :, :], k.H[:, :, :], each(n[:, :]), ALU.mult)
                dve.drain()
                v.scalar_tensor_tensor(t[:, :, :], t[:, :, :], 0.0, y[:, :, :], ALU.max, ALU.add)
                dve.drain()
                v.tensor_scalar(y[:, :, :], t[:, :, :], 1.0e15, None, ALU.min)
                dve.drain()
                v.tensor_tensor(t[:, :, :], y[:, :, :], y[:, :, :], ALU.mult)
                dve.drain()
                v.tensor_reduce(ms[:, :], t[:, :, :], AXX, ALU.add)
                dve.drain()
                v.tensor_scalar(ok[:, :], ms[:, :], 3.4028235e38 * SHRINK * SHRINK, None, ALU.is_le)
                v.tensor_scalar(sd[:, :], ms[:, :], 1.0 / D, 1.0e-6 * SHRINK * SHRINK, ALU.mult, ALU.add)
                dve.drain().then_inc(s_ms, 1)
                dve.wait_ge(s_sd, 1)
                v.reciprocal(sd[:, :], sd[:, :])
                dve.drain()
                v.tensor_tensor(sd[:, :], sd[:, :], ok[:, :], ALU.mult)
                dve.drain()
                v.tensor_tensor(y[:, :, :], y[:, :, :], each(sd[:, :]), ALU.mult)
                dve.drain()
                v.tensor_tensor(y[:, :, :], y[:, :, :], over(bc[:, 0, :]), ALU.mult)
                dve.drain()
                v.tensor_tensor(y[:, :, :], y[:, :, :], over(bc[:, 1, :]), ALU.add)
                dve.drain()
                v.tensor_tensor(y[:, :, :], y[:, :, :], k.X[:, :, :], ALU.add).then_inc(s_y, 1)

            @block.scalar
            def _(act):
                act.wait_ge(s_ms, 1)
                nc.scalar.activation(sd[:, :], sd[:, :], ACT.Sqrt).then_inc(s_sd, 1)


def program(nc, arrays, out):
    with ExitStack() as ctx:
        k = Shared(nc, ctx, arrays)

        def sbuf(name, shape, dt=F32):
            return nc.sbuf_tensor(name, shape, dt)

        def sb(name, shape, dt=F32):
            return ctx.enter_context(sbuf(name, shape, dt))

        def dram(name, shape, dt=F32):
            return nc.dram_tensor(name, shape, dt).ap()
        k.ones_row = sb("ones_row", [1, P])
        k.ident = sb("ident", [P, P])
        k.iota_row = sb("iota_row", [P, P])
        k.iota_p = sb("iota_p", [P, 1])
        k.eps5 = sb("eps5", [P, 1])
        k.mask_t = sb("mask_t", [P, 2, GROUP + 1])
        k.first_t = sb("first_t", [P, 2, GROUP])
        k.last_t = sb("last_t", [P, 2, GROUP])
        k.step_masks = sb("step_masks", [HEADS, 4, STEPS])
        k.dloc_e = sb("dloc_e", [P, TILES])
        k.end_e = sb("end_e", [P, TILES])
        k.src_e = sb("src_e", [P, TILES], I32)
        k.win_hot = sb("win_hot", [P, 2, WINDOWS])
        k.win = sb("win", [1, ITERS], I32)
        k.X = sb("X", [P, WINDOWS, D])
        k.H = sb("H", [P, WINDOWS, D])
        k.G = sb("G", [P, WINDOWS, D])
        k.att = sb("att", [P, D])
        k.dloc_dram = dram("dloc_dram", [STEPS, GROUP], BF16)
        k.lo_dram = dram("lo_dram", [STEPS, GROUP], BF16)
        k.mask_dram = dram("mask_dram", [STEPS, GROUP], BF16)
        k.hot_dram = dram("hot_dram", [P, STEPS * GROUP], BF16)
        k.slots_dram = dram("slots_dram", [P, TILES * (D + 4)])
        k.g_dram = dram("g_dram", [ROWS, D])
        k.h_dram = dram("h_dram", [ROWS, D + 4])
        k.k_dram = dram("k_dram", [ROWS, HD])
        k.v_dram = dram("v_dram", [ROWS, HW1])
        k.sums_dram = dram("sums_dram", [P, WINDOWS * HW1])
        graph_phase(nc, k)
        load_phase(nc, k)

        edge_conv_in_phase(nc, k)
        with sbuf("acc", [P, WINDOWS * (D + 1)]) as k.acc:
            edge_max_phase(nc, k)
            edge_conv_out_phase(nc, k)

        with sbuf("logits_conv", [P, HEADS, TILES]) as k.logits:
            with sbuf("u_table", [P, WINDOWS * 3 * HW1], BF16) as k.U:
                conv1_in_phase(nc, k)
                edge_logits_phase(nc, k, k.h_dram, D + 4, False, HW1, keep=True)
            segment_softmax_phase(nc, k, HEADS, float(D) ** -0.5)
            edge_sum_phase(nc, k, None, D + 4, [(k.logits[:, h, :], 0, D + 1) for h in range(HEADS)],
                           k.sums_dram)
            with sbuf("q_table", [P, WINDOWS * 3 * HD], BF16) as k.U:
                conv_mid_phase(nc, k)
                edge_logits_phase(nc, k, k.k_dram, HD, True, HD)
            segment_softmax_phase(nc, k, HEADS, float(D) ** -0.5)
            edge_sum_phase(nc, k, k.v_dram, HW1, [(k.logits[:, h, :], h * (D + 1), D + 1) for h in range(HEADS)],
                           k.sums_dram)
            conv2_out_phase(nc, k)

        k.logits, k.selfs, k.ends = sb("logits3", [P, 1, TILES]), sb("selfs", [P, TILES]), sb("ends", [P, TILES, 2])
        with sbuf("r_table", [P, WINDOWS * 3 * (D + 1)], BF16) as k.U:
            gat_in_phase(nc, k)
            edge_logits_phase(nc, k, k.h_dram, D + 4, False, D + 1, gat=True, keep=True)
        segment_softmax_phase(nc, k, 1, 1.0, with_self=True)
        edge_sum_phase(nc, k, None, D + 4, [(k.logits[:, 0, :], 0, D + 1),
                                                (None, k.ends[:, :, :].rearrange("p t n -> p (t n)"), 2)], k.sums_dram)
        gat_out_phase(nc, k)

        k.parts = sb("parts", [P, TILES, 3], BF16)
        k.node_sums = sb("node_sums", [P, WINDOWS])
        with sbuf("s_table", [P, WINDOWS * 3], BF16) as k.U, sbuf("v_table", [P, 3, WINDOWS], BF16) as k.V:
            last_in_phase(nc, k)
            value_logits_phase(nc, k)
        last_weights_phase(nc, k)
        value_sums_phase(nc, k)
        last_out_phase(nc, k, out)


def kernel(**inputs):
    import numpy as _np
    import concourse.bacc as _bacc
    from concourse import mybir as _mybir
    from concourse.bass_utils import run_bass_kernel_spmd as _run

    nc = _bacc.Bacc("TRN2", target_bir_lowering=False, num_devices=1)
    host = {n: _np.ascontiguousarray(v) for n, v in inputs.items()}
    pad = SLOTS - EDGES
    host["src"] = _np.concatenate([host["src"], _np.zeros(pad, host["src"].dtype)])
    host["dst"] = _np.concatenate([host["dst"], _np.full(pad, ROWS - 1, host["dst"].dtype)])
    arrays = {f"in_{n}": a for n, a in host.items()}
    aps = {n: nc.dram_tensor(f"in_{n}", a.shape, _mybir.dt.from_np(a.dtype), kind="ExternalInput").ap()
           for n, a in host.items()}
    out = nc.dram_tensor("out_0", [NODES, D], _mybir.dt.float32, kind="ExternalOutput").ap()
    program(nc, aps, out)
    r = _run(nc, [arrays], core_ids=[0])
    return r.results[0]["out_0"]
```

```python
import numpy as np
import concourse.bass as bass
from concourse import mybir
from contextlib import ExitStack

F32, I32, BF16 = mybir.dt.float32, mybir.dt.int32, mybir.dt.bfloat16
ALU = mybir.AluOpType
ACT = mybir.ActivationFunctionType
AXX = mybir.AxisListType.X

NODES, EDGES, D = 3125, 50000, 128
HEADS = 4
FFN = 4 * D
HD = HEADS * D
HW1 = HEADS * (D + 1)
P = 128
WINDOWS = -(-NODES // P)
ROWS = WINDOWS * P
LAST = NODES - (WINDOWS - 1) * P
GROUP = 256
GROUPS = -(-EDGES // GROUP)
SLOTS = GROUPS * GROUP
STEPS = GROUPS + WINDOWS - 1
HALF = STEPS // 2
TILES = 2 * STEPS
U = 4
ITERS = STEPS // U
WBITS = 5
REPEAT = 5
CH = 5
CHUNKS = WINDOWS // CH
BIG = 1.0e30
ds = bass.ds


class Count:

    def __init__(self, sem, ahead, unit):
        self.sem, self.ahead, self.unit, self.base = sem, ahead, unit, 0

    def done(self, n):
        return self.sem, n * self.unit + (self.base + self.ahead * self.unit)

    def free(self, n, depth):
        return self.sem, n * self.unit + (self.base + (self.ahead - depth) * self.unit)


def repeat(eng, count, times, body):
    with eng.Fori(0, count // times) as n:
        for r in range(times):
            body(n * times + r)
    for i in range(count // times * times, count):
        body(i)


def windows_of(eng, k, i):
    packed = eng.value_load(k.win[0:1, ds(i, 1)], min_val=0, max_val=(1 << (U * WBITS)) - 1)
    return [((packed >> (u * WBITS)) & ((1 << WBITS) - 1)).with_bounds(min_val=0, max_val=WINDOWS - 1) for u in range(U)]


def graph_phase(nc, k):
    with ExitStack() as ctx:
        def sb(name, shape, dt=F32):
            return ctx.enter_context(nc.sbuf_tensor(k.own(name), shape, dt))

        def pb(name, shape):
            return ctx.enter_context(nc.psum_tensor(k.own(name), shape, F32))

        def sem(name):
            return ctx.enter_context(nc.semaphore(k.own(name)))

        last_i = sb("last_i", [1, GROUPS], I32)
        lastw_i = sb("lastw_i", [1, GROUPS], I32)
        lastw = sb("lastw", [1, GROUPS])
        grp_i = sb("grp_i", [1, GROUPS], I32)
        grp = sb("grp", [1, GROUPS])
        key = sb("key", [1, GROUPS])
        step_col = sb("step_col", [P, 2])
        hits = sb("hits", [P, GROUPS])
        gcol = sb("gcol", [P, 2])
        gcol_i = sb("gcol_i", [P, 2], I32)
        wcol = sb("wcol", [P, 2])
        base = sb("base", [P, 2])
        it_i = sb("it_i", [P, P], I32)
        ip_i = sb("ip_i", [P, 1], I32)
        dst_i = sb("dst_i", [P, 2, GROUP], I32)
        src_i = sb("src_i", [P, 2, GROUP], I32)
        dst = sb("dst", [P, 2, GROUP])
        srcf = sb("srcf", [P, 2, GROUP])
        lo_i = sb("lo_i", [P, 2, GROUP], I32)
        lo_b = sb("lo_b", [P, 2, GROUP], BF16)
        dloc = sb("dloc", [P, 2, GROUP])
        dloc_b = sb("dloc_b", [P, 2, GROUP], BF16)
        same = sb("same", [P, 2, GROUP])
        end = sb("end", [P, 2, GROUP])
        mask_b = sb("mask_b", [P, 2, GROUP], BF16)
        rows = sb("rows", [1, 2, STEPS])
        cont = sb("cont", [1, STEPS + 1])
        whole = sb("whole", [1, STEPS])
        mrows = sb("mrows", [1, 4, STEPS])
        wpack = sb("packed_windows", [1, ITERS])
        cont_c = sb("cont_c", [P, 2, 2])

        pa = pb("pa", [P, 512])
        pc = pb("pc", [P, 512])
        pd = pb("pd", [P, 12, P])

        s_last = sem("last_loaded")
        s_iota = sem("iotas_made")
        s_const = sem("consts_made")
        s_key = sem("key_made")
        s_keyb = sem("key_broadcast")
        s_g = sem("group_index_made")
        s_edges = sem("edges_gathered")
        s_winrow = sem("window_row_made")
        s_dst = sem("dst_floats_made")
        s_rows = sem("first_last_rows")
        s_mrow = sem("mask_rows_made")
        s_mrowb = sem("mask_rows_spread")
        s_end = sem("end_flags_made")
        s_cols = sem("edge_major_made")
        s_stored = sem("rows_stored")
        s_pad = sem("x_padding_cleared")
        s_x = sem("x_loaded")

        block = ctx.enter_context(nc.Block())

        @block.sync
        def _(sp):
            with nc.allow_non_contiguous_dma(reason="one value of each group"):
                sp.dma_start(last_i[:, :], k.dst.rearrange("(o g e) -> o g e", o=1, e=GROUP)[:, :, GROUP - 1])\
                  .then_inc(s_last, 16)
            sp.dma_start(k.X[:, 0:WINDOWS - 1, :], k.x[0:(WINDOWS - 1) * P, :].rearrange("(w p) d -> p w d", p=P))\
              .then_inc(s_x, 16)
            sp.wait_ge(s_pad, 1)
            sp.dma_start(k.X[0:LAST, WINDOWS - 1, :], k.x[(WINDOWS - 1) * P:NODES, :]).then_inc(s_x, 16)
            sp.wait_ge(s_end, 1)
            for h in range(2):
                sp.dma_start(k.dloc_dram[h * HALF:(h + 1) * HALF, :], dloc_b[0:HALF, h, :]).then_inc(s_stored, 16)
                sp.dma_start(k.mask_dram[h * HALF:(h + 1) * HALF, :], mask_b[0:HALF, h, :]).then_inc(s_stored, 16)
                sp.dma_start(k.lo_dram[h * HALF:(h + 1) * HALF, :], lo_b[0:HALF, h, :]).then_inc(s_stored, 16)
            sp.wait_ge(s_stored, 96)
            sp.wait_ge(s_x, 32)

        @block.gpsimd
        def _(pool):
            nc.gpsimd.iota(it_i[:, :], [[1, P]], base=0, channel_multiplier=0)
            nc.gpsimd.iota(ip_i[:, :], [[1, 1]], base=0, channel_multiplier=1)
            nc.gpsimd.iota(grp_i[:, :], [[1, GROUPS]], base=0, channel_multiplier=0)
            nc.gpsimd.memset(k.ones_row[:, :], 1.0)
            nc.gpsimd.memset(k.ident[:, :], 0.0)
            pool.drain().then_inc(s_iota, 1)
            nc.gpsimd.affine_select(out=k.ident[:, :], in_=k.ident[:, :], compare_op=ALU.not_equal, fill=1.0,
                                    base=0, pattern=[[-1, P]], channel_multiplier=1).then_inc(s_const, 1)
            pool.wait_ge(s_g, 1)
            for h in range(2):
                for rows_i, table in ((dst_i, k.dst), (src_i, k.src)):
                    nc.gpsimd.indirect_dma_start(
                        rows_i[0:HALF, h, :], None, table.rearrange("(g e) -> g e", e=GROUP),
                        bass.IndirectOffsetOnAxis(ap=gcol_i[0:HALF, h:h + 1], axis=0)).then_inc(s_edges, 16)

        @block.vector
        def _(dve):
            v = nc.vector
            v.memset(k.X[:, WINDOWS - 1, :], 0.0).then_inc(s_pad, 1)
            v.memset(k.eps5[:, :], 1.0e-5)
            dve.wait_ge(s_last, 16)
            v.tensor_scalar(lastw_i[:, :], last_i[:, :], 7, None, ALU.arith_shift_right)
            dve.wait_ge(s_iota, 1)
            v.tensor_copy(k.iota_row[:, :], it_i[:, :])
            v.tensor_copy(k.iota_p[:, :], ip_i[:, :])
            v.tensor_copy(grp[:, :], grp_i[:, :])
            dve.drain()
            v.tensor_copy(lastw[:, :], lastw_i[:, :])
            v.tensor_copy(step_col[:, 0:1], k.iota_p[:, :])
            v.tensor_scalar(step_col[:, 1:2], k.iota_p[:, :], float(HALF), None, ALU.add)
            dve.drain()
            v.tensor_tensor(key[:, :], lastw[:, :], grp[:, :], ALU.add).then_inc(s_key, 1)
            dve.wait_ge(s_keyb, 1)
            for h in range(2):
                v.tensor_scalar(hits[:, :], pa[:, 0:GROUPS], step_col[:, h:h + 1], None, ALU.is_lt, ALU.add,
                                accum_out=gcol[:, h:h + 1])
                dve.drain()
            v.tensor_copy(gcol_i[:, :], gcol[:, :]).then_inc(s_g, 1)
            v.tensor_tensor(wcol[:, :], step_col[:, :], gcol[:, :], ALU.subtract)
            dve.drain()
            v.tensor_scalar(base[:, :], wcol[:, :], float(P), None, ALU.mult)
            dve.wait_ge(s_edges, 64)
            v.tensor_copy(dst[0:HALF], dst_i[0:HALF])
            v.tensor_copy(srcf[0:HALF], src_i[0:HALF])
            v.tensor_scalar(lo_i[0:HALF], src_i[0:HALF], P - 1, None, ALU.bitwise_and)
            for h in range(2):
                v.tensor_scalar(k.win_hot[:, h, :], k.iota_row[:, 0:WINDOWS], wcol[:, h:h + 1], None, ALU.is_equal)
            dve.drain().then_inc(s_dst, 1)
            for h in range(2):
                v.tensor_scalar(dloc[0:HALF, h, :], dst[0:HALF, h, :], base[0:HALF, h:h + 1], None, ALU.subtract)
            dve.drain()
            v.tensor_scalar(dloc[0:HALF], dloc[0:HALF], -1.0, float(P), ALU.max, ALU.min)
            v.tensor_tensor(same[0:HALF, :, 1:GROUP], dst[0:HALF, :, 1:GROUP], dst[0:HALF, :, 0:GROUP - 1],
                            ALU.is_equal)
            dve.drain()
            v.tensor_copy(dloc_b[0:HALF], dloc[0:HALF])
            v.tensor_copy(lo_b[0:HALF], lo_i[0:HALF])
            v.memset(k.mask_t[:, :, 0:1], -BIG)
            v.memset(k.mask_t[:, :, GROUP:GROUP + 1], -BIG)
            v.tensor_scalar(k.mask_t[0:HALF, :, 1:GROUP], same[0:HALF, :, 1:GROUP], -1.0, BIG, ALU.add, ALU.mult)
            v.tensor_scalar(end[0:HALF, :, 0:GROUP - 1], same[0:HALF, :, 1:GROUP], -1.0, 1.0, ALU.mult, ALU.add)
            for h in range(2):
                for out, c in ((k.first_t, 0), (k.last_t, GROUP - 1)):
                    v.tensor_scalar(out[0:HALF, h, :], dst[0:HALF, h, :], dst[0:HALF, h, c:c + 1], None, ALU.is_equal)
            dve.drain()
            for out in (k.first_t, k.last_t):
                v.tensor_scalar(out[0:HALF], out[0:HALF], -1.0, BIG, ALU.add, ALU.mult)
            v.tensor_copy(mask_b[0:HALF, :, 1:GROUP], k.mask_t[0:HALF, :, 1:GROUP])
            dve.wait_ge(s_rows, 1)
            v.tensor_copy(rows[:, :, :], pc[0:1, 0:2 * STEPS].rearrange("o (a s) -> o a s", a=2))
            v.memset(cont[:, :], 0.0)
            dve.drain()
            v.tensor_tensor(cont[:, 1:STEPS], rows[:, 0, 1:STEPS], rows[:, 1, 0:STEPS - 1], ALU.is_equal)
            v.tensor_tensor(whole[:, :], rows[:, 0, :], rows[:, 1, :], ALU.is_equal)
            dve.drain()
            v.tensor_tensor(mrows[:, 0, :], whole[:, :], cont[:, 0:STEPS], ALU.mult)
            v.tensor_tensor(mrows[:, 1, :], whole[:, :], cont[:, 1:STEPS + 1], ALU.mult)
            v.tensor_copy(mrows[:, 2, :], cont[:, 0:STEPS])
            v.tensor_copy(mrows[:, 3, :], cont[:, 1:STEPS + 1])
            dve.drain()
            v.tensor_scalar(mrows[:, :, :], mrows[:, :, :], -1.0, BIG, ALU.add, ALU.mult).then_inc(s_mrow, 1)
            dve.wait_ge(s_mrowb, 1)
            v.tensor_copy(cont_c[0:HALF, :, :], pc[0:HALF, 0:4].rearrange("p (a h) -> p a h", a=2))
            v.tensor_copy(k.step_masks[:, 0:2, :], pa[0:HEADS, 0:2 * STEPS].rearrange("o (a s) -> o a s", a=2))
            dve.wait_ge(s_mrowb, 2)
            v.tensor_copy(k.step_masks[:, 2:4, :], pd[0:HEADS, 0:4, :].rearrange("o a s -> o (a s)")[:, 0:2 * STEPS]
                          .rearrange("o (a s) -> o a s", a=2))
            dve.drain()
            for h in range(2):
                v.tensor_scalar(mask_b[0:HALF, h, 0:1], cont_c[0:HALF, 0, h:h + 1], -1.0, BIG, ALU.add, ALU.mult)
                v.tensor_scalar(end[0:HALF, h, GROUP - 1:GROUP], cont_c[0:HALF, 1, h:h + 1], -1.0, 1.0,
                                ALU.mult, ALU.add)
            dve.drain().then_inc(s_end, 1)
            dve.wait_ge(s_cols, 1)
            for n, out in enumerate((k.dloc_e, k.end_e, k.src_e)):
                for h in range(2):
                    for j in range(2):
                        v.tensor_copy(out[:, 2 * HALF * h + j:2 * HALF * (h + 1):2], pd[:, 4 * n + 2 * h + j, 0:HALF])
            dve.wait_ge(s_winrow, 1)
            winrow = pc[0:1, 8:8 + STEPS].rearrange("o (i u) -> o i u", u=U)
            v.tensor_copy(wpack[:, :], winrow[:, :, U - 1])
            for u in reversed(range(U - 1)):
                dve.drain()
                v.scalar_tensor_tensor(wpack[:, :], wpack[:, :], float(1 << WBITS), winrow[:, :, u], ALU.mult, ALU.add)
            dve.drain()
            v.tensor_copy(k.win[:, :], wpack[:, :])
            dve.drain()

        @block.tensor
        def _(pe):
            t = nc.tensor
            pe.wait_ge(s_const, 1)
            pe.wait_ge(s_key, 1)
            t.matmul(pa[:, 0:GROUPS], k.ones_row[:, :], key[:, :], start=True, stop=True).then_inc(s_keyb, 1)
            pe.wait_ge(s_dst, 1)
            for a, c in ((0, 0), (1, GROUP - 1)):
                for h in range(2):
                    last = t.matmul(pc[0:1, a * STEPS + h * HALF:a * STEPS + (h + 1) * HALF],
                                    dst[0:HALF, h, c:c + 1], k.ident[0:HALF, 0:HALF], start=True, stop=True)
            last.then_inc(s_rows, 1)
            pe.wait_ge(s_mrow, 1)
            for a in range(2):
                for h in range(2):
                    t.matmul(pc[0:HALF, 2 * a + h:2 * a + h + 1], cont[:, a + h * HALF:a + (h + 1) * HALF],
                             k.ones_row[0:1, 0:1], start=True, stop=True)
            t.matmul(pa[0:HEADS, 0:2 * STEPS], k.ones_row[0:1, 0:HEADS], mrows[:, 0:2, :],
                     start=True, stop=True).then_inc(s_mrowb, 1)
            pm = pd[:, 0:4, :].rearrange("o a s -> o (a s)")
            t.matmul(pm[0:HEADS, 0:2 * STEPS], k.ones_row[0:1, 0:HEADS], mrows[:, 2:4, :],
                     start=True, stop=True).then_inc(s_mrowb, 1)
            pe.wait_ge(s_end, 1)
            for n, tt in enumerate((dloc, end, srcf)):
                for h in range(2):
                    for j in range(2):
                        last = t.transpose(pd[:, 4 * n + 2 * h + j, 0:HALF], tt[0:HALF, h, j * P:(j + 1) * P],
                                           k.ident[0:HALF, 0:HALF])
            last.then_inc(s_cols, 1)
            for h in range(2):
                last = t.matmul(pc[0:1, 8 + h * HALF:8 + (h + 1) * HALF], wcol[0:HALF, h:h + 1],
                                k.ident[0:HALF, 0:HALF], start=True, stop=True)
            last.then_inc(s_winrow, 1)


class Shared:

    def __init__(self, nc, ctx, arrays):
        self.x = arrays["x"]
        self.src = arrays["src"]
        self.dst = arrays["dst"]
        self.L0_gnn_W_in_b = arrays["L0_gnn_W_in_b"]
        self.L0_gnn_W_in_w = arrays["L0_gnn_W_in_w"]
        self.L0_gnn_W_out_b = arrays["L0_gnn_W_out_b"]
        self.L0_gnn_W_out_w = arrays["L0_gnn_W_out_w"]
        self.L0_gnn_W_upd_b = arrays["L0_gnn_W_upd_b"]
        self.L0_gnn_W_upd_w = arrays["L0_gnn_W_upd_w"]
        self.L0_gnn_ffn1_b = arrays["L0_gnn_ffn1_b"]
        self.L0_gnn_ffn1_w = arrays["L0_gnn_ffn1_w"]
        self.L0_gnn_ffn2_b = arrays["L0_gnn_ffn2_b"]
        self.L0_gnn_ffn2_w = arrays["L0_gnn_ffn2_w"]
        self.L0_gnn_ln1_b = arrays["L0_gnn_ln1_b"]
        self.L0_gnn_ln1_g = arrays["L0_gnn_ln1_g"]
        self.L0_gnn_ln2_b = arrays["L0_gnn_ln2_b"]
        self.L0_gnn_ln2_g = arrays["L0_gnn_ln2_g"]
        self.L1_gnn_Wk0 = arrays["L1_gnn_Wk0"]
        self.L1_gnn_Wk1 = arrays["L1_gnn_Wk1"]
        self.L1_gnn_Wq0 = arrays["L1_gnn_Wq0"]
        self.L1_gnn_Wq1 = arrays["L1_gnn_Wq1"]
        self.L1_gnn_Ws0 = arrays["L1_gnn_Ws0"]
        self.L1_gnn_Ws1 = arrays["L1_gnn_Ws1"]
        self.L1_gnn_Wv0 = arrays["L1_gnn_Wv0"]
        self.L1_gnn_Wv1 = arrays["L1_gnn_Wv1"]
        self.L1_gnn_bk0 = arrays["L1_gnn_bk0"]
        self.L1_gnn_bk1 = arrays["L1_gnn_bk1"]
        self.L1_gnn_bq0 = arrays["L1_gnn_bq0"]
        self.L1_gnn_bq1 = arrays["L1_gnn_bq1"]
        self.L1_gnn_bs0 = arrays["L1_gnn_bs0"]
        self.L1_gnn_bs1 = arrays["L1_gnn_bs1"]
        self.L1_gnn_bv0 = arrays["L1_gnn_bv0"]
        self.L1_gnn_bv1 = arrays["L1_gnn_bv1"]
        self.L2_gnn_W_l = arrays["L2_gnn_W_l"]
        self.L2_gnn_W_r = arrays["L2_gnn_W_r"]
        self.L2_gnn_att = arrays["L2_gnn_att"]
        self.L2_gnn_bias = arrays["L2_gnn_bias"]
        self.L2_gnn_ln_b = arrays["L2_gnn_ln_b"]
        self.L2_gnn_ln_w = arrays["L2_gnn_ln_w"]
        self.L3_gnn_W = arrays["L3_gnn_W"]
        self.L3_gnn_att_w = arrays["L3_gnn_att_w"]
        self.L3_gnn_b = arrays["L3_gnn_b"]
        self.L3_gnn_norm_b = arrays["L3_gnn_norm_b"]
        self.L3_gnn_norm_w = arrays["L3_gnn_norm_w"]
        self.nc, self.ctx, self.counts, self.names = nc, ctx, {}, {}

    def own(self, name):
        self.names[name] = self.names.get(name, -1) + 1
        return f"{name}_{self.names[name]}" if self.names[name] else name

    def fresh(self, name):
        return self.ctx.enter_context(self.nc.semaphore(name))

    def count(self, name, ahead=0, unit=1):
        if name not in self.counts:
            self.counts[name] = Count(self.fresh(name), ahead, unit)
        c = self.counts[name]
        c.ahead, c.unit = ahead, unit
        return c

    def close(self, n, *counts):
        for c in counts:
            c.base += (n + c.ahead) * c.unit


class OneHotWriter:
    UO = 5
    W = 4 * GROUP
    N = (STEPS * GROUP) // W

    def __init__(self, nc, ctx, k):
        self.nc, self.k = nc, k
        self.local = ctx.enter_context(nc.sbuf_tensor(k.own("local_dst"), [P, self.UO, self.W], BF16))
        self.hot = ctx.enter_context(nc.sbuf_tensor(k.own("one_hot"), [P, self.UO, self.W], BF16))
        self.loaded = [k.fresh(f"local_loaded{u}") for u in range(self.UO)]
        self.made = [k.fresh(f"one_hot_made{u}") for u in range(self.UO)]
        self.stored = [k.fresh(f"one_hot_stored{u}") for u in range(self.UO)]
        self.passed = k.fresh("one_hot_passed")

    def load(self, sp):
        UO, W = self.UO, self.W
        flat = self.k.dloc_dram.rearrange("s (o e) -> o (s e)", o=1)
        with sp.Fori(0, self.N // UO) as i:
            for u in range(UO):
                sp.wait_ge(self.made[u], i + 1)
                sp.dma_start(self.local[:, u, :], flat[:, ds((i * UO + u) * W, W)].partition_broadcast(P)
                             ).then_inc(self.loaded[u], 16)

    def write(self, pool):
        UO, W = self.UO, self.W

        def chunk_out(i, u, first=False):
            pool.wait_ge(self.loaded[u], i * 16 + 16)
            if not first:
                pool.wait_ge(self.stored[u], i * 16)
            pool.sem_inc(self.passed)
            self.nc.gpsimd.tensor_scalar(self.hot[:, u, :], self.local[:, u, :], self.k.iota_p[:, 0:1], None,
                                         ALU.is_equal).then_inc(self.made[u], 1)
            pool.wait_ge(self.made[u], i + 2)
            pool.sem_inc(self.passed)
            pool.dma_start(self.k.hot_dram[:, ds((i * UO + u) * W, W)], self.hot[:, u, :]).then_inc(self.stored[u], 16)
        for u in range(UO):
            pool.sem_inc(self.made[u], 1)
        for u in range(UO):
            chunk_out(0, u, first=True)
        with pool.Fori(1, self.N // UO) as i:
            for u in range(UO):
                chunk_out(i, u)
        for u in range(UO):
            pool.wait_ge(self.stored[u], 16 * (self.N // UO))



def norm_head(dve, x, w, var_made):
    v = w.vector
    v.tensor_reduce(w.mean[:, :], x, AXX, ALU.add)
    dve.drain()
    v.tensor_scalar(w.mean[:, :], w.mean[:, :], 1.0 / D, None, ALU.mult)
    dve.drain()
    v.tensor_tensor(w.c[:, :, :], x, w.mean[:, :].unsqueeze(2).broadcast_to([P, CH, D]), ALU.subtract)
    dve.drain()
    v.tensor_tensor(w.sq[:, :, :], w.c[:, :, :], w.c[:, :, :], ALU.mult)
    dve.drain()
    v.tensor_reduce(w.var[:, :], w.sq[:, :, :], AXX, ALU.add).then_inc(var_made.sem, 1)


def norm_sqrt(act, nc, w, var_made, sd_made, n):
    act.wait_ge(*var_made.done(n))
    nc.scalar.activation(w.sd[:, :], w.var[:, :], ACT.Sqrt, bias=w.eps[:, 0:1], scale=1.0 / D)\
      .then_inc(sd_made.sem, 1)


def norm_tail(dve, w, out, sd_made, n):
    v = w.vector
    dve.wait_ge(*sd_made.done(n))
    v.reciprocal(w.rstd[:, :], w.sd[:, :])
    dve.drain()
    v.tensor_tensor(out, w.c[:, :, :], w.rstd[:, :].unsqueeze(2).broadcast_to([P, CH, D]), ALU.mult)
    dve.drain()


def over_rows(row):
    return row.unsqueeze(1).broadcast_to([P, CH, D])


class Scratch:

    def __init__(self, nc, sb, name, eps):
        self.vector = nc.vector
        self.mean = sb(name + "_mean", [P, CH])
        self.var = sb(name + "_var", [P, CH])
        self.sd = sb(name + "_sd", [P, CH])
        self.rstd = sb(name + "_rstd", [P, CH])
        self.c = sb(name + "_c", [P, CH, D])
        self.sq = sb(name + "_sq", [P, CH, D])
        self.eps = eps


def chunk(t, i):
    return t[:, ds(i * CH, CH), :]


def rows_of(dram, i, width):
    return dram.rearrange("(w p) d -> p w d", p=P)[:, ds(i * CH, CH), 0:width]


def edge_conv_in_phase(nc, k):
    with ExitStack() as ctx:
        def sb(name, shape, dt=F32):
            return ctx.enter_context(nc.sbuf_tensor(k.own(name), shape, dt))
        wts = sb("w_in", [D, D])
        b = sb("b_in", [P, D])
        w = Scratch(nc, sb, "n0", k.eps5)
        h = sb("h", [P, CH, D])
        hT = sb("hT", [P, CH, D])
        g = sb("g", [P, CH, D])
        pT = ctx.enter_context(nc.psum_tensor(k.own("pT"), [P, 8, D], F32))
        pG = ctx.enter_context(nc.psum_tensor(k.own("pG"), [P, 8, D], F32))
        s_w = k.fresh("weights_in")
        var, sd, h_made, turned, hT_made, g_prod, g_made = (k.count(n) for n in (
            "var_made", "sd_made", "h_made", "h_turned", "hT_made", "g_product", "g_made"))
        g_out, moved = k.count("rows_stored_chunk", 1, 16), k.count("product_moved", 1)
        with nc.Block() as block:
            @block.sync
            def _(sp):
                sp.dma_start(wts[:, :], k.L0_gnn_W_in_w).then_inc(s_w, 16)
                sp.dma_start(b[:, :], k.L0_gnn_W_in_b.rearrange("(o n) -> o n", o=1).partition_broadcast(P)).then_inc(s_w, 16)
                with sp.Fori(0, CHUNKS) as i:
                    sp.wait_ge(*g_made.done(i + 1))
                    sp.dma_start(rows_of(k.g_dram, i, D), g[:, :, :]).then_inc(g_out.sem, 16)
                sp.wait_ge(*g_out.done(CHUNKS))

            @block.vector
            def _(dve):
                v = nc.vector
                dve.wait_ge(s_w, 32)
                dve.sem_inc(g_out.sem, 16)
                dve.sem_inc(moved.sem)

                def normed(i, first=False):
                    norm_head(dve, chunk(k.X, i), w, var)
                    if not first:
                        dve.wait_ge(*turned.done(i))
                    norm_tail(dve, w, h[:, :, :], sd, i + 1)
                    v.tensor_scalar(h[:, :, :], h[:, :, :], 0.0, None, ALU.max)
                    dve.drain()
                    v.tensor_copy(chunk(k.H, i), h[:, :, :])
                    dve.drain().then_inc(h_made.sem, 1)

                def take(i):
                    dve.wait_ge(*g_prod.done(i + 1))
                    dve.wait_ge(*g_out.free(i + 1, 1))
                    v.tensor_tensor(g[:, :, :], pG[:, 0:CH, :], over_rows(b[:, :]), ALU.add)
                    dve.drain().then_inc(g_made.sem, 1)
                    dve.sem_inc(moved.sem)
                    v.tensor_copy(chunk(k.G, i), g[:, :, :])
                    dve.drain()
                normed(0, first=True)
                with dve.Fori(0, CHUNKS - 1) as i:
                    normed(i + 1)
                    take(i)
                take(CHUNKS - 1)

            @block.scalar
            def _(act):
                def turn(i):
                    act.wait_ge(*turned.done(i + 1))
                    nc.scalar.copy(hT[:, :, :], pT[:, 0:CH, :]).then_inc(hT_made.sem, 1)
                norm_sqrt(act, nc, w, var, sd, 1)
                with act.Fori(0, CHUNKS - 1) as i:
                    turn(i)
                    norm_sqrt(act, nc, w, var, sd, i + 2)
                turn(CHUNKS - 1)

            @block.tensor
            def _(pe):
                pe.wait_ge(s_w, 32)
                with pe.Fori(0, CHUNKS) as i:
                    pe.wait_ge(*h_made.done(i + 1))
                    for c in range(CH):
                        last = nc.tensor.transpose(pT[:, c, :], h[:, c, :], k.ident[:, :])
                    last.then_inc(turned.sem, 1)
                    pe.wait_ge(*hT_made.done(i + 1))
                    pe.wait_ge(*moved.free(i + 1, 1))
                    for c in range(CH):
                        last = nc.tensor.matmul(pG[:, c, :], hT[:, c, :], wts[:, :], start=True, stop=True)
                    last.then_inc(g_prod.sem, 1)
        k.close(CHUNKS, var, sd, h_made, turned, hT_made, g_prod, g_made, g_out, moved)


def edge_max_phase(nc, k):
    with ExitStack() as ctx:
        def sb(name, shape, dt=F32):
            return ctx.enter_context(nc.sbuf_tensor(k.own(name), shape, dt))

        def pb(name):
            return ctx.enter_context(nc.psum_tensor(k.own(name), [P, 512], F32))
        idx = sb("staged_src", [P, REPEAT, 2 * U], I32)
        rows = sb("g_rows", [P, U, 2, D])
        mask = sb("mask_all", [P, 2, 2 * GROUP], BF16)
        scan = sb("running_max", [P, 2, GROUP])
        msg = sb("max_rows", [P, 2, 2, D + 4])
        sel = sb("select_end", [P, 2, 2, P])
        pT = [pb(f"gT{p}") for p in range(2)]
        pB = [pb(f"back{p}") for p in range(2)]
        pO = [pb(f"picked{p}") for p in range(2)]
        staged, turned, scanned, back, moved, selected, summed, added, passed = (k.count(n, a) for n, a in (
            ("src_staged", 0), ("rows_turned", U), ("max_scanned", U), ("max_turned_back", U),
            ("max_moved", U), ("selection_made", 0), ("window_summed", U), ("window_added", U), ("pool_passed", 0)))
        gathered = [k.count(f"rows_gathered{u}", 0, 32) for u in range(U)]
        masked = [k.count(f"mask_loaded{v}", 0, 16) for v in range(2)]
        flat = k.mask_dram.rearrange("s (o e) -> o (s e)", o=1)
        with nc.Block() as block:
            @block.sync
            def _(sp):
                with sp.Fori(0, ITERS) as i:
                    for h in range(2):
                        sp.wait_ge(*scanned.free(U * i + 2 * h + 2, U))
                        sp.dma_start(mask[:, h, :], flat[:, ds((2 * i + h) * 2 * GROUP, 2 * GROUP)].partition_broadcast(P)
                                     ).then_inc(masked[h].sem, 16)

            @block.gpsimd
            def _(pool):
                gather_rows(nc, k, pool, idx, rows, D, k.g_dram, staged, passed, (turned,), gathered)

            @block.tensor
            def _(pe):
                t = nc.tensor
                for c in (turned, back, summed):
                    pe.sem_inc(c.sem, U)

                def turn(i, u):
                    pe.wait_ge(*gathered[u].done(i + 1))
                    pe.wait_ge(*scanned.free(U * i + u + 1, 2))
                    for j in range(2):
                        last = t.transpose(pT[u % 2][:, j * P:(j + 1) * P], rows[:, u, j, :], k.ident[:, :])
                    last.then_inc(turned.sem, 1)

                def turn_back(i, u):
                    pe.wait_ge(*scanned.done(U * i + u + 1))
                    pe.wait_ge(*moved.free(U * i + u + 1, 2))
                    for j in range(2):
                        last = t.transpose(pB[u % 2][:, j * P:(j + 1) * P], scan[:, u % 2, j * P:(j + 1) * P],
                                           k.ident[:, :])
                    last.then_inc(back.sem, 1)

                def pick(i, u):
                    pe.wait_ge(*moved.done(U * i + u + 1))
                    pe.wait_ge(*selected.done(U * i + u + 1))
                    pe.wait_ge(*added.free(U * i + u + 1, 2))
                    for j in range(2):
                        last = t.matmul(pO[u % 2][:, 0:D + 1], sel[:, u % 2, j, :], msg[:, u % 2, j, 0:D + 1],
                                        start=(j == 0), stop=(j == 1))
                    last.then_inc(summed.sem, 1)

                def slot(i, u, to_come):
                    if to_come > 2:
                        turn(i + (u + 2) // U, (u + 2) % U)
                    if to_come > 1:
                        turn_back(i + (u + 1) // U, (u + 1) % U)
                    pick(i, u)
                turn(0, 0)
                turn(0, 1)
                turn_back(0, 0)
                with pe.Fori(0, ITERS - 1) as i:
                    for u in range(U):
                        slot(i, u, U)
                for u in range(U):
                    slot(ITERS - 1, u, U - u)

            @block.scalar
            def _(act):
                act.sem_inc(moved.sem, U)
                with act.Fori(0, ITERS) as i:
                    for u in range(U):
                        act.wait_ge(*back.done(U * i + u + 1))
                        act.wait_ge(*summed.free(U * i + u + 1, 2))
                        nc.scalar.copy(msg[:, u % 2, :, 0:D], pB[u % 2][:, 0:2 * P].rearrange("p (j d) -> p j d", j=2)
                                       ).then_inc(moved.sem, 1)

            @block.vector
            def _(dve):
                v = nc.vector
                v.memset(k.acc[:, 0:WINDOWS * (D + 1)], 0.0)
                v.memset(msg[:, :, :, D:D + 1], 1.0)
                v.memset(scan[:, 1, GROUP - 1:GROUP], -BIG)
                dve.drain()
                dve.sem_inc(scanned.sem, U)
                dve.sem_inc(added.sem, U)

                def run_max(i, u):
                    dve.drain()
                    dve.wait_ge(*turned.done(U * i + u + 1))
                    dve.wait_ge(*back.free(U * i + u + 1, 2))
                    if u % 2 == 0:
                        dve.wait_ge(*masked[u // 2].done(i + 1))
                    v.tensor_tensor_scan(scan[:, u % 2, :], mask[:, u // 2, (u % 2) * GROUP:(u % 2 + 1) * GROUP],
                                         pT[u % 2][:, 0:GROUP], scan[:, 1 - u % 2, GROUP - 1:GROUP], ALU.add, ALU.max
                                         ).then_inc(scanned.sem, 1)

                def select(i, u):
                    dve.wait_ge(*summed.free(U * i + u + 1, 2))
                    for j in range(2):
                        col = U * 2 * i + 2 * u + j
                        last = v.tensor_scalar(sel[:, u % 2, j, :], k.iota_row[:, :], k.dloc_e[:, ds(col, 1)],
                                               k.end_e[:, ds(col, 1)], ALU.is_equal, ALU.mult)
                    last.then_inc(selected.sem, 1)

                def add(i, u, win):
                    dve.drain()
                    dve.wait_ge(*summed.done(U * i + u + 1))
                    acc = k.acc[:, ds(win[u] * (D + 1), D + 1)]
                    v.tensor_tensor(acc, acc, pO[u % 2][:, 0:D + 1], ALU.add).then_inc(added.sem, 1)

                def slot(i, u, win, to_come):
                    if to_come > 2:
                        run_max(i + (u + 2) // U, (u + 2) % U)
                    if to_come > 1:
                        select(i + (u + 1) // U, (u + 1) % U)
                    add(i, u, win)
                run_max(0, 0)
                run_max(0, 1)
                select(0, 0)
                with dve.Fori(0, ITERS - 1) as i:
                    win = windows_of(dve, k, i)
                    for u in range(U):
                        slot(i, u, win, U)
                win = windows_of(dve, k, ITERS - 1)
                for u in range(U):
                    slot(ITERS - 1, u, win, U - u)
        k.close(STEPS, turned, scanned, back, moved, selected, summed, added)
        k.close(ITERS, staged, passed)
        k.close(ITERS, *gathered, *masked)


def gather_rows(nc, k, pool, idx, rows, width, table, staged, passed, taken, gathered, kept=()):
    with pool.Fori(0, ITERS // REPEAT) as n:
        for r in range(REPEAT):
            i = n * REPEAT + r
            nc.gpsimd.tensor_copy(idx[:, r, :], k.src_e[:, ds(2 * U * i, 2 * U)]).then_inc(staged.sem, 1)
            pool.wait_ge(*staged.done(i + 1))
            pool.sem_inc(passed.sem)
            for u in range(U):
                for c in taken:
                    pool.wait_ge(*c.free(U * i + u + 1, U))
                if kept:
                    pool.wait_ge(*kept[u].free(i + 1, 1))
                pool.sem_inc(passed.sem)
                for j in range(2):
                    nc.gpsimd.indirect_dma_start(rows[:, u, j, 0:width], None, table,
                                                 bass.IndirectOffsetOnAxis(ap=idx[:, r, 2 * u + j:2 * u + j + 1], axis=0)
                                                 ).then_inc(gathered[u].sem, 16)


def edge_conv_out_phase(nc, k):
    with ExitStack() as ctx:
        def sb(name, shape, dt=F32):
            return ctx.enter_context(nc.sbuf_tensor(k.own(name), shape, dt))

        def pb(name):
            return ctx.enter_context(nc.psum_tensor(k.own(name), [P, 8, D], F32))
        w_upd = sb("w_upd", [D, 2, D])
        w_out = sb("w_out", [D, D])
        w_f1 = sb("w_f1", [D, 4, D])
        w_f2 = sb("w_f2", [D, 4, D])
        b_upd = sb("b_upd", [D, 1])
        b_f1 = sb("b_f1", [D, 4])
        bc = sb("rows_bc", [P, 6, D])
        w = Scratch(nc, sb, "n1", k.eps5)
        one_hots = OneHotWriter(nc, ctx, k)
        md = sb("max_diff", [P, CH, D])
        res = sb("residual", [P, CH, D])
        gT = sb("gT", [P, CH, D])
        mT = sb("mT", [P, CH, D])
        uT = sb("uT", [P, CH, D])
        x1 = sb("x1", [P, CH, D])
        x1T = sb("x1T", [P, CH, D])
        y = sb("y", [P, CH, D])
        fT = sb("fT", [P, 4, CH, D])
        pA, pB, pC, pD = pb("pA"), pb("pB"), pb("pC"), pb("pD")
        s_w = k.fresh("weights_out")
        (md_made, turned, gT_made, u_prod, uT_made, o_prod, var, sd, x1_made, x1_turned, x1T_made, f_prod, f_made,
         y_prod, chunk_done) = (k.count(n) for n in (
             "h_made", "h_turned", "hT_made", "u_product", "uT_made", "o_product", "var_made", "sd_made",
             "x1_made", "x1_turned", "x1T_made", "ffn_product", "ffn_made", "y_product", "chunk_done"))
        srcs = ((w_upd[:, :, :], k.L0_gnn_W_upd_w.rearrange("(c p) n -> p c n", p=D)),
                (w_out[:, :], k.L0_gnn_W_out_w),
                (w_f1[:, :, :], k.L0_gnn_ffn1_w.rearrange("p (c n) -> p c n", n=D)),
                (w_f2[:, :, :], k.L0_gnn_ffn2_w.rearrange("(c p) n -> p c n", p=D)),
                (b_upd[:, :], k.L0_gnn_W_upd_b.rearrange("(p o) -> p o", o=1)),
                (b_f1[:, :], k.L0_gnn_ffn1_b.rearrange("(c p) -> p c", p=D)))
        rows = (k.L0_gnn_W_out_b, k.L0_gnn_ln1_g, k.L0_gnn_ln1_b, k.L0_gnn_ffn2_b, k.L0_gnn_ln2_g, k.L0_gnn_ln2_b)
        loaded = 16 * (len(srcs) + len(rows))
        with nc.Block() as block:
            @block.sync
            def _(sp):
                with nc.allow_non_contiguous_dma(reason="small columns of biases"):
                    for out, src in srcs:
                        sp.dma_start(out, src).then_inc(s_w, 16)
                for n, row in enumerate(rows):
                    sp.dma_start(bc[:, n, :], row.rearrange("(o n) -> o n", o=1).partition_broadcast(P)).then_inc(s_w, 16)
                one_hots.load(sp)

            @block.gpsimd
            def _(pool):
                one_hots.write(pool)

            @block.vector
            def _(dve):
                v = nc.vector
                acc = k.acc[:, 0:WINDOWS * (D + 1)].rearrange("p (w d) -> p w d", d=D + 1)
                dve.wait_ge(s_w, loaded)
                with dve.Fori(0, CHUNKS) as i:
                    a = acc[:, ds(i * CH, CH), :]
                    v.tensor_tensor(md[:, :, :], chunk(k.G, i), a[:, :, D:D + 1].broadcast_to([P, CH, D]), ALU.mult)
                    v.tensor_copy(y[:, :, :], chunk(k.G, i))
                    dve.drain()
                    v.tensor_tensor(md[:, :, :], a[:, :, 0:D], md[:, :, :], ALU.subtract).then_inc(md_made.sem, 1)
                    v.tensor_tensor(res[:, :, :], chunk(k.H, i), over_rows(bc[:, 0, :]), ALU.add)
                    dve.drain()
                    dve.wait_ge(*o_prod.done(i + 1))
                    v.tensor_tensor(x1[:, :, :], pA[:, 0:CH, :], res[:, :, :], ALU.add)
                    dve.drain()
                    norm_head(dve, x1[:, :, :], w, var)
                    norm_tail(dve, w, x1[:, :, :], sd, 2 * i + 1)
                    v.tensor_tensor(x1[:, :, :], x1[:, :, :], over_rows(bc[:, 1, :]), ALU.mult)
                    dve.drain()
                    v.tensor_tensor(x1[:, :, :], x1[:, :, :], over_rows(bc[:, 2, :]), ALU.add).then_inc(x1_made.sem, 1)
                    dve.drain()
                    v.tensor_tensor(res[:, :, :], x1[:, :, :], over_rows(bc[:, 3, :]), ALU.add)
                    v.tensor_tensor(chunk(k.X, i), chunk(k.X, i), over_rows(bc[:, 5, :]), ALU.add)
                    dve.drain()
                    dve.wait_ge(*y_prod.done(i + 1))
                    v.tensor_tensor(y[:, :, :], pB[:, 0:CH, :], res[:, :, :], ALU.add)
                    dve.drain()
                    norm_head(dve, y[:, :, :], w, var)
                    norm_tail(dve, w, y[:, :, :], sd, 2 * i + 2)
                    v.tensor_tensor(y[:, :, :], y[:, :, :], over_rows(bc[:, 4, :]), ALU.mult)
                    dve.drain()
                    v.tensor_tensor(chunk(k.X, i), chunk(k.X, i), y[:, :, :], ALU.add)
                    dve.drain().then_inc(chunk_done.sem, 1)

            @block.scalar
            def _(act):
                s = nc.scalar
                with act.Fori(0, CHUNKS) as i:
                    act.wait_ge(*turned.done(i + 1))
                    s.copy(gT[:, :, :], pA[:, 0:CH, :])
                    s.copy(mT[:, :, :], pB[:, 0:CH, :]).then_inc(gT_made.sem, 1)
                    act.wait_ge(*u_prod.done(i + 1))
                    s.activation(uT[:, :, :], pC[:, 0:CH, :], ACT.Identity, bias=b_upd[:, 0:1]).then_inc(uT_made.sem, 1)
                    norm_sqrt(act, nc, w, var, sd, 2 * i + 1)
                    act.wait_ge(*x1_turned.done(i + 1))
                    s.copy(x1T[:, :, :], pA[:, 0:CH, :]).then_inc(x1T_made.sem, 1)
                    for f in range(4):
                        act.wait_ge(*f_prod.done(4 * i + f + 1))
                        s.activation(fT[:, f, :, :], (pC, pD)[f % 2][:, 0:CH, :], ACT.Gelu, bias=b_f1[:, f:f + 1]
                                     ).then_inc(f_made.sem, 1)
                    norm_sqrt(act, nc, w, var, sd, 2 * i + 2)

            @block.tensor
            def _(pe):
                t = nc.tensor

                def wide(out, lhsT, rhs, start, stop):
                    t.matmul(out[:, 0:4, :], lhsT, rhs[:, 0:4, :], start=start, stop=stop)
                    return t.matmul(out[:, 4:CH, :], lhsT, rhs[:, 4:CH, :], start=start, stop=stop)
                pe.wait_ge(s_w, loaded)

                with pe.Fori(0, CHUNKS) as i:
                    pe.wait_ge(*md_made.done(i + 1))
                    for c in range(CH):
                        t.transpose(pA[:, c, :], y[:, c, :], k.ident[:, :])
                        last = t.transpose(pB[:, c, :], md[:, c, :], k.ident[:, :])
                    last.then_inc(turned.sem, 1)
                    pe.wait_ge(*gT_made.done(i + 1))
                    wide(pC, w_upd[:, 0, :], gT, True, False)
                    wide(pC, w_upd[:, 1, :], mT, False, True).then_inc(u_prod.sem, 1)
                    pe.wait_ge(*uT_made.done(i + 1))
                    for c in range(CH):
                        last = t.matmul(pA[:, c, :], uT[:, c, :], w_out[:, :], start=True, stop=True)
                    last.then_inc(o_prod.sem, 1)
                    pe.wait_ge(*x1_made.done(i + 1))
                    for c in range(CH):
                        last = t.transpose(pA[:, c, :], x1[:, c, :], k.ident[:, :])
                    last.then_inc(x1_turned.sem, 1)
                    pe.wait_ge(*x1T_made.done(i + 1))
                    for f in range(4):
                        if f >= 2:
                            pe.wait_ge(*f_made.done(4 * i + f - 1))
                        wide((pC, pD)[f % 2], w_f1[:, f, :], x1T, True, True).then_inc(f_prod.sem, 1)
                    pe.wait_ge(*f_made.done(4 * i + 4))
                    for c in range(CH):
                        for f in range(4):
                            last = t.matmul(pB[:, c, :], fT[:, f, c, :], w_f2[:, f, :], start=(f == 0), stop=(f == 3))
                    last.then_inc(y_prod.sem, 1)
        k.close(CHUNKS, md_made, turned, gT_made, u_prod, uT_made, o_prod, x1_made, x1_turned, x1T_made, y_prod,
                chunk_done)
        k.close(2 * CHUNKS, var, sd)
        k.close(4 * CHUNKS, f_prod, f_made)



def split3(dve, nc, full, hi, mid, lo, rest):
    v = nc.vector
    v.tensor_copy(hi, full)
    dve.drain()
    v.tensor_tensor(rest, full, hi, ALU.subtract)
    dve.drain()
    v.tensor_copy(mid, rest)
    dve.drain()
    return v.tensor_tensor(lo, rest, mid, ALU.subtract)


def conv1_in_phase(nc, k):
    C = HEADS * (D + 1)
    with ExitStack() as ctx:
        def sb(name, shape, dt=F32):
            return ctx.enter_context(nc.sbuf_tensor(k.own(name), shape, dt))

        def pb(name, shape):
            return ctx.enter_context(nc.psum_tensor(k.own(name), shape, F32))
        wq = sb("wq", [D, HEADS, D])
        wk = sb("wk", [D, HEADS, D])
        wqT = sb("wqT", [D, HEADS, D])
        wkT = sb("wkT", [D, HEADS, D + 1])
        bq = sb("bq", [D, HEADS])
        bq_wide = sb("bq_wide", [D, HEADS, D])
        both = sb("wq_wk", [D, C])
        bias = sb("bq_wk", [P, C])
        w = Scratch(nc, sb, "n2", k.eps5)
        h = sb("h", [P, CH, D + 4])
        hT = sb("hT", [P, CH, D])
        u = sb("u", [P, CH, C])
        pT = pb("pT", [P, 8, D])
        pW = pb("pW", [P, 2, 512])
        pU = [pb(f"pU{n}", [P, 2, 512]) for n in range(2)]
        s_w = k.fresh("weights_conv1")
        s_wide = k.fresh("bq_spread")
        s_k = k.fresh("wk_turned")
        s_kT = k.fresh("wkT_made")
        s_m = k.fresh("wq_wk_product")
        s_mm = k.fresh("wq_wk_made")
        var, sd, h_made, turned, hT_made = (k.count(n) for n in (
            "var_made", "sd_made", "h_made", "h_turned", "hT_made"))
        h_out = k.count("rows_stored_chunk", 1, 16)
        u_prod, u_read = k.count("u_product"), k.count("u_read", 2)
        u_made, hi_made, rest_made, mid_made = (k.count(n) for n in ("u_made", "u_hi_made", "u_rest_made", "u_mid_made"))
        act_passed = k.count("act_passed")

        def part(i, c, n):
            return k.U[:, ds(i * (CH * 3 * C) + (3 * c + n) * C, C)]
        with nc.Block() as block:
            @block.sync
            def _(sp):
                with nc.allow_non_contiguous_dma(reason="small columns of biases"):
                    sp.dma_start(wq[:, :, :], k.L1_gnn_Wq0.rearrange("p (h n) -> p h n", n=D)).then_inc(s_w, 16)
                    sp.dma_start(wk[:, :, :], k.L1_gnn_Wk0.rearrange("p (h n) -> p h n", n=D)).then_inc(s_w, 16)
                    sp.dma_start(bq[:, :], k.L1_gnn_bq0.rearrange("(h p) -> p h", p=D)).then_inc(s_w, 16)
                    sp.dma_start(wkT[:, :, D], k.L1_gnn_bk0.rearrange("(h p) -> p h", p=D)).then_inc(s_w, 16)
                with sp.Fori(0, CHUNKS) as i:
                    sp.wait_ge(*h_made.done(i + 1))
                    sp.dma_start(rows_of(k.h_dram, i, D + 4), h[:, :, :]).then_inc(h_out.sem, 16)
                sp.wait_ge(*h_out.done(CHUNKS))

            @block.vector
            def _(dve):
                v = nc.vector
                v.memset(h[:, :, D:D + 4], 1.0)
                dve.wait_ge(s_w, 64)
                v.tensor_copy(bq_wide[:, :, :], bq[:, :].unsqueeze(2).broadcast_to([D, HEADS, D])).then_inc(s_wide, 1)
                dve.wait_ge(s_k, 1)
                v.tensor_copy(wkT[:, :, 0:D], pT[:, 0:HEADS, :])
                v.tensor_copy(wqT[:, :, :], pT[:, HEADS:2 * HEADS, :])
                dve.drain().then_inc(s_kT, 1)
                dve.sem_inc(h_out.sem, 16)
                dve.sem_inc(u_read.sem, 2)
                dve.wait_ge(s_m, 1)
                v.tensor_copy(both[:, :].rearrange("p (b n) -> p b n", b=2), pW[:, :, 0:C // 2]).then_inc(s_mm, 1)
                dve.wait_ge(s_m, 2)
                v.tensor_copy(bias[:, :].rearrange("p (b n) -> p b n", b=2), pU[1][:, :, 0:C // 2]).then_inc(s_mm, 1)

                def normed(i, first=False):
                    norm_head(dve, chunk(k.X, i), w, var)
                    dve.wait_ge(*h_out.free(i + 1, 1))
                    if not first:
                        dve.wait_ge(*turned.done(i))
                    norm_tail(dve, w, h[:, :, 0:D], sd, i + 1)
                    v.tensor_scalar(h[:, :, 0:D], h[:, :, 0:D], 0.0, None, ALU.max)
                    dve.drain().then_inc(h_made.sem, 1)
                    v.tensor_copy(chunk(k.H, i), h[:, :, 0:D])
                    dve.drain()

                def split(i):
                    for n in range(CH + 2):
                        if n < CH:
                            dve.wait_ge(*u_prod.done(CH * i + n + 1))
                            v.tensor_tensor(u[:, n, :].rearrange("p (b n) -> p b n", b=2), pU[n % 2][:, :, 0:C // 2],
                                            bias[:, :].rearrange("p (b n) -> p b n", b=2), ALU.add)
                            dve.drain().then_inc(u_made.sem, 1)
                            dve.sem_inc(u_read.sem, 1)
                        if 1 <= n < CH + 1:
                            c = n - 1
                            dve.wait_ge(*hi_made.done(CH * i + c + 1))
                            v.tensor_tensor(u[:, c, :], u[:, c, :], part(i, c, 0), ALU.subtract).then_inc(rest_made.sem, 1)
                        if n >= 2:
                            c = n - 2
                            dve.wait_ge(*mid_made.done(CH * i + c + 1))
                            v.tensor_tensor(part(i, c, 2), u[:, c, :], part(i, c, 1), ALU.subtract)
                    dve.drain()
                normed(0, first=True)
                with dve.Fori(0, CHUNKS - 1) as i:
                    normed(i + 1)
                    split(i)
                split(CHUNKS - 1)

            @block.scalar
            def _(act):
                def rounded(i):
                    for n in range(CH + 1):
                        if n < CH:
                            act.wait_ge(*u_made.done(CH * i + n + 1))
                            act.sem_inc(act_passed.sem)
                            nc.scalar.copy(part(i, n, 0), u[:, n, :]).then_inc(hi_made.sem, 1)
                        if n >= 1:
                            act.wait_ge(*rest_made.done(CH * i + n))
                            act.sem_inc(act_passed.sem)
                            nc.scalar.copy(part(i, n - 1, 1), u[:, n - 1, :]).then_inc(mid_made.sem, 1)

                def turn(i):
                    act.wait_ge(*turned.done(i + 1))
                    nc.scalar.copy(hT[:, :, :], pT[:, 0:CH, :]).then_inc(hT_made.sem, 1)
                norm_sqrt(act, nc, w, var, sd, 1)
                with act.Fori(0, CHUNKS - 1) as i:
                    turn(i)
                    norm_sqrt(act, nc, w, var, sd, i + 2)
                    rounded(i)
                turn(CHUNKS - 1)
                rounded(CHUNKS - 1)

            @block.tensor
            def _(pe):
                t = nc.tensor
                pe.wait_ge(s_w, 64)
                for n, wt in enumerate((wk, wq)):
                    for hh in range(HEADS):
                        last = t.transpose(pT[:, n * HEADS + hh, :], wt[:, hh, :], k.ident[:, :])
                last.then_inc(s_k, 1)
                pe.wait_ge(s_kT, 1)
                pe.wait_ge(s_wide, 1)
                for out, lhsT in ((pW, wqT), (pU[1], bq_wide)):
                    for hh in range(HEADS):
                        at = (hh % 2) * (D + 1)
                        last = t.matmul(out[:, hh // 2, at:at + D + 1], lhsT[:, hh, :], wkT[:, hh, :],
                                        start=True, stop=True)
                    last.then_inc(s_m, 1)
                pe.wait_ge(s_mm, 2)
                with pe.Fori(0, CHUNKS) as i:
                    pe.wait_ge(*h_made.done(i + 1))
                    for c in range(CH):
                        last = t.transpose(pT[:, c, :], h[:, c, 0:D], k.ident[:, :])
                    last.then_inc(turned.sem, 1)
                    pe.wait_ge(*hT_made.done(i + 1))
                    for c in range(CH):
                        pe.wait_ge(*u_read.free(CH * i + c + 1, 2 if c else 1))
                        for b in range(2):
                            last = t.matmul(pU[c % 2][:, b, 0:C // 2], hT[:, c, :], both[:, b * (C // 2):(b + 1) * (C // 2)],
                                            start=True, stop=True)
                        last.then_inc(u_prod.sem, 1)
        k.close(CHUNKS, var, sd, h_made, turned, hT_made, h_out)
        k.close(WINDOWS, u_prod, u_read, u_made, hi_made, rest_made, mid_made)


def edge_logits_phase(nc, k, table, width, per_head, row, gat=False, keep=False):
    per = row // HEADS
    banks = 2 if row > 512 else 1
    bw = row // banks
    terms = D if gat else per
    dots = 1 if gat else HEADS
    on_dve = 0 if gat else 1
    with ExitStack() as ctx:
        def sb(name, shape, dt=F32):
            return ctx.enter_context(nc.sbuf_tensor(k.own(name), shape, dt))
        idx = sb("staged_src", [P, REPEAT, 2 * U], I32)
        rows = sb("src_rows", [P, U, 2, width])
        hot = sb("one_hot", [P, 2, 2 * GROUP], BF16)
        prod = sb("products", [P, U, 2, dots * terms])
        msg = sb("messages", [P, 2, 2, D if gat else 1])
        pU = [ctx.enter_context(nc.psum_tensor(k.own(f"dst_rows{n}"), [P, banks, 512], F32)) for n in range(4)]
        staged, picked, read, made, dotted, passed, act_passed = (k.count(n, a) for n, a in (
            ("src_staged", 0), ("dst_rows_picked", 0), ("edge_rows_read", U), ("products_made", 0),
            ("logits_made", U), ("pool_passed", 0), ("act_passed", 0)))
        gathered = [k.count(f"rows_gathered{u}", 0, 32) for u in range(U)]
        loaded = [k.count(f"one_hot_loaded{v}", 0, 16) for v in range(2)]
        kept = [k.count(f"slot_rows_kept{u}", 1, 16) for u in range(U)] if keep else ()
        with nc.Block() as block:
            if keep:
                @block.sync
                def _(sp):
                    for c in kept:
                        sp.sem_inc(c.sem, 16)
                    with sp.Fori(0, ITERS) as i:
                        for u in range(U):
                            sp.wait_ge(*gathered[u].done(i + 1))
                            sp.dma_start(k.slots_dram[:, ds((U * i + u) * 2 * width, 2 * width)],
                                         rows[:, u].rearrange("p j d -> p (j d)")).then_inc(kept[u].sem, 16)
                    for c in kept:
                        sp.wait_ge(*c.done(ITERS))

            @block.gpsimd
            def _(pool):
                gather_rows(nc, k, pool, idx, rows, width, table, staged, passed, (read,), gathered, kept)

            @block.tensor
            def _(pe):
                def steps(i):
                    win = windows_of(pe, k, i)
                    for u in range(U):
                        pe.wait_ge(*read.free(U * i + u + 1, 2))
                        if u % 2 == 0:
                            pe.wait_ge(*loaded[u // 2].done(i + 1))
                        for j in range(2):
                            lhsT = hot[:, u // 2, (u % 2) * GROUP + j * P:(u % 2) * GROUP + (j + 1) * P]
                            for part in range(3):
                                for b in range(banks):
                                    last = nc.tensor.matmul(
                                        pU[2 * (u % 2) + j][:, b, 0:bw], lhsT,
                                        k.U[:, ds(win[u] * (3 * row) + (part * row + b * bw), bw)],
                                        start=(part == 0), stop=(part == 2))
                        last.then_inc(picked.sem, 1)
                repeat(pe, ITERS, REPEAT, steps)

            @block.vector
            def _(dve):
                v = nc.vector
                dve.sem_inc(read.sem, U)

                def head_products(src_rows, dst_rows, out):
                    hb = HEADS // banks
                    for j in range(2):
                        for b in range(banks):
                            if per_head:
                                src = src_rows[:, j, b * bw:(b + 1) * bw].rearrange("p (h d) -> p h d", h=hb)
                            else:
                                src = src_rows[:, j, 0:per].unsqueeze(1).broadcast_to([P, hb, per])
                            last = v.tensor_tensor(out[:, j, b * bw:(b + 1) * bw].rearrange("p (h d) -> p h d", h=hb),
                                                   dst_rows[j][:, b, 0:bw].rearrange("p (h d) -> p h d", h=hb),
                                                   src, ALU.mult)
                    return last

                with dve.Fori(0, ITERS) as i:
                    for u in range(U):
                        dve.wait_ge(*gathered[u].done(i + 1))
                        dve.wait_ge(*picked.done(U * i + u + 1))
                        dve.wait_ge(*dotted.free(U * i + u + 1, U))
                        dst_rows = [pU[2 * (u % 2) + j] for j in range(2)]
                        if gat:
                            m = msg[:, u % 2]
                            for j in range(2):
                                v.tensor_copy(k.selfs[:, ds(2 * U * i + 2 * u + j, 1)], dst_rows[j][:, 0, D:D + 1])
                                last = v.tensor_tensor(m[:, j], dst_rows[j][:, 0, 0:D], rows[:, u, j, 0:D], ALU.add)
                            last.then_inc(read.sem, 1)
                            dve.drain()
                            v.scalar_tensor_tensor(prod[:, u], m, 0.2, m, ALU.mult, ALU.max)
                            dve.drain()
                            v.tensor_tensor(prod[:, u], prod[:, u], k.att[:, :].unsqueeze(1).broadcast_to([P, 2, D]),
                                            ALU.mult).then_inc(made.sem, 1)
                        else:
                            head_products(rows[:, u], dst_rows, prod[:, u]).then_inc(read.sem, 1)
                            dve.drain().then_inc(made.sem, 1)
                            v.tensor_reduce(k.logits[:, 0, ds(2 * U * i + 2 * u, 2)], prod[:, u, :, 0:terms],
                                            AXX, ALU.add)

            @block.scalar
            def _(act):
                act.sem_inc(dotted.sem, U)

                def load_hot(i, h):
                    act.dma_start(hot[:, h, :], k.hot_dram[:, ds((2 * i + h) * 2 * GROUP, 2 * GROUP)]
                                  ).then_inc(loaded[h].sem, 16)

                def sum_terms(i, u):
                    act.wait_ge(*made.done(U * i + u + 1))
                    act.sem_inc(act_passed.sem)
                    for j in range(2):
                        for h in range(on_dve, dots):
                            part = prod[:, u, j, h * terms:(h + 1) * terms]
                            last = nc.scalar.activation(part, part, ACT.Copy,
                                                        accum_out=k.logits[:, h, ds(2 * U * i + 2 * u + j, 1)])
                    last.then_inc(dotted.sem, 1)
                load_hot(0, 0)
                load_hot(0, 1)
                with act.Fori(0, ITERS - 1) as i:
                    for u in range(U):
                        if u % 2:
                            act.wait_ge(*picked.done(U * i + u + 1))
                            load_hot(i + 1, u // 2)
                        sum_terms(i, u)
                for u in range(U):
                    sum_terms(ITERS - 1, u)
        k.close(STEPS, picked, read, made, dotted, act_passed)
        k.close(ITERS, staged, passed)
        k.close(ITERS, *gathered, *loaded, *kept)


def value_logits_phase(nc, k):
    R = 5
    T = 2 * U
    S = 3 * WINDOWS
    with ExitStack() as ctx:
        def sb(name, shape, dt=F32):
            return ctx.enter_context(nc.sbuf_tensor(k.own(name), shape, dt))
        hot = sb("one_hot", [P, R, U * GROUP], BF16)
        lo = sb("src_lo", [P, R, U * GROUP], BF16)
        lo_hot = sb("one_hot_lo", [P, R, U * GROUP], BF16)
        hi = sb("src_hi", [P, TILES], I32)
        hi_f = sb("src_hi_f", [P, TILES])
        hi_hot = sb("one_hot_hi", [P, T, WINDOWS])
        found = sb("found", [P, T, 3, WINDOWS])
        vals = sb("values", [P, 2, T])
        pV = [ctx.enter_context(nc.psum_tensor(k.own(f"looked_up{n}"), [P, T, 128], F32)) for n in range(2)]
        loaded = [k.count(f"lookup_loaded{n}", 0, 32) for n in range(R)]
        lo_made, looked, used = k.count("one_hot_lo_made"), k.count("values_looked_up", R), k.count("values_used", 2)
        lo_flat = k.lo_dram.rearrange("s (o e) -> o (s e)", o=1)
        N = U * GROUP
        with nc.Block() as block:
            @block.sync
            def _(sp):
                def load(i, n):
                    sp.wait_ge(*looked.free(R * i + n + 1, R))
                    sp.dma_start(lo[:, n, :], lo_flat[:, ds((R * i + n) * N, N)].partition_broadcast(P)
                                 ).then_inc(loaded[n].sem, 16)
                    sp.dma_start(hot[:, n, :], k.hot_dram[:, ds((R * i + n) * N, N)]).then_inc(loaded[n].sem, 16)
                with sp.Fori(0, ITERS // R) as i:
                    for n in range(R):
                        load(i, n)

            @block.vector
            def _(dve):
                v = nc.vector
                v.tensor_scalar(hi[:, :], k.src_e[:, :], 7, None, ALU.arith_shift_right)
                dve.drain()
                v.tensor_copy(hi_f[:, :], hi[:, :])
                dve.drain()
                dve.sem_inc(used.sem, 2)

                def find_lo(i, n):
                    dve.wait_ge(*loaded[n].done(i + 1))
                    v.tensor_scalar(lo_hot[:, n, :], lo[:, n, :], k.iota_p[:, 0:1], None, ALU.is_equal
                                    ).then_inc(lo_made.sem, 1)

                def take(i, n):
                    v.tensor_tensor(hi_hot[:, :, :], k.iota_row[:, 0:WINDOWS].unsqueeze(1).broadcast_to([P, T, WINDOWS]),
                                    hi_f[:, ds((R * i + n) * T, T)].unsqueeze(2).broadcast_to([P, T, WINDOWS]),
                                    ALU.is_equal)
                    dve.drain()
                    dve.wait_ge(*looked.done(R * i + n + 1))
                    v.tensor_tensor(found[:, :, :, :], pV[n % 2][:, :, 0:S].rearrange("p t (c w) -> p t c w", c=3),
                                    hi_hot[:, :, :].unsqueeze(2).broadcast_to([P, T, 3, WINDOWS]), ALU.mult)
                    v.tensor_reduce(vals[:, 1, :], pV[n % 2][:, :, S:S + 3], AXX, ALU.add).then_inc(used.sem, 1)
                    dve.drain()
                    v.tensor_reduce(vals[:, 0, :], found[:, :, :, :].rearrange("p t c w -> p t (c w)"), AXX, ALU.add)
                    dve.drain()
                    v.tensor_tensor(k.logits[:, 0, ds((R * i + n) * T, T)], vals[:, 0, :], vals[:, 1, :], ALU.add)
                    dve.drain()
                find_lo(0, 0)
                with dve.Fori(0, ITERS // R - 1) as i:
                    for n in range(R):
                        find_lo(i + (n + 1) // R, (n + 1) % R)
                        take(i, n)
                for n in range(R):
                    if n + 1 < R:
                        find_lo(ITERS // R - 1, n + 1)
                    take(ITERS // R - 1, n)

            @block.tensor
            def _(pe):
                pe.sem_inc(looked.sem, R)

                def look_up(i, n):
                    win = windows_of(pe, k, R * i + n)
                    pe.wait_ge(*lo_made.done(R * i + n + 1))
                    pe.wait_ge(*used.free(R * i + n + 1, 2 if n else 1))
                    for t in range(T):
                        nc.tensor.matmul(pV[n % 2][:, t, 0:S], lo_hot[:, n, t * P:(t + 1) * P],
                                         k.V[:, :, :].rearrange("p c w -> p (c w)"), start=True, stop=True)
                        last = nc.tensor.matmul(pV[n % 2][:, t, S:S + 3], hot[:, n, t * P:(t + 1) * P],
                                                k.U[:, ds(win[t // 2] * 3, 3)], start=True, stop=True)
                    last.then_inc(looked.sem, 1)
                with pe.Fori(0, ITERS // R) as i:
                    for n in range(R):
                        look_up(i, n)
        k.close(ITERS, lo_made, looked, used)
        k.close(ITERS // R, *loaded)


def value_sums_phase(nc, k):
    R = 5
    with ExitStack() as ctx:
        def sb(name, shape, dt=F32):
            return ctx.enter_context(nc.sbuf_tensor(k.own(name), shape, dt))
        sel = sb("selection", [P, R, U, 2, P], BF16)
        cols = sb("step_sums", [P, STEPS])
        colsT = sb("step_sums_t", [P, 2, P])
        pS = ctx.enter_context(nc.psum_tensor(k.own("step_sum"), [P, 256, 4], F32))
        pT = ctx.enter_context(nc.psum_tensor(k.own("step_sum_t"), [P, 4, P], F32))
        selected, summed = k.count("selection_made", 0), k.count("window_summed", R)
        s_cols, s_turned, s_colsT, s_sums = (k.fresh(n) for n in (
            "step_sums_moved", "step_sums_turned", "step_sums_t_moved", "node_sums_made"))
        with nc.Block() as block:
            @block.vector
            def _(dve):
                v = nc.vector

                def select(i, n):
                    dve.wait_ge(*summed.free(R * i + n + 1, R))
                    at = (R * i + n) * 2 * U
                    v.tensor_tensor(sel[:, n, :, :, :], k.iota_row[:, :].unsqueeze(1).broadcast_to([P, 2 * U, P]),
                                    k.dloc_e[:, ds(at, 2 * U)].unsqueeze(2).broadcast_to([P, 2 * U, P]),
                                    ALU.is_equal).then_inc(selected.sem, 1)
                with dve.Fori(0, ITERS // R) as i:
                    for n in range(R):
                        select(i, n)
                dve.wait_ge(*summed.done(ITERS))
                v.tensor_reduce(cols[:, :], pS[:, 0:STEPS, 0:3], AXX, ALU.add).then_inc(s_cols, 1)
                dve.wait_ge(s_turned, 1)
                v.tensor_copy(colsT[0:HALF, :, :], pT[0:HALF, 0:2, :]).then_inc(s_colsT, 1)
                dve.wait_ge(s_sums, 1)
                v.tensor_copy(k.node_sums[:, :], pT[:, 2, 0:WINDOWS])
                dve.drain()

            @block.tensor
            def _(pe):
                pe.sem_inc(summed.sem, R)

                def total(i, n):
                    pe.wait_ge(*selected.done(R * i + n + 1))
                    for u in range(U):
                        s = (R * i + n) * U + u
                        for j in range(2):
                            last = nc.tensor.matmul(pS[:, ds(s, 1), 0:3], sel[:, n, u, j, :],
                                                    k.parts[:, ds(2 * s + j, 1), :], start=(j == 0), stop=(j == 1))
                    last.then_inc(summed.sem, 1)
                with pe.Fori(0, ITERS // R) as i:
                    for n in range(R):
                        total(i, n)
                pe.wait_ge(s_cols, 1)
                for h in range(2):
                    last = nc.tensor.transpose(pT[0:HALF, h, :], cols[:, h * HALF:(h + 1) * HALF], k.ident[:, :])
                last.then_inc(s_turned, 1)
                pe.wait_ge(s_colsT, 1)
                for h in range(2):
                    last = nc.tensor.matmul(pT[:, 2, 0:WINDOWS], colsT[0:HALF, h, :], k.win_hot[0:HALF, h, :],
                                            start=(h == 0), stop=(h == 1))
                last.then_inc(s_sums, 1)
        k.close(ITERS, selected, summed)


def segment_softmax_phase(nc, k, heads, scale, with_self=False):
    with ExitStack() as ctx:
        def sb(name, shape, dt=F32):
            return ctx.enter_context(nc.sbuf_tensor(k.own(name), shape, dt))

        def pb(name, shape):
            return ctx.enter_context(nc.psum_tensor(k.own(name), shape, F32))
        N = heads + 2 * with_self
        lt = sb("logits_t", [P, N, 2, GROUP])
        m = sb("max_t", [P, heads, 2, GROUP])
        mf = sb("max_fwd_t", [P, heads, 2, GROUP])
        edge = sb("step_ends", [HEADS, 2, STEPS])
        run = sb("running", [HEADS, 2, STEPS])
        carry = sb("carry", [HEADS, 2, STEPS])
        cc = sb("carry_t", [P, 2, 2, HEADS])
        pt = pb("pt", [P, 4, 2, GROUP])
        pr = pb("pr", [P, 512])
        pe_back = pb("pcol", [P, 4, 2, P])
        names = ("sm_turned", "sm_local", "sm_ends", "sm_carry", "sm_carry_turned", "sm_diff", "sm_exp", "sm_exp_turned",
                 "sm_done")
        turned, local, ends, carried, carry_t, diff, exped, exp_turned, back = (k.count(n) for n in names)
        HH = HALF
        with nc.Block() as block:
            @block.tensor
            def _(pe):
                t = nc.tensor
                for n in range(N):
                    src = (k.logits[:, n, :] if n < heads else (k.selfs, k.end_e)[n - heads][:, :])
                    for h in range(2):
                        for j in range(2):
                            last = t.transpose(pt[0:HH, n, h, j * P:(j + 1) * P],
                                               src[:, 2 * HH * h + j:2 * HH * (h + 1):2], k.ident[:, :])
                last.then_inc(turned.sem, 1)
                pe.wait_ge(*local.done(1))
                for a, c in ((0, GROUP - 1), (1, 0)):
                    for h in range(2):
                        last = t.matmul(pr[0:heads, a * STEPS + h * HH:a * STEPS + (h + 1) * HH],
                                        m[0:HH, :, h, c], k.ident[0:HH, 0:HH], start=True, stop=True)
                last.then_inc(ends.sem, 1)
                pe.wait_ge(*carried.done(1))
                for a in range(2):
                    for h in range(2):
                        o = (2 * a + h) * HEADS
                        last = t.matmul(pr[0:HH, o:o + heads], carry[0:heads, a, h * HH:(h + 1) * HH],
                                        k.ident[0:heads, 0:heads], start=True, stop=True)
                last.then_inc(carry_t.sem, 1)
                pe.wait_ge(*exped.done(1))
                M = heads + with_self
                for h in range(2):
                    if h:
                        pe.wait_ge(*back.done(1))
                    for n in range(M):
                        for j in range(2):
                            last = t.transpose(pe_back[:, n, j, 0:HH], lt[0:HH, n, h, j * P:(j + 1) * P],
                                               k.ident[0:HH, 0:HH])
                    last.then_inc(exp_turned.sem, 1)

            @block.vector
            def _(dve):
                v = nc.vector
                dve.wait_ge(*turned.done(1))
                v.tensor_scalar(lt[0:HH], pt[0:HH, 0:N], scale, None, ALU.mult)
                dve.drain()
                top = lt
                if with_self:
                    v.tensor_tensor(mf[0:HH, 0], lt[0:HH, 0], lt[0:HH, 1], ALU.max)
                    dve.drain()
                    v.tensor_copy(m[0:HH, 0], mf[0:HH, 0])
                    dve.drain()
                    top = m
                for n in range(heads):
                    for h in range(2):
                        v.tensor_tensor_scan(mf[0:HH, n, h, :], k.mask_t[0:HH, h, 0:GROUP], top[0:HH, n, h, :], -BIG,
                                             ALU.add, ALU.max)
                dve.drain()
                for n in range(heads):
                    for h in range(2):
                        v.tensor_tensor_scan(m[0:HH, n, h, ::-1], k.mask_t[0:HH, h, GROUP:0:-1], mf[0:HH, n, h, ::-1],
                                             -BIG, ALU.add, ALU.max)
                dve.drain().then_inc(local.sem, 1)
                dve.wait_ge(*ends.done(1))
                v.tensor_copy(edge[0:heads], pr[0:heads, 0:2 * STEPS].rearrange("p (a s) -> p a s", a=2))
                v.memset(carry[0:heads], -BIG)
                dve.drain()
                v.tensor_tensor_scan(run[0:heads, 0, :], k.step_masks[0:heads, 0, :], edge[0:heads, 0, :], -BIG,
                                     ALU.add, ALU.max)
                v.tensor_tensor_scan(run[0:heads, 1, ::-1], k.step_masks[0:heads, 1, ::-1], edge[0:heads, 1, ::-1],
                                     -BIG, ALU.add, ALU.max)
                dve.drain()
                v.tensor_tensor(carry[0:heads, 0, 1:STEPS], run[0:heads, 0, 0:STEPS - 1],
                                k.step_masks[0:heads, 2, 1:STEPS], ALU.add)
                v.tensor_tensor(carry[0:heads, 1, 0:STEPS - 1], run[0:heads, 1, 1:STEPS],
                                k.step_masks[0:heads, 3, 0:STEPS - 1], ALU.add)
                dve.drain().then_inc(carried.sem, 1)
                dve.wait_ge(*carry_t.done(1))
                v.tensor_copy(cc[0:HH, :, :, 0:heads], pr[0:HH, 0:4 * HEADS].rearrange(
                    "p (a h n) -> p a h n", a=2, h=2)[:, :, :, 0:heads])
                for a, seg in enumerate((k.first_t, k.last_t)):
                    dve.drain()
                    for n in range(heads):
                        for h in range(2):
                            v.scalar_tensor_tensor(m[0:HH, n, h, :], seg[0:HH, h, :], cc[0:HH, a, h, n:n + 1],
                                                   m[0:HH, n, h, :], ALU.add, ALU.max)
                dve.drain()
                v.tensor_tensor(lt[0:HH, 0:heads], lt[0:HH, 0:heads], m[0:HH], ALU.subtract)
                if with_self:
                    v.tensor_tensor(lt[0:HH, 1], lt[0:HH, 1], m[0:HH, 0], ALU.subtract)
                dve.drain().then_inc(diff.sem, 1)
                M = heads + with_self
                for h in range(2):
                    dve.wait_ge(*exp_turned.done(h + 1))
                    for n in range(M):
                        out = k.logits[:, n, :] if n < heads else k.selfs[:, :]
                        v.tensor_copy(out[:, 2 * HH * h:2 * HH * (h + 1)].rearrange("p (s j) -> p j s", j=2),
                                      pe_back[:, n, :, 0:HH])
                    dve.drain().then_inc(back.sem, 1)
                if with_self:
                    v.tensor_tensor(k.ends[:, :, 0], k.selfs[:, :], k.end_e[:, :], ALU.mult)
                    v.tensor_copy(k.ends[:, :, 1], k.end_e[:, :])
                    dve.drain()

            @block.scalar
            def _(act):
                act.wait_ge(*diff.done(1))
                nc.scalar.activation(lt[0:HH, 0:heads + with_self], lt[0:HH, 0:heads + with_self], ACT.Exp
                                     ).then_inc(exped.sem, 1)
        k.close(1, turned, local, ends, carried, carry_t, diff, exped)
        k.close(2, back, exp_turned)


def edge_sum_phase(nc, k, table, width, blocks, out_dram=None):
    size = sum(b[2] for b in blocks)
    banks = -(-size // 512)
    bw = size // banks
    weighted = [b for b in blocks if b[0] is not None]
    plain = [b for b in blocks if b[0] is None]
    on_pool = weighted[2:] if table is None else []
    on_dve = weighted[:1] if len(weighted) > 1 and not on_pool else []
    on_act = weighted[len(on_dve):len(weighted) - len(on_pool)]
    wide = sum(b[2] for b in weighted)
    ahead = 3
    with ExitStack() as ctx:
        def sb(name, shape, dt=F32):
            return ctx.enter_context(nc.sbuf_tensor(k.own(name), shape, dt))
        acc = k.sums if out_dram is None else sb("sums", [P, WINDOWS * size])
        sel = sb("selection", [P, U, 2, P])
        idx = sb("staged_src", [P, REPEAT, 2 * U], I32)
        rows = sb("src_rows", [P, U, 2, width])
        msg = sb("weighted_rows", [P, U, 2, size])
        pO = [ctx.enter_context(nc.psum_tensor(k.own(f"window_sum{p}"), [P, banks, 512], F32)) for p in range(U)]
        staged, selected, weighed, summed, added, passed, act_passed = (k.count(n, a) for n, a in (
            ("src_staged", 0), ("selection_made", U), ("rows_weighed", U), ("window_summed", U), ("window_added", U),
            ("pool_passed", 0), ("act_passed", 0)))
        if table is not None:
            arrived = [k.count(f"rows_gathered{u}", 0, 32) for u in range(U)]
        else:
            arrived = [k.count(f"slot_rows_loaded{u}", 0, 16) for u in range(U)]
        sp_passed = k.count("sp_passed")
        pool_weighed, weigh_passed = k.count("pool_rows_weighed", U), k.count("pool_weigh_passed")
        readers = [weighed] + [selected] * bool(on_dve) + [pool_weighed] * bool(on_pool)
        s_out = k.count("sums_stored", 0, 16)
        with nc.Block() as block:
            if table is not None:
                @block.gpsimd
                def _(pool):
                    gather_rows(nc, k, pool, idx, rows, width, table, staged, passed, readers, arrived)

            if on_pool:
                @block.gpsimd
                def _(pool):
                    pool.sem_inc(pool_weighed.sem, U)

                    def weigh(i):
                        for u in range(U):
                            pool.wait_ge(*arrived[u].done(i + 1))
                            pool.sem_inc(weigh_passed.sem)
                            pool.wait_ge(*summed.free(U * i + u + 1, U))
                            pool.sem_inc(weigh_passed.sem)
                            at = wide - sum(b[2] for b in on_pool)
                            for weight, col, n in on_pool:
                                each = weight[:, ds(U * 2 * i + 2 * u, 2)].unsqueeze(2).broadcast_to([P, 2, n])
                                last = nc.gpsimd.tensor_tensor(msg[:, u, :, at:at + n], rows[:, u, :, col:col + n], each,
                                                               ALU.mult)
                                at += n
                            last.then_inc(pool_weighed.sem, 1)
                    repeat(pool, ITERS, REPEAT, weigh)

            @block.scalar
            def _(act):
                act.sem_inc(weighed.sem, U)

                def weigh(i):
                    for u in range(U):
                        act.wait_ge(*arrived[u].done(i + 1))
                        act.wait_ge(*summed.free(U * i + u + 1, U))
                        act.sem_inc(act_passed.sem)
                        for j in range(2):
                            at = sum(b[2] for b in on_dve)
                            for weight, col, n in on_act:
                                last = nc.scalar.activation(msg[:, u, j, at:at + n], rows[:, u, j, col:col + n],
                                                            ACT.Copy, scale=weight[:, ds(U * 2 * i + 2 * u + j, 1)])
                                at += n
                        for _, values, n in plain:
                            last = nc.scalar.copy(msg[:, u, :, wide:wide + n], values[:, ds(U * 2 * i + 2 * u, 2), :])
                        last.then_inc(weighed.sem, 1)
                repeat(act, ITERS, REPEAT, weigh)

            @block.vector
            def _(dve):
                v = nc.vector
                v.memset(acc[:, :], 0.0)
                dve.sem_inc(selected.sem, U)
                dve.sem_inc(added.sem, U)

                def prepare(i, u):
                    dve.wait_ge(*summed.free(U * i + u + 1, U))
                    last = v.tensor_tensor(sel[:, u, :, :], k.iota_row[:, :].unsqueeze(1).broadcast_to([P, 2, P]),
                                           k.dloc_e[:, ds(U * 2 * i + 2 * u, 2)].unsqueeze(2).broadcast_to([P, 2, P]),
                                           ALU.is_equal)
                    if on_dve:
                        dve.wait_ge(*arrived[u].done(i + 1))
                        for j in range(2):
                            for weight, col, n in on_dve:
                                last = v.tensor_scalar(msg[:, u, j, 0:n], rows[:, u, j, col:col + n],
                                                       weight[:, ds(U * 2 * i + 2 * u + j, 1)], None, ALU.mult)
                    last.then_inc(selected.sem, 1)

                def add(i, u, win):
                    dve.drain()
                    dve.wait_ge(*summed.done(U * i + u + 1))
                    a = acc[:, ds(win[u] * size, size)].rearrange("p (b n) -> p b n", b=banks)
                    v.tensor_tensor(a, a, pO[u][:, :, 0:bw], ALU.add).then_inc(added.sem, 1)

                for u in range(ahead):
                    prepare(0, u)

                def steps(i):
                    win = windows_of(dve, k, i)
                    for u in range(U):
                        prepare(i + (u + ahead) // U, (u + ahead) % U)
                        add(i, u, win)
                repeat(dve, ITERS - 1, REPEAT, steps)
                win = windows_of(dve, k, ITERS - 1)
                for u in range(U):
                    if u + ahead < U:
                        prepare(ITERS - 1, u + ahead)
                    add(ITERS - 1, u, win)

            @block.tensor
            def _(pe):
                pe.sem_inc(summed.sem, U)

                def steps(i):
                    for u in range(U):
                        pe.wait_ge(*selected.done(U * i + u + 1))
                        pe.wait_ge(*weighed.done(U * i + u + 1))
                        if on_pool:
                            pe.wait_ge(*pool_weighed.done(U * i + u + 1))
                        pe.wait_ge(*added.free(U * i + u + 1, U))
                        for b in range(banks):
                            for j in range(2):
                                last = nc.tensor.matmul(pO[u][:, b, 0:bw], sel[:, u, j, :],
                                                        msg[:, u, j, b * bw:(b + 1) * bw],
                                                        start=(j == 0), stop=(j == 1))
                        last.then_inc(summed.sem, 1)
                repeat(pe, ITERS, REPEAT, steps)

            @block.sync
            def _(sp):
                if table is None:
                    with sp.Fori(0, ITERS) as i:
                        for u in range(U):
                            for c in readers:
                                sp.wait_ge(*c.free(U * i + u + 1, U))
                                sp.sem_inc(sp_passed.sem)
                            sp.dma_start(rows[:, u].rearrange("p j d -> p (j d)"),
                                         k.slots_dram[:, ds((U * i + u) * 2 * width, 2 * width)]
                                         ).then_inc(arrived[u].sem, 16)
                if out_dram is not None:
                    sp.wait_ge(*added.done(STEPS))
                    sp.dma_start(out_dram[:, 0:WINDOWS * size], acc[:, :]).then_inc(s_out.sem, 16)
                    sp.wait_ge(*s_out.done(1))
        k.close(STEPS, selected, summed, added, weighed, act_passed)
        if on_pool:
            k.close(STEPS, pool_weighed)
        if table is not None:
            k.close(ITERS, staged, passed)
        k.close(ITERS, *arrived)
        if out_dram is not None:
            k.close(1, s_out)


def conv_mid_phase(nc, k):
    H = HEADS
    with ExitStack() as ctx:
        def sb(name, shape, dt=F32):
            return ctx.enter_context(nc.sbuf_tensor(k.own(name), shape, dt))

        def pb(name, shape):
            return ctx.enter_context(nc.psum_tensor(k.own(name), shape, F32))
        wv = sb("wv0", [D, H, D])
        ws = sb("ws0", [D, H, D])
        bs = sb("bs0", [D, H])
        bv = sb("bv0_block", [H, H, D])
        w2 = sb("w_qkv1", [D, 3, H, HD])
        ws1 = sb("ws1", [D, H, D])
        b2 = sb("b_qkv1", [P, 3, HD])
        bs1 = sb("bs1", [P, D])
        agg = sb("agg", [P, CH, H, D + 1])
        den = sb("den", [P, CH, H])
        ratio = sb("ratio", [P, CH, H])
        ratioT = sb("ratioT", [H, CH, D])
        aggT = [sb(f"aggT{n}", [P, CH, D]) for n in range(2)]
        hc = sb("h", [P, CH, D])
        hT = sb("hT", [P, CH, D])
        h1T = sb("h1T", [P, H, CH, D])
        work = k.logits[:, :, :].rearrange("p h t -> p (h t)")
        q = work[:, 0:HD]
        kk = work[:, HD:2 * HD]
        vv = work[:, 2 * HD:2 * HD + HW1].rearrange("p (h d) -> p h d", h=H)
        pA = [pb(f"pA{n}", [P, 8, D]) for n in range(2)]
        pB = pb("pB", [P, 8, D])
        pX = [pb(f"pX{n}", [P, 512]) for n in range(2)]
        s_w = k.fresh("weights_conv2")
        s_bv = k.fresh("bias_block_cleared")
        names = ("agg_scaled", "aggT_ready", "aggT_made", "h1_product", "h1_made", "ratio_turned", "ratio_made")
        scaled, a_turned, aT_made, h1_prod, h1_made, r_turned, r_made = (k.count(n) for n in names)
        agg_in = k.count("agg_loaded", 0, 16)
        prods = [k.count(f"proj{n}_product") for n in range(4)]
        used = [k.count(f"proj{n}_used", 1) for n in range(4)]
        stored = [k.count(f"{n}_rows_stored", 1, 16) for n in ("k", "v")]
        with nc.Block() as block:
            @block.sync
            def _(sp):
                with nc.allow_non_contiguous_dma(reason="small columns of biases"):
                    for out, src in (
                            (wv[:, :, :], k.L1_gnn_Wv0.rearrange("p (h n) -> p h n", n=D)),
                            (ws[:, :, :], k.L1_gnn_Ws0.rearrange("p (h n) -> p h n", n=D)),
                            (bs[:, :], k.L1_gnn_bs0.rearrange("(h p) -> p h", p=D)),
                            (ws1[:, :, :], k.L1_gnn_Ws1.rearrange("(c p) n -> p c n", p=D)),
                            (bs1[:, :], k.L1_gnn_bs1.rearrange("(o n) -> o n", o=1).partition_broadcast(P))):
                        sp.dma_start(out, src).then_inc(s_w, 16)
                    for n, (w, b) in enumerate(((k.L1_gnn_Wq1, k.L1_gnn_bq1), (k.L1_gnn_Wk1, k.L1_gnn_bk1),
                                                (k.L1_gnn_Wv1, k.L1_gnn_bv1))):
                        sp.dma_start(w2[:, n, :, :], w.rearrange("(c p) n -> p c n", p=D)).then_inc(s_w, 16)
                        sp.dma_start(b2[:, n, :], b.rearrange("(o n) -> o n", o=1).partition_broadcast(P)).then_inc(s_w, 16)
                    sp.wait_ge(s_bv, 1)
                    for h in range(H):
                        sp.dma_start(bv[h:h + 1, h, :], k.L1_gnn_bv0.rearrange("(h n) -> h n", n=D)[h:h + 1, :])\
                          .then_inc(s_w, 16)

                def load_sums(i):
                    sp.dma_start(agg[:, :, :, :], k.sums_dram[:, ds(i * CH * HW1, CH * HW1)]).then_inc(agg_in.sem, 16)

                def store_rows(i):
                    for c in range(CH):
                        for n, (src, dram) in enumerate(((kk[:, :], k.k_dram), (vv[:, :, :], k.v_dram))):
                            sp.wait_ge(*used[1 + n].done(CH * i + c + 1))
                            sp.dma_start(dram[ds((i * CH + c) * P, P), :], src).then_inc(stored[n].sem, 16)
                load_sums(0)
                with sp.Fori(0, CHUNKS - 1) as i:
                    sp.wait_ge(*a_turned.done(5 * i + 5))
                    load_sums(i + 1)
                    store_rows(i)
                store_rows(CHUNKS - 1)
                for n in range(2):
                    sp.wait_ge(*stored[n].done(WINDOWS))

            @block.vector
            def _(dve):
                v = nc.vector
                v.memset(bv[:, :, :], 0.0).then_inc(s_bv, 1)
                v.memset(vv[:, :, D:D + 1], 1.0)
                for n in range(2):
                    dve.sem_inc(stored[n].sem, 16)
                for n in range(4):
                    dve.sem_inc(used[n].sem)
                dve.wait_ge(s_w, 16 * 15)

                def scale(i):
                    dve.wait_ge(*agg_in.done(i + 1))
                    v.tensor_copy(hc[:, :, :], chunk(k.H, i))
                    v.tensor_scalar(den[:, :, :], agg[:, :, :, D], 1.0e-16, None, ALU.add)
                    dve.drain()
                    v.reciprocal(den[:, :, :], den[:, :, :])
                    dve.drain()
                    v.tensor_tensor(ratio[:, :, :], agg[:, :, :, D], den[:, :, :], ALU.mult)
                    for h in range(H):
                        v.tensor_tensor(agg[:, :, h, 0:D], agg[:, :, h, 0:D],
                                        den[:, :, h:h + 1].broadcast_to([P, CH, D]), ALU.mult)
                    dve.drain().then_inc(scaled.sem, 1)

                def rows_out(i, c):
                    dve.wait_ge(*prods[0].done(CH * i + c + 1))
                    v.tensor_tensor(q[:, :], pX[0][:, :], b2[:, 0, :], ALU.add)
                    dve.drain().then_inc(used[0].sem, 1)
                    part = [k.U[:, ds(i * (CH * 3 * HD) + (3 * c + n) * HD, HD)] for n in range(3)]
                    split3(dve, nc, q[:, :], *part, q[:, :])
                    dve.drain()
                    dve.wait_ge(*prods[1].done(CH * i + c + 1))
                    dve.wait_ge(*stored[0].free(CH * i + c + 1, 1))
                    v.tensor_tensor(kk[:, :], pX[1][:, :], b2[:, 1, :], ALU.add).then_inc(used[1].sem, 1)
                    dve.wait_ge(*prods[2].done(CH * i + c + 1))
                    dve.wait_ge(*stored[1].free(CH * i + c + 1, 1))
                    v.tensor_tensor(vv[:, :, 0:D], pX[0][:, :].rearrange("p (h d) -> p h d", h=H),
                                    b2[:, 2, :].rearrange("p (h d) -> p h d", h=H), ALU.add).then_inc(used[2].sem, 1)
                    dve.wait_ge(*prods[3].done(CH * i + c + 1))
                    v.tensor_tensor(k.G[:, ds(i * CH + c, 1), :].rearrange("p o d -> p (o d)"), pX[1][:, 0:D],
                                    bs1[:, :], ALU.add).then_inc(used[3].sem, 1)
                scale(0)
                with dve.Fori(0, CHUNKS - 1) as i:
                    for c in range(CH):
                        rows_out(i, c)
                        if c == 1:
                            scale(i + 1)
                for c in range(CH):
                    rows_out(CHUNKS - 1, c)

            @block.scalar
            def _(act):
                s = nc.scalar
                act.wait_ge(s_w, 16 * 15)
                with act.Fori(0, CHUNKS) as i:
                    act.wait_ge(*a_turned.done(5 * i + 1))
                    s.copy(hT[:, :, :], pA[1][:, 0:CH, :]).then_inc(aT_made.sem, 1)
                    act.wait_ge(*r_turned.done(i + 1))
                    s.copy(ratioT[:, :, :], pB[0:H, 0:CH, :]).then_inc(r_made.sem, 1)
                    for h in range(H + 1):
                        if h < H:
                            act.wait_ge(*a_turned.done(5 * i + h + 2))
                            s.copy(aggT[h % 2][:, :, :], pA[h % 2][:, 0:CH, :]).then_inc(aT_made.sem, 1)
                        if h:
                            act.wait_ge(*h1_prod.done(H * i + h))
                            s.activation(h1T[:, h - 1, :, :], pB[:, 0:CH, :], ACT.Relu, bias=bs[:, h - 1:h])\
                             .then_inc(h1_made.sem, 1)

            @block.tensor
            def _(pe):
                t = nc.tensor

                def wide(out, lhsT, rhs, start, stop):
                    t.matmul(out[:, 0:4, :], lhsT, rhs[:, 0:4, :], start=start, stop=stop)
                    return t.matmul(out[:, 4:CH, :], lhsT, rhs[:, 4:CH, :], start=start, stop=stop)

                def turn(i, h):
                    for c in range(CH):
                        last = t.transpose(pA[h % 2][:, c, :], agg[:, c, h, 0:D], k.ident[:, :])
                    last.then_inc(a_turned.sem, 1)

                pe.wait_ge(s_w, 16 * 15)
                with pe.Fori(0, CHUNKS) as i:
                    pe.wait_ge(*scaled.done(i + 1))
                    for c in range(CH):
                        last = t.transpose(pA[1][:, c, :], hc[:, c, :], k.ident[:, :])
                    last.then_inc(a_turned.sem, 1)
                    for c in range(CH):
                        last = t.matmul(pB[0:H, c, :], ratio[:, c, :], k.ident[:, :], start=True, stop=True)
                    last.then_inc(r_turned.sem, 1)
                    turn(i, 0)
                    pe.wait_ge(*aT_made.done(5 * i + 1))
                    turn(i, 1)
                    pe.wait_ge(*r_made.done(i + 1))
                    for h in range(H):
                        pe.wait_ge(*aT_made.done(5 * i + h + 2))
                        if h:
                            pe.wait_ge(*h1_made.done(H * i + h))
                        wide(pB, wv[:, h, :], aggT[h % 2], True, False)
                        wide(pB, ws[:, h, :], hT, False, False)
                        wide(pB, bv[:, h, :], ratioT, False, True).then_inc(h1_prod.sem, 1)
                        if h + 2 < H:
                            turn(i, h + 2)
                    pe.wait_ge(*h1_made.done(H * i + H))
                    for c in range(CH):
                        for n in range(4):
                            pe.wait_ge(*(used[n - 2].done(CH * i + c + 1) if n >= 2 else
                                         used[n + 2].free(CH * i + c + 1, 1)))
                            for kc in range(H):
                                rhs = w2[:, n, kc, :] if n < 3 else ws1[:, kc, :]
                                last = t.matmul(pX[n % 2][:, 0:rhs.shape[1]], h1T[:, kc, c, :], rhs,
                                                start=(kc == 0), stop=(kc == H - 1))
                            last.then_inc(prods[n].sem, 1)
        k.close(CHUNKS, scaled, r_turned, r_made, agg_in)
        k.close(5 * CHUNKS, a_turned, aT_made)
        k.close(H * CHUNKS, h1_prod, h1_made)
        k.close(WINDOWS, *prods, *used, *stored)


def conv2_out_phase(nc, k):
    H = HEADS
    with ExitStack() as ctx:
        den = ctx.enter_context(nc.sbuf_tensor(k.own("den"), [P, CH, H], F32))
        t = ctx.enter_context(nc.sbuf_tensor(k.own("scaled_sums"), [P, CH, H, D], F32))
        with nc.Block() as block:
            @block.vector
            def _(dve):
                v = nc.vector
                with dve.Fori(0, CHUNKS) as i:
                    agg = k.sums[:, ds(i * CH * HW1, CH * HW1)].rearrange("p (c h d) -> p c h d", c=CH, h=H)
                    v.tensor_scalar(den[:, :, :], agg[:, :, :, D], 1.0e-16, None, ALU.add)
                    dve.drain()
                    v.reciprocal(den[:, :, :], den[:, :, :])
                    dve.drain()
                    v.tensor_scalar(den[:, :, :], den[:, :, :], 1.0 / H, None, ALU.mult)
                    dve.drain()
                    for h in range(H):
                        v.tensor_tensor(t[:, :, h, :], agg[:, :, h, 0:D], den[:, :, h:h + 1].broadcast_to([P, CH, D]),
                                        ALU.mult)
                    dve.drain()
                    v.tensor_tensor(t[:, :, 0:2, :], t[:, :, 0:2, :], t[:, :, 2:4, :], ALU.add)
                    dve.drain()
                    v.tensor_tensor(t[:, :, 0, :], t[:, :, 0, :], t[:, :, 1, :], ALU.add)
                    v.tensor_tensor(t[:, :, 2, :], chunk(k.X, i), chunk(k.G, i), ALU.add)
                    dve.drain()
                    v.tensor_tensor(chunk(k.X, i), t[:, :, 0, :], t[:, :, 2, :], ALU.add)
                    dve.drain()


def gat_in_phase(nc, k):
    with ExitStack() as ctx:
        def sb(name, shape, dt=F32):
            return ctx.enter_context(nc.sbuf_tensor(k.own(name), shape, dt))

        def pb(name):
            return ctx.enter_context(nc.psum_tensor(k.own(name), [P, 8, D], F32))
        wl = sb("wl", [D, D])
        wr = sb("wr", [D, D])
        w = Scratch(nc, sb, "n3", k.eps5)
        h = sb("h", [P, CH, D])
        hT = sb("hT", [P, CH, D])
        xl = sb("xl", [P, CH, D + 4])
        xr = sb("xr", [P, CH, D + 1])
        m = sb("m", [P, CH, D])
        lk = sb("lk", [P, CH, D])
        rest = sb("rest", [P, CH, D + 1])
        pT, pL, pR = pb("pT"), pb("pL"), pb("pR")
        s_w = k.fresh("weights_gat")
        var, sd, h_made, turned, hT_made, prod, made = (k.count(n) for n in (
            "var_made", "sd_made", "h_made", "h_turned", "hT_made", "g_product", "g_made"))
        out, moved = k.count("rows_stored_chunk", 1, 16), k.count("product_moved", 1)
        with nc.Block() as block:
            @block.sync
            def _(sp):
                sp.dma_start(wl[:, :], k.L2_gnn_W_l).then_inc(s_w, 16)
                sp.dma_start(wr[:, :], k.L2_gnn_W_r).then_inc(s_w, 16)
                sp.dma_start(k.att[:, :], k.L2_gnn_att.rearrange("(o n) -> o n", o=1).partition_broadcast(P)).then_inc(s_w, 16)
                with sp.Fori(0, CHUNKS) as i:
                    sp.wait_ge(*made.done(i + 1))
                    sp.dma_start(rows_of(k.h_dram, i, D + 4), xl[:, :, :]).then_inc(out.sem, 16)
                sp.wait_ge(*out.done(CHUNKS))

            @block.vector
            def _(dve):
                v = nc.vector
                dve.wait_ge(s_w, 48)
                dve.sem_inc(out.sem, 16)
                dve.sem_inc(moved.sem)
                v.memset(xl[:, :, D:D + 4], 1.0)

                def normed(i, first=False):
                    norm_head(dve, chunk(k.X, i), w, var)
                    if not first:
                        dve.wait_ge(*turned.done(i))
                    norm_tail(dve, w, h[:, :, :], sd, i + 1)
                    v.tensor_scalar(h[:, :, :], h[:, :, :], 0.0, None, ALU.max).then_inc(h_made.sem, 1)

                def take(i):
                    dve.wait_ge(*prod.done(i + 1))
                    dve.wait_ge(*out.free(i + 1, 1))
                    v.tensor_copy(xl[:, :, 0:D], pL[:, 0:CH, :])
                    v.tensor_copy(xr[:, :, 0:D], pR[:, 0:CH, :])
                    dve.drain().then_inc(made.sem, 1)
                    dve.sem_inc(moved.sem)
                    v.tensor_copy(chunk(k.H, i), xl[:, :, 0:D])
                    v.tensor_tensor(m[:, :, :], xl[:, :, 0:D], xr[:, :, 0:D], ALU.add)
                    dve.drain()
                    v.scalar_tensor_tensor(lk[:, :, :], m[:, :, :], 0.2, m[:, :, :], ALU.mult, ALU.max)
                    dve.drain()
                    v.tensor_tensor(m[:, :, :], lk[:, :, :], over_rows(k.att[:, :]), ALU.mult)
                    dve.drain()
                    v.tensor_reduce(xr[:, :, D], m[:, :, :], AXX, ALU.add)
                    dve.drain()
                    u = k.U[:, ds(i * (CH * 3 * (D + 1)), CH * 3 * (D + 1))].rearrange("p (c n d) -> p c n d", c=CH, n=3)
                    split3(dve, nc, xr[:, :, :], u[:, :, 0, :], u[:, :, 1, :], u[:, :, 2, :], rest[:, :, :])
                    dve.drain()
                normed(0, first=True)
                with dve.Fori(0, CHUNKS - 1) as i:
                    normed(i + 1)
                    take(i)
                take(CHUNKS - 1)

            @block.scalar
            def _(act):
                def turn(i):
                    act.wait_ge(*turned.done(i + 1))
                    nc.scalar.copy(hT[:, :, :], pT[:, 0:CH, :]).then_inc(hT_made.sem, 1)
                norm_sqrt(act, nc, w, var, sd, 1)
                with act.Fori(0, CHUNKS - 1) as i:
                    turn(i)
                    norm_sqrt(act, nc, w, var, sd, i + 2)
                turn(CHUNKS - 1)

            @block.tensor
            def _(pe):
                pe.wait_ge(s_w, 48)
                with pe.Fori(0, CHUNKS) as i:
                    pe.wait_ge(*h_made.done(i + 1))
                    for c in range(CH):
                        last = nc.tensor.transpose(pT[:, c, :], h[:, c, :], k.ident[:, :])
                    last.then_inc(turned.sem, 1)
                    pe.wait_ge(*hT_made.done(i + 1))
                    pe.wait_ge(*moved.free(i + 1, 1))
                    for c in range(CH):
                        nc.tensor.matmul(pL[:, c, :], hT[:, c, :], wl[:, :], start=True, stop=True)
                        last = nc.tensor.matmul(pR[:, c, :], hT[:, c, :], wr[:, :], start=True, stop=True)
                    last.then_inc(prod.sem, 1)
        k.close(CHUNKS, var, sd, h_made, turned, hT_made, prod, made, out, moved)


def gat_out_phase(nc, k):
    S = D + 3
    with ExitStack() as ctx:
        def sb(name, shape, dt=F32):
            return ctx.enter_context(nc.sbuf_tensor(k.own(name), shape, dt))
        sums = k.sums[:, :].rearrange("p (w n) -> p w n", n=S)
        bc = sb("rows_bc", [P, 3, D])
        own = sb("own", [P, WINDOWS])
        den = sb("den", [P, WINDOWS])
        o = sb("o", [P, WINDOWS, D])
        t = sb("t", [P, WINDOWS, D])
        part = sb("part", [P, WINDOWS])
        tot = sb("tot", [P, 1])
        valid = sb("valid", [P, 1])
        ones = sb("ones", [P, P])
        mu = sb("mu", [P, 1])
        sd = sb("sd_all", [P, 1])
        pS = ctx.enter_context(nc.psum_tensor(k.own("pS"), [P, 512], F32))
        s_in = k.fresh("gat_out_loaded")
        s_part = k.fresh("partition_sums")
        s_all = k.fresh("whole_sums")
        s_sd = k.fresh("whole_sd")
        over = lambda row: row.unsqueeze(1).broadcast_to([P, WINDOWS, D])
        each = lambda col: col.unsqueeze(2).broadcast_to([P, WINDOWS, D])
        with nc.Block() as block:
            @block.sync
            def _(sp):
                for n, row in enumerate((k.L2_gnn_bias, k.L2_gnn_ln_w, k.L2_gnn_ln_b)):
                    sp.dma_start(bc[:, n, :], row.rearrange("(o n) -> o n", o=1).partition_broadcast(P)).then_inc(s_in, 16)

            @block.vector
            def _(dve):
                v = nc.vector

                def total(src, value):
                    v.tensor_reduce(part[:, :], src, AXX, ALU.add)
                    dve.drain()
                    v.tensor_tensor(part[:, WINDOWS - 1:WINDOWS], part[:, WINDOWS - 1:WINDOWS], valid[:, :], ALU.mult)
                    dve.drain()
                    v.tensor_reduce(tot[:, :], part[:, :], AXX, ALU.add).then_inc(s_part, 1)
                    dve.wait_ge(s_all, value)
                v.memset(ones[:, :], 1.0)
                v.tensor_scalar(valid[:, :], k.iota_p[:, :], float(LAST), None, ALU.is_lt)
                dve.wait_ge(s_in, 48)
                v.tensor_scalar(own[:, :], sums[:, :, D + 2], -1.0, 1.0, ALU.mult, ALU.add)
                dve.drain()
                v.tensor_tensor(own[:, :], own[:, :], sums[:, :, D + 1], ALU.add)
                dve.drain()
                v.tensor_tensor(den[:, :], own[:, :], sums[:, :, D], ALU.add)
                v.tensor_tensor(t[:, :, :], k.H[:, :, :], each(own[:, :]), ALU.mult)
                dve.drain()
                v.reciprocal(den[:, :], den[:, :])
                v.tensor_tensor(t[:, :, :], t[:, :, :], sums[:, :, 0:D], ALU.add)
                dve.drain()
                v.tensor_tensor(t[:, :, :], t[:, :, :], each(den[:, :]), ALU.mult)
                dve.drain()
                v.tensor_tensor(t[:, :, :], t[:, :, :], over(bc[:, 0, :]), ALU.add)
                dve.drain()
                v.scalar_tensor_tensor(o[:, :, :], t[:, :, :], 0.01, t[:, :, :], ALU.mult, ALU.max)
                dve.drain()
                total(o[:, :, :], 1)
                v.tensor_scalar(mu[:, :], pS[:, 0:1], 1.0 / (NODES * D), None, ALU.mult)
                dve.drain()
                v.tensor_scalar(o[:, :, :], o[:, :, :], mu[:, 0:1], None, ALU.subtract)
                dve.drain()
                v.tensor_tensor(t[:, :, :], o[:, :, :], o[:, :, :], ALU.mult)
                dve.drain()
                total(t[:, :, :], 2)
                dve.wait_ge(s_sd, 1)
                v.tensor_scalar(sd[:, :], sd[:, :], 1.0e-5, None, ALU.add)
                dve.drain()
                v.reciprocal(sd[:, :], sd[:, :])
                dve.drain()
                v.scalar_tensor_tensor(t[:, :, :], o[:, :, :], sd[:, 0:1], over(bc[:, 1, :]), ALU.mult, ALU.mult)
                dve.drain()
                v.tensor_tensor(t[:, :, :], t[:, :, :], over(bc[:, 2, :]), ALU.add)
                dve.drain()
                v.tensor_tensor(k.X[:, :, :], k.X[:, :, :], t[:, :, :], ALU.add)
                dve.drain()

            @block.tensor
            def _(pe):
                for n in range(2):
                    pe.wait_ge(s_part, n + 1)
                    nc.tensor.matmul(pS[:, n:n + 1], ones[:, :], tot[:, :], start=True, stop=True).then_inc(s_all, 1)

            @block.scalar
            def _(act):
                act.wait_ge(s_all, 2)
                nc.scalar.activation(sd[:, :], pS[:, 1:2], ACT.Sqrt, scale=1.0 / (NODES * D)).then_inc(s_sd, 1)


def last_in_phase(nc, k):
    with ExitStack() as ctx:
        def sb(name, shape, dt=F32):
            return ctx.enter_context(nc.sbuf_tensor(k.own(name), shape, dt))

        def pb(name):
            return ctx.enter_context(nc.psum_tensor(k.own(name), [P, 8, D], F32))
        w3 = sb("w3", [D, D])
        w3T = sb("w3T", [D, D])
        bc = sb("rows_bc", [P, 3, D])
        w = Scratch(nc, sb, "n4", k.eps5)
        h = sb("h", [P, CH, D])
        hT = sb("hT", [P, CH, D])
        tt = sb("tt", [P, CH, D])
        m = sb("m", [P, CH, 2, D])
        vals = sb("vals", [P, CH, 2])
        rest = sb("rest", [P, CH])
        pT, pL = pb("pT"), pb("pL")
        moved = k.count("product_moved", 1)
        s_w = k.fresh("weights_last")
        s_t = k.fresh("w3_turned")
        s_wT = k.fresh("w3T_made")
        var, sd, h_made, turned, hT_made, prod = (k.count(n) for n in (
            "var_made", "sd_made", "h_made", "h_turned", "hT_made", "g_product"))
        with nc.Block() as block:
            @block.sync
            def _(sp):
                sp.dma_start(w3[:, :], k.L3_gnn_W).then_inc(s_w, 16)
                for n, row in enumerate((k.L3_gnn_b.rearrange("(o n) -> o n", o=1), k.L3_gnn_att_w[:, 0:D],
                                         k.L3_gnn_att_w[:, D:2 * D])):
                    sp.dma_start(bc[:, n, :], row.partition_broadcast(P)).then_inc(s_w, 16)

            @block.vector
            def _(dve):
                v = nc.vector
                dve.sem_inc(moved.sem)
                dve.wait_ge(s_t, 1)
                v.tensor_copy(w3T[:, :], pT[:, 0, :]).then_inc(s_wT, 1)

                def normed(i, first=False):
                    norm_head(dve, chunk(k.X, i), w, var)
                    if not first:
                        dve.wait_ge(*turned.done(i))
                    norm_tail(dve, w, h[:, :, :], sd, i + 1)
                    v.tensor_scalar(h[:, :, :], h[:, :, :], 0.0, None, ALU.max).then_inc(h_made.sem, 1)
                    dve.drain()
                    v.tensor_copy(chunk(k.H, i), h[:, :, :])

                def take(i):
                    dve.wait_ge(*prod.done(i + 1))
                    v.tensor_tensor(tt[:, :, :], pL[:, 0:CH, :], over_rows(bc[:, 0, :]), ALU.add)
                    dve.drain().then_inc(moved.sem, 1)
                    for n in range(2):
                        v.tensor_tensor(m[:, :, n, :], tt[:, :, :], over_rows(bc[:, 1 + n, :]), ALU.mult)
                    dve.drain()
                    v.tensor_reduce(vals[:, :, :], m[:, :, :, :], AXX, ALU.add)
                    dve.drain()
                    split3(dve, nc, vals[:, :, 0], *(k.V[:, n, ds(i * CH, CH)] for n in range(3)), rest[:, :])
                    dve.drain()
                    u = k.U[:, ds(i * (CH * 3), CH * 3)].rearrange("p (c n) -> p c n", c=CH)
                    split3(dve, nc, vals[:, :, 1], u[:, :, 0], u[:, :, 1], u[:, :, 2], rest[:, :])
                    dve.drain()
                normed(0, first=True)
                with dve.Fori(0, CHUNKS - 1) as i:
                    normed(i + 1)
                    take(i)
                take(CHUNKS - 1)

            @block.scalar
            def _(act):
                def turn(i):
                    act.wait_ge(*turned.done(i + 1))
                    nc.scalar.copy(hT[:, :, :], pT[:, 0:CH, :]).then_inc(hT_made.sem, 1)
                norm_sqrt(act, nc, w, var, sd, 1)
                with act.Fori(0, CHUNKS - 1) as i:
                    turn(i)
                    norm_sqrt(act, nc, w, var, sd, i + 2)
                turn(CHUNKS - 1)

            @block.tensor
            def _(pe):
                pe.wait_ge(s_w, 64)
                nc.tensor.transpose(pT[:, 0, :], w3[:, :], k.ident[:, :]).then_inc(s_t, 1)
                pe.wait_ge(s_wT, 1)
                with pe.Fori(0, CHUNKS) as i:
                    pe.wait_ge(*h_made.done(i + 1))
                    for c in range(CH):
                        last = nc.tensor.transpose(pT[:, c, :], h[:, c, :], k.ident[:, :])
                    last.then_inc(turned.sem, 1)
                    pe.wait_ge(*hT_made.done(i + 1))
                    pe.wait_ge(*moved.free(i + 1, 1))
                    for c in range(CH):
                        last = nc.tensor.matmul(pL[:, c, :], hT[:, c, :], w3T[:, :], start=True, stop=True)
                    last.then_inc(prod.sem, 1)
        k.close(CHUNKS, var, sd, h_made, turned, hT_made, prod, moved)


CAP = 1.0e36
TINY = 1.1754944e-38
SHRINK = 2.0 ** -30


def last_weights_phase(nc, k):
    with ExitStack() as ctx:
        a = ctx.enter_context(nc.sbuf_tensor(k.own("leaky"), [P, TILES], F32))
        z = ctx.enter_context(nc.sbuf_tensor(k.own("normal"), [P, TILES], F32))
        s_l = k.fresh("leaky_made")
        s_e = k.fresh("weights_made")
        with nc.Block() as block:
            @block.vector
            def _(dve):
                v = nc.vector
                lg = k.logits[:, 0, :]
                v.scalar_tensor_tensor(a[:, :], lg, 0.2, lg, ALU.mult, ALU.max)
                dve.drain()
                v.tensor_scalar(a[:, :], a[:, :], 88.0, -100.0, ALU.min, ALU.max).then_inc(s_l, 1)
                dve.wait_ge(s_e, 1)
                v.tensor_scalar(z[:, :], a[:, :], TINY, None, ALU.is_ge)
                v.tensor_scalar(a[:, :], a[:, :], CAP, None, ALU.min)
                dve.drain()
                v.tensor_tensor(a[:, :], a[:, :], z[:, :], ALU.mult)
                dve.drain()
                split3(dve, nc, a[:, :], k.parts[:, :, 0], k.parts[:, :, 1], k.parts[:, :, 2], a[:, :])
                dve.drain()

            @block.scalar
            def _(act):
                act.wait_ge(s_l, 1)
                nc.scalar.activation(a[:, :], a[:, :], ACT.Exp).then_inc(s_e, 1)


def last_out_phase(nc, k, out):
    with ExitStack() as ctx:
        def sb(name, shape, dt=F32):
            return ctx.enter_context(nc.sbuf_tensor(k.own(name), shape, dt))
        n = sb("n_sum", [P, WINDOWS])
        z = sb("n_zero", [P, WINDOWS])
        y = sb("y", [P, WINDOWS, D])
        t = sb("t", [P, WINDOWS, D])
        ms = sb("ms", [P, WINDOWS])
        ok = sb("ok", [P, WINDOWS])
        sd = sb("sd_last", [P, WINDOWS])
        bc = sb("rows_bc", [P, 2, D])
        s_in = k.fresh("last_loaded_sums")
        s_ms = k.fresh("mean_square_made")
        s_sd = k.fresh("rms_made")
        s_y = k.fresh("result_made")
        s_out = k.fresh("result_stored")
        over = lambda row: row.unsqueeze(1).broadcast_to([P, WINDOWS, D])
        each = lambda col: col.unsqueeze(2).broadcast_to([P, WINDOWS, D])
        with nc.Block() as block:
            @block.sync
            def _(sp):
                for j, row in enumerate((k.L3_gnn_norm_w, k.L3_gnn_norm_b)):
                    sp.dma_start(bc[:, j, :], row.rearrange("(o n) -> o n", o=1).partition_broadcast(P)).then_inc(s_in, 16)
                sp.wait_ge(s_y, 1)
                sp.dma_start(out[0:(WINDOWS - 1) * P, :].rearrange("(w p) d -> p w d", p=P), y[:, 0:WINDOWS - 1, :])\
                  .then_inc(s_out, 16)
                sp.dma_start(out[(WINDOWS - 1) * P:NODES, :], y[0:LAST, WINDOWS - 1, :]).then_inc(s_out, 16)
                sp.wait_ge(s_out, 32)

            @block.vector
            def _(dve):
                v = nc.vector
                dve.wait_ge(s_in, 32)
                v.tensor_scalar(z[:, :], k.node_sums[:, :], 0.0, None, ALU.is_equal)
                v.tensor_scalar(n[:, :], k.node_sums[:, :], CAP, None, ALU.min)
                dve.drain()
                v.tensor_tensor(n[:, :], n[:, :], z[:, :], ALU.add)
                dve.drain()
                v.reciprocal(n[:, :], n[:, :])
                dve.drain()
                v.tensor_scalar(n[:, :], n[:, :], SHRINK, None, ALU.mult)
                v.tensor_scalar(y[:, :, :], k.H[:, :, :], SHRINK, None, ALU.mult)
                dve.drain()
                v.tensor_tensor(t[:, :, :], k.H[:, :, :], each(n[:, :]), ALU.mult)
                dve.drain()
                v.scalar_tensor_tensor(t[:, :, :], t[:, :, :], 0.0, y[:, :, :], ALU.max, ALU.add)
                dve.drain()
                v.tensor_scalar(y[:, :, :], t[:, :, :], 1.0e15, None, ALU.min)
                dve.drain()
                v.tensor_tensor(t[:, :, :], y[:, :, :], y[:, :, :], ALU.mult)
                dve.drain()
                v.tensor_reduce(ms[:, :], t[:, :, :], AXX, ALU.add)
                dve.drain()
                v.tensor_scalar(ok[:, :], ms[:, :], 3.4028235e38 * SHRINK * SHRINK, None, ALU.is_le)
                v.tensor_scalar(sd[:, :], ms[:, :], 1.0 / D, 1.0e-6 * SHRINK * SHRINK, ALU.mult, ALU.add)
                dve.drain().then_inc(s_ms, 1)
                dve.wait_ge(s_sd, 1)
                v.reciprocal(sd[:, :], sd[:, :])
                dve.drain()
                v.tensor_tensor(sd[:, :], sd[:, :], ok[:, :], ALU.mult)
                dve.drain()
                v.tensor_tensor(y[:, :, :], y[:, :, :], each(sd[:, :]), ALU.mult)
                dve.drain()
                v.tensor_tensor(y[:, :, :], y[:, :, :], over(bc[:, 0, :]), ALU.mult)
                dve.drain()
                v.tensor_tensor(y[:, :, :], y[:, :, :], over(bc[:, 1, :]), ALU.add)
                dve.drain()
                v.tensor_tensor(y[:, :, :], y[:, :, :], k.X[:, :, :], ALU.add).then_inc(s_y, 1)

            @block.scalar
            def _(act):
                act.wait_ge(s_ms, 1)
                nc.scalar.activation(sd[:, :], sd[:, :], ACT.Sqrt).then_inc(s_sd, 1)


def program(nc, arrays, out):
    with ExitStack() as ctx:
        k = Shared(nc, ctx, arrays)

        def sbuf(name, shape, dt=F32):
            return nc.sbuf_tensor(name, shape, dt)

        def sb(name, shape, dt=F32):
            return ctx.enter_context(sbuf(name, shape, dt))

        def dram(name, shape, dt=F32):
            return nc.dram_tensor(name, shape, dt).ap()
        k.ones_row = sb("ones_row", [1, P])
        k.ident = sb("ident", [P, P])
        k.iota_row = sb("iota_row", [P, P])
        k.iota_p = sb("iota_p", [P, 1])
        k.eps5 = sb("eps5", [P, 1])
        k.mask_t = sb("mask_t", [P, 2, GROUP + 1])
        k.first_t = sb("first_t", [P, 2, GROUP])
        k.last_t = sb("last_t", [P, 2, GROUP])
        k.step_masks = sb("step_masks", [HEADS, 4, STEPS])
        k.dloc_e = sb("dloc_e", [P, TILES])
        k.end_e = sb("end_e", [P, TILES])
        k.src_e = sb("src_e", [P, TILES], I32)
        k.win_hot = sb("win_hot", [P, 2, WINDOWS])
        k.win = sb("win", [1, ITERS], I32)
        k.X = sb("X", [P, WINDOWS, D])
        k.H = sb("H", [P, WINDOWS, D])
        k.G = sb("G", [P, WINDOWS, D])
        k.att = sb("att", [P, D])
        k.dloc_dram = dram("dloc_dram", [STEPS, GROUP], BF16)
        k.lo_dram = dram("lo_dram", [STEPS, GROUP], BF16)
        k.mask_dram = dram("mask_dram", [STEPS, GROUP], BF16)
        k.hot_dram = dram("hot_dram", [P, STEPS * GROUP], BF16)
        k.slots_dram = dram("slots_dram", [P, TILES * (D + 4)])
        k.g_dram = dram("g_dram", [ROWS, D])
        k.h_dram = dram("h_dram", [ROWS, D + 4])
        k.k_dram = dram("k_dram", [ROWS, HD])
        k.v_dram = dram("v_dram", [ROWS, HW1])
        k.sums_dram = dram("sums_dram", [P, WINDOWS * HW1])
        graph_phase(nc, k)

        edge_conv_in_phase(nc, k)
        with sbuf("acc", [P, WINDOWS * (D + 1)]) as k.acc:
            edge_max_phase(nc, k)
            edge_conv_out_phase(nc, k)

        with sbuf("logits_conv", [P, HEADS, TILES]) as k.logits:
            with sbuf("u_table", [P, WINDOWS * 3 * HW1], BF16) as k.U:
                conv1_in_phase(nc, k)
                edge_logits_phase(nc, k, k.h_dram, D + 4, False, HW1, keep=True)
            segment_softmax_phase(nc, k, HEADS, float(D) ** -0.5)
            edge_sum_phase(nc, k, None, D + 4, [(k.logits[:, h, :], 0, D + 1) for h in range(HEADS)],
                           k.sums_dram)
            with sbuf("q_table", [P, WINDOWS * 3 * HD], BF16) as k.U:
                conv_mid_phase(nc, k)
                edge_logits_phase(nc, k, k.k_dram, HD, True, HD)
            segment_softmax_phase(nc, k, HEADS, float(D) ** -0.5)
            with sbuf("sums_conv2", [P, WINDOWS * HW1]) as k.sums:
                edge_sum_phase(nc, k, k.v_dram, HW1, [(k.logits[:, h, :], h * (D + 1), D + 1) for h in range(HEADS)])
                conv2_out_phase(nc, k)

        k.logits, k.selfs, k.ends = sb("logits3", [P, 1, TILES]), sb("selfs", [P, TILES]), sb("ends", [P, TILES, 2])
        with sbuf("r_table", [P, WINDOWS * 3 * (D + 1)], BF16) as k.U:
            gat_in_phase(nc, k)
            edge_logits_phase(nc, k, k.h_dram, D + 4, False, D + 1, gat=True, keep=True)
        segment_softmax_phase(nc, k, 1, 1.0, with_self=True)
        with sbuf("sums_gat", [P, WINDOWS * (D + 3)]) as k.sums:
            edge_sum_phase(nc, k, None, D + 4, [(k.logits[:, 0, :], 0, D + 1), (None, k.ends, 2)])
            gat_out_phase(nc, k)

        k.parts = sb("parts", [P, TILES, 3], BF16)
        k.node_sums = sb("node_sums", [P, WINDOWS])
        with sbuf("s_table", [P, WINDOWS * 3], BF16) as k.U, sbuf("v_table", [P, 3, WINDOWS], BF16) as k.V:
            last_in_phase(nc, k)
            value_logits_phase(nc, k)
        last_weights_phase(nc, k)
        value_sums_phase(nc, k)
        last_out_phase(nc, k, out)


def kernel(**inputs):
    import numpy as _np
    import concourse.bacc as _bacc
    from concourse import mybir as _mybir
    from concourse.bass_utils import run_bass_kernel_spmd as _run

    nc = _bacc.Bacc("TRN2", target_bir_lowering=False, num_devices=1)
    host = {n: _np.ascontiguousarray(v) for n, v in inputs.items()}
    pad = SLOTS - EDGES
    host["src"] = _np.concatenate([host["src"], _np.zeros(pad, host["src"].dtype)])
    host["dst"] = _np.concatenate([host["dst"], _np.full(pad, ROWS - 1, host["dst"].dtype)])
    arrays = {f"in_{n}": a for n, a in host.items()}
    aps = {n: nc.dram_tensor(f"in_{n}", a.shape, _mybir.dt.from_np(a.dtype), kind="ExternalInput").ap()
           for n, a in host.items()}
    out = nc.dram_tensor("out_0", [NODES, D], _mybir.dt.float32, kind="ExternalOutput").ap()
    program(nc, aps, out)
    r = _run(nc, [arrays], core_ids=[0])
    return r.results[0]["out_0"]
```
